# Optimizing a Trainium2 kernel written in Bass

```python
import numpy as np
import jax
import jax.numpy as jnp

def _softmax(x, axis=-1):
    return jax.nn.softmax(x, axis=axis)

def _gelu(x):
    return jax.nn.gelu(x, approximate=True)

def _silu(x):
    return jax.nn.silu(x)

def _sigmoid(x):
    return jax.nn.sigmoid(x)

def _layernorm(x, axis=-1, eps=1e-05):
    m = jnp.mean(x, axis=axis, keepdims=True)
    v = jnp.var(x, axis=axis, keepdims=True)
    return (x - m) / jnp.sqrt(v + eps)

def _scatter_add(tgt, idx, src, axis=0):
    return tgt.at[idx].add(src)

def _segment_sum(src, seg, n):
    return jax.ops.segment_sum(src, seg, n)
kernel_name = 'mk_conv_preact_d2_conv_nhwc128_r4_c935c3'

def setup_inputs(seed: int=0):
    np.random.seed(seed)
    _w = jnp.asarray

    def _rec_inputs():
        import jax
        import jax.numpy as jnp
        _gk = jax.random.key(seed)
        x = -0.000125 + 0.9999 * jax.random.normal(jax.random.fold_in(_gk, 1), (16, 32, 32, 32), jnp.float32)
        return x
    x = _rec_inputs()

    def _L0_conv_setup():
        import jax, jax.numpy as jnp
        import numpy as np
        N, L, D = (16, 32, 32)
        H, C = (8, 16)
        EPS = 1e-05
        key = jax.random.key(seed)
        ks = jax.random.split(key, 10)
        s = 0.02
        return {'z': jax.random.normal(ks[0], (N, L, L, D), dtype=jnp.float32), 'ln_w': jnp.ones((D,), jnp.float32), 'ln_b': jnp.zeros((D,), jnp.float32), 'Wq': jax.random.normal(ks[1], (D, H * C), jnp.float32) * s, 'Wk': jax.random.normal(ks[2], (D, H * C), jnp.float32) * s, 'Wv': jax.random.normal(ks[3], (D, H * C), jnp.float32) * s, 'Wg': jax.random.normal(ks[4], (D, H * C), jnp.float32) * s, 'bg': jnp.zeros((H * C,), jnp.float32), 'Wo': jax.random.normal(ks[5], (H * C, D), jnp.float32) * s, 'bo': jnp.zeros((D,), jnp.float32)}
    _L0_conv_all = _L0_conv_setup()
    _L0_conv_in = {k: v for k, v in _L0_conv_all.items() if k in ('ln_w', 'ln_b', 'Wq', 'Wk', 'Wv', 'Wg', 'bg', 'Wo', 'bo')}
    del _L0_conv_all

    def _L1_conv_setup():
        import jax, jax.numpy as jnp
        import numpy as np
        EPS = 1e-05
        AXIS = 1

        def _sparse_norm(x, alpha, beta):
            m = jnp.mean(x)
            v = jnp.var(x)
            nv = jax.lax.stop_gradient((x - m) * jax.lax.rsqrt(v + EPS))
            return alpha * nv + beta

        def _lin(x, W, b):
            return jnp.einsum('bijc,oc->bijo', x, W) + b
        key = jax.random.key(seed)
        ks = jax.random.split(key, 8)
        L, Cin, Cd = (128, 32, 32)
        g = 1.0 / np.sqrt(2.0)
        std_proj = g * np.sqrt(2.0 / (Cin + Cd))
        std_gate = np.sqrt(2.0 / (Cin + Cd))

        def w(k, o, i, s):
            return (jax.random.normal(k, (o, i), jnp.float32) * s).astype(jnp.float32)
        return {'z': jax.random.normal(ks[0], (1, L, L, Cin), jnp.float32), 'alpha_in': jnp.ones((1,), jnp.float32), 'beta_in': jnp.zeros((1,), jnp.float32), 'W_la': w(ks[1], Cd, Cin, std_proj), 'b_la': jnp.zeros((Cd,), jnp.float32), 'W_ga': w(ks[2], Cd, Cin, std_gate), 'b_ga': jnp.zeros((Cd,), jnp.float32), 'W_lb': w(ks[3], Cd, Cin, std_proj), 'b_lb': jnp.zeros((Cd,), jnp.float32), 'W_gb': w(ks[4], Cd, Cin, std_gate), 'b_gb': jnp.zeros((Cd,), jnp.float32), 'alpha_o': jnp.ones((1,), jnp.float32), 'beta_o': jnp.zeros((1,), jnp.float32), 'W_go': w(ks[5], Cin, Cin, std_gate), 'b_go': jnp.zeros((Cin,), jnp.float32), 'W_lo': w(ks[6], Cin, Cd, std_proj), 'b_lo': jnp.zeros((Cin,), jnp.float32)}
    _L1_conv_all = _L1_conv_setup()
    _L1_conv_in = {k: v for k, v in _L1_conv_all.items() if k in ('alpha_in', 'beta_in', 'W_la', 'b_la', 'W_ga', 'b_ga', 'W_lb', 'b_lb', 'W_gb', 'b_gb', 'alpha_o', 'beta_o', 'W_go', 'b_go', 'W_lo', 'b_lo')}
    del _L1_conv_all
    return {'x': x, 'L0_conv_ln_w': _L0_conv_in['ln_w'], 'L0_conv_ln_b': _L0_conv_in['ln_b'], 'L0_conv_Wq': _L0_conv_in['Wq'], 'L0_conv_Wk': _L0_conv_in['Wk'], 'L0_conv_Wv': _L0_conv_in['Wv'], 'L0_conv_Wg': _L0_conv_in['Wg'], 'L0_conv_bg': _L0_conv_in['bg'], 'L0_conv_Wo': _L0_conv_in['Wo'], 'L0_conv_bo': _L0_conv_in['bo'], 'L1_conv_alpha_in': _L1_conv_in['alpha_in'], 'L1_conv_beta_in': _L1_conv_in['beta_in'], 'L1_conv_W_la': _L1_conv_in['W_la'], 'L1_conv_b_la': _L1_conv_in['b_la'], 'L1_conv_W_ga': _L1_conv_in['W_ga'], 'L1_conv_b_ga': _L1_conv_in['b_ga'], 'L1_conv_W_lb': _L1_conv_in['W_lb'], 'L1_conv_b_lb': _L1_conv_in['b_lb'], 'L1_conv_W_gb': _L1_conv_in['W_gb'], 'L1_conv_b_gb': _L1_conv_in['b_gb'], 'L1_conv_alpha_o': _L1_conv_in['alpha_o'], 'L1_conv_beta_o': _L1_conv_in['beta_o'], 'L1_conv_W_go': _L1_conv_in['W_go'], 'L1_conv_b_go': _L1_conv_in['b_go'], 'L1_conv_W_lo': _L1_conv_in['W_lo'], 'L1_conv_b_lo': _L1_conv_in['b_lo']}

def reference(x, L0_conv_ln_w, L0_conv_ln_b, L0_conv_Wq, L0_conv_Wk, L0_conv_Wv, L0_conv_Wg, L0_conv_bg, L0_conv_Wo, L0_conv_bo, L1_conv_alpha_in, L1_conv_beta_in, L1_conv_W_la, L1_conv_b_la, L1_conv_W_ga, L1_conv_b_ga, L1_conv_W_lb, L1_conv_b_lb, L1_conv_W_gb, L1_conv_b_gb, L1_conv_alpha_o, L1_conv_beta_o, L1_conv_W_go, L1_conv_b_go, L1_conv_W_lo, L1_conv_b_lo):
    import jax
    import jax.numpy as jnp

    def _L0_conv_ref(z, ln_w, ln_b, Wq, Wk, Wv, Wg, bg, Wo, bo):
        import jax, jax.numpy as jnp
        import numpy as np
        N, L, D = (16, 32, 32)
        H, C = (8, 16)
        EPS = 1e-05
        n, l, _, d = z.shape
        mu = jnp.mean(z, axis=-1, keepdims=True)
        var = jnp.var(z, axis=-1, keepdims=True)
        zn = (z - mu) * jax.lax.rsqrt(var + EPS) * ln_w + ln_b
        q = (zn @ Wq).reshape(n, l, l, H, C)
        k = (zn @ Wk).reshape(n, l, l, H, C)
        v = (zn @ Wv).reshape(n, l, l, H, C)
        g = jax.nn.sigmoid(zn @ Wg + bg).reshape(n, l, l, H, C)
        att = jnp.einsum('iabhc,jabhc->ijabh', q, k) * (1.0 / np.sqrt(C))
        att = jax.nn.softmax(att, axis=1)
        o = jnp.einsum('ijabh,jabhc->iabhc', att, v) * g
        out = o.reshape(n, l, l, H * C) @ Wo + bo
        return out

    def _L1_conv_ref(z, alpha_in, beta_in, W_la, b_la, W_ga, b_ga, W_lb, b_lb, W_gb, b_gb, alpha_o, beta_o, W_go, b_go, W_lo, b_lo):
        import jax, jax.numpy as jnp
        import numpy as np
        EPS = 1e-05
        AXIS = 1

        def _sparse_norm(x, alpha, beta):
            m = jnp.mean(x)
            v = jnp.var(x)
            nv = jax.lax.stop_gradient((x - m) * jax.lax.rsqrt(v + EPS))
            return alpha * nv + beta

        def _lin(x, W, b):
            return jnp.einsum('bijc,oc->bijo', x, W) + b
        zn = _sparse_norm(z, alpha_in, beta_in)
        a = jax.nn.sigmoid(_lin(zn, W_ga, b_ga)) * _lin(zn, W_la, b_la)
        b = jax.nn.sigmoid(_lin(zn, W_gb, b_gb)) * _lin(zn, W_lb, b_lb)
        if AXIS == 1:
            k = jnp.einsum('bitc,bjtc->bijc', a, b)
        else:
            k = jnp.einsum('btic,btjc->bijc', a, b)
        kn = _sparse_norm(k, alpha_o, beta_o)
        return jax.nn.sigmoid(_lin(zn, W_go, b_go)) * _lin(kn, W_lo, b_lo)

    def _gn(v, G=32, eps=1e-05):
        B_, H_, W_, C_ = v.shape
        g = v.reshape(B_, H_, W_, G, C_ // G)
        m = jnp.mean(g, axis=(1, 2, 4), keepdims=True)
        s = jnp.var(g, axis=(1, 2, 4), keepdims=True)
        return ((g - m) / jnp.sqrt(s + eps)).reshape(v.shape)

    def _ln_c(v, eps=1e-06):
        m = jnp.mean(v, axis=-1, keepdims=True)
        s = jnp.var(v, axis=-1, keepdims=True)
        return (v - m) / jnp.sqrt(s + eps)

    def _ln_t(v, eps=1e-05):
        m = jnp.mean(v, axis=-1, keepdims=True)
        s = jnp.var(v, axis=-1, keepdims=True)
        return (v - m) / jnp.sqrt(s + eps)

    def _to_tokens(v):
        B_, H_, W_, C_ = v.shape
        return v.reshape(B_, H_ * W_, C_)

    def _from_tokens(t, like):
        return t.reshape(like.shape)
    x = x + _L0_conv_ref(_gn(x), L0_conv_ln_w, L0_conv_ln_b, L0_conv_Wq, L0_conv_Wk, L0_conv_Wv, L0_conv_Wg, L0_conv_bg, L0_conv_Wo, L0_conv_bo)
    x = x + _L1_conv_ref(_gn(x), L1_conv_alpha_in, L1_conv_beta_in, L1_conv_W_la, L1_conv_b_la, L1_conv_W_ga, L1_conv_b_ga, L1_conv_W_lb, L1_conv_b_lb, L1_conv_W_gb, L1_conv_b_gb, L1_conv_alpha_o, L1_conv_beta_o, L1_conv_W_go, L1_conv_b_go, L1_conv_W_lo, L1_conv_b_lo)
    return x

_drawn_inputs = setup_inputs


def setup_inputs(seed=0):
    import zlib

    import numpy as np

    out = dict(_drawn_inputs(seed))
    spreads = {'L0_conv_ln_w': (1.0, 0.6),
     'L0_conv_ln_b': (0.0, 0.8),
     'L0_conv_bg': (0.0, 0.8),
     'L0_conv_bo': (0.0, 0.1),
     'L1_conv_b_la': (0.0, 0.324),
     'L1_conv_b_ga': (0.0, 0.649),
     'L1_conv_b_lb': (0.0, 0.293),
     'L1_conv_b_gb': (0.0, 0.487),
     'L1_conv_b_go': (0.0, 0.471),
     'L1_conv_b_lo': (0.0, 0.3)}
    factors = {'L0_conv_Wq': 8.0,
     'L0_conv_Wk': 8.0,
     'L0_conv_Wv': 8.0,
     'L0_conv_Wg': 8.0,
     'L0_conv_Wo': 8.0}
    for name, (base, spread) in spreads.items():
        noise = np.random.default_rng([zlib.crc32(name.encode()), seed]).standard_normal(out[name].shape)
        drawn = base * np.exp(spread * noise) if base else spread * noise
        out[name] = jnp.asarray(drawn.astype(out[name].dtype))
    for name, factor in factors.items():
        out[name] = (out[name] * factor).astype(out[name].dtype)
    return out
```

```python
import concourse.bass as bass
from concourse import mybir
from contextlib import ExitStack

f32 = mybir.dt.float32
f16 = mybir.dt.float16
bf16 = mybir.dt.bfloat16
ACT = mybir.ActivationFunctionType
ALU = mybir.AluOpType
AX = mybir.AxisListType

N, L, D, H, C = 16, 32, 32, 8, 16
A2, A4 = 4, 8
SB = 4
NS = L // SB
QS = SB * A4
COLS = QS * N
HP = H // 2
EPS = 1e-5
HI, LO = 0, 1


def build(nc, x, ln_w, ln_b, Wq, Wk, Wv, Wg, bg, Wo, bo, al_in, be_in, W_la, b_la, W_ga, b_ga,
          W_lb, b_lb, W_gb, b_gb, al_o, be_o, W_go, b_go, W_lo, b_lo, out):
    ctx = ExitStack()
    with ctx:
        def sb(name, shape, dt=f32):
            return ctx.enter_context(nc.sbuf_tensor(name, shape, dt))

        sem_names = {}

        def sem(name):
            s = ctx.enter_context(nc.semaphore(name))
            sem_names[name] = s
            return s

        x_tok = sb("x_tok", [128, A2, L, D])
        xT = sb("xT", [128, NS * COLS])
        zc = sb("zc", [128, 2, A2, SB, D])
        sq = sb("sq", [128, 1024])
        sqx = sb("sqx", [128, COLS])
        zn_tok = sb("zn_tok", [128, 2, A2, D, SB, 2], f16)
        znT = sb("znT", [128, 2, COLS], f16)
        zbd = sb("zbd", [128, A2, 2, COLS], f16)
        Z = sb("Z", [128, 2, A4, A2, D, SB, 2], f16)
        t_sb = sb("t_sb", [128, 2, QS, H, N], f16)
        S_sb = sb("S_sb", [128, QS, A2, N])
        PP = sb("PP", [128, 2, QS, 128], f16)
        P2 = PP[:, 0].rearrange("p q (k m) -> p q k m", k=2)
        PT = PP[:, 1]
        u_sb = sb("u_sb", [128, H, QS, N])
        th = sb("th", [128, 2, HP, COLS])
        og = sb("og", [128, HP, COLS])
        sums = sb("sums", [128, QS * A2])
        rden = sb("rden", [128, QS * A2])
        nmax = sb("nmax", [128, 2, 32])

        ident = sb("ident", [128, 128])
        ident16 = sb("ident16", [128, 128], f16)
        seqsum = sb("seqsum", [128, 128])
        chsum = sb("chsum", [128, 128])
        allsum = sb("allsum", [128, 2, 128])
        headmask = sb("headmask", [128, H])
        wq_in = sb("wq_in", [D, 2, H * C])
        wqT = sb("wqT", [128, A2, D])
        wkT = sb("wkT", [128, D])
        wqTm = S_sb[:, 0:16].rearrange("p q a n -> p (q a n)").rearrange("p (h m) -> p h m", h=H)
        A_bd = sb("A_bd", [128, 2, H, A2, D], f16)
        wg_in = sb("wg_in", [128, H, C])
        Wg_bd = sb("Wg_bd", [128, 2, H, A2, C], f16)
        wv_in = sb("wv_in", [128, H, C])
        Wv_bd = sb("Wv_bd", [128, H, A2, C])
        Wo_bd = sb("Wo_bd", [128, HP, A2, D])
        Wo_h = sb("Wo_h", [128, HP, A2, D])
        bg_in = sb("bg_in", [128, HP])
        bg_h = sb("bg_h", [128, HP])
        w_bc = sb("w_bc", [128, D])
        b_bc = sb("b_bc", [128, D])
        bo_col = sb("bo_col", [128, 1])
        gn_part = sb("gn_part", [128, 2, D, A2])
        gn_sum = sb("gn_sum", [128, 2, D])
        gn_mv = sb("gn_mv", [128, 2, D])
        gn_tmp = sb("gn_tmp", [128, 3, D])
        gn_r = sb("gn_r", [128, D])
        gn_sh = sb("gn_sh", [128, D])
        minus_half = sb("minus_half", [128, D])
        ln_mu = sb("ln_mu", [128, 2, A2 * SB])
        ln_var = sb("ln_var", [128, 2, A2 * SB])
        ln_ve = sb("ln_ve", [128, 2, A2 * SB])
        ln_rs = sb("ln_rs", [128, 2, A2 * SB])
        st1 = sb("st1", [128, 2, NS, N])
        w1_in = sb("w1_in", [128, A2, D])
        w2_in = sb("w2_in", [64, A2, D])
        W1_f = sb("W1_f", [128, 2, 2, D])
        W1_bd = sb("W1_bd", [128, 2, 2, A2, 2, D], f16)
        W2_f = sb("W2_f", [128, 2, D])
        Wgo_bd = sb("Wgo_bd", [128, 2, A2, D], f16)
        Wlo_bd = sb("Wlo_bd", [128, A2, D])
        b1_in = sb("b1_in", [128, 2, 2, D])
        b1_r = sb("b1_r", [128, 2, 2, 2, D])
        b1_s = sb("b1_s", [128, 3, 2, 2, D], bf16)
        B1 = sb("B1", [128, 2, A2, 2, D], bf16)
        ones_bf = sb("ones_bf", [128, 128], bf16)
        ones_col = sb("ones_col", [128, 1])
        col = sb("col", [128, 16])
        g2 = sb("g2", [128, 12, N])
        ksum = sb("ksum", [128, 2, 8])
        ksum2 = sb("ksum2", [128, 2])
        (Bgo, Blo, Ain, Bin, Aout, Bout, V, RV, SC, KR, KS, KT, CV, T0, BGH, RW) = range(16)

        z1 = [t_sb[:, k].rearrange("p q h i -> p (q h i)").rearrange("p (a n b) -> p a n b", a=A4, n=N)
              for k in (HI, LO)]
        z1f = [zc[:, k].rearrange("p a b d -> p (a b d)") for k in (0, 1)]
        a_buf = [u_sb[:, 2 * k:2 * k + 2].rearrange("p h q i -> p (h q i)")
                 .rearrange("p (i c) -> p i c", c=D) for k in (0, 1)]
        b_buf = [u_sb[:, 4 + 2 * k:6 + 2 * k].rearrange("p h q i -> p (h q i)")
                 .rearrange("p (i c) -> p i c", c=D) for k in (0, 1)]
        x_perm = u_sb[:, :, :, :].rearrange("p h q i -> p (h q i)").rearrange("p (b e d) -> p b e d", b=L, e=A2)
        bbd = [PP[:, :, :, :].rearrange("p k q m -> p (k q m)").bitcast(f32)
               .rearrange("p (n j c) -> p n j c", n=4, j=L), x_tok[:, :, :, :]]
        gt = [S_sb[:, 4 * k:4 * k + 4].rearrange("p q a n -> p (q a n)")
              .rearrange("p (a m c) -> p a m c", a=A2, m=2) for k in range(3)]
        k_sb = og[:, :, :].rearrange("p h c -> p (h c)")
        kT = th[:, :, :, :].rearrange("p k h c -> p (k h c)")
        tg = Z[:, :, :, :, :, :, :].rearrange("p r f e d b k -> p (r f e d b k)").bitcast(f32)
        x2 = tg[:, 4096:8192]
        tg = tg[:, 0:4096]
        out_tok = u_sb[:, :, :, :].rearrange("p h q i -> p (h q i)").rearrange("p (a b d) -> p a b d", a=A2, b=L)

        zn_dram = nc.dram_tensor("zn_dram", [N, A4, NS, A2, D * SB * 2], f16, kind="Internal").ap()
        k_dram = nc.dram_tensor("k_dram", [D, A4, A2, N * L], f32, kind="Internal").ap()

        PS = [ctx.enter_context(nc.psum_tensor(f"PS{i}", [128, 512], f32)) for i in range(8)]
        bank_tg = lambda i: PS[i % 3]
        bank_s = lambda i: PS[3 + i % 2]
        bank_b = lambda i: PS[5 + i % 2]
        bank_w = PS[7]

        x_in = [sem(f"x_in{i}") for i in range(A2)]
        wts_in = sem("wts_in")
        wts2_in = sem("wts2_in")
        zeros_w = sem("zeros_w")
        zeros_z = sem("zeros_z")
        sq_ok = sem("sq_ok")
        sqred = sem("sqred")
        gn_ok = sem("gn_ok")
        rsq = sem("rsq")
        gn_mm = sem("gn_mm")
        wT_mm = sem("wT_mm")
        wprep = sem("wprep")
        wprep_a = sem("wprep_a")
        xp_ok = sem("xp_ok")
        xT_mm = sem("xT_mm")
        xT_ok = sem("xT_ok")
        ln_z = sem("ln_z")
        ln_v = sem("ln_v")
        ln_a = sem("ln_a")
        zn_st = sem("zn_st")
        Z_ld = [sem("Z_ld0"), sem("Z_ld1")]
        zbd_ld = sem("zbd_ld")
        zT_mm = sem("zT_mm")
        zT_ok = sem("zT_ok")
        t_mm = sem("t_mm")
        t_hi = sem("t_hi")
        t_lo = sem("t_lo")
        g_mm = sem("g_mm")
        g_th = sem("g_th")
        s_mm = sem("s_mm")
        s_max = sem("s_max")
        s_sub = sem("s_sub")
        s_exp = sem("s_exp")
        p_sum = sem("p_sum")
        p_rec = sem("p_rec")
        p_nrm = sem("p_nrm")
        p_hi = sem("p_hi")
        p_lo = sem("p_lo")
        pt_mm = sem("pt_mm")
        pt_ok = sem("pt_ok")
        u_mm = sem("u_mm")
        u_ok = sem("u_ok")
        o_mm = sem("o_mm")
        o_ok = sem("o_ok")
        w_mm = sem("w_mm")
        x1_ok = sem("x1_ok")
        x1_sq = sem("x1_sq")
        x1_st = sem("x1_st")
        g2_ok = sem("g2_ok")
        g2_mm = sem("g2_mm")
        bbd_z = sem("bbd_z")
        z1_m = sem("z1_m")
        z1_b = sem("z1_b")
        z1_h = sem("z1_h")
        z1_l = sem("z1_l")
        pj_mm = sem("pj_mm")
        pj_th = sem("pj_th")
        pj_ok = sem("pj_ok")
        bbd_ld = [sem("bbd_ld0"), sem("bbd_ld1")]
        k_mm = sem("k_mm")
        k_cp = sem("k_cp")
        k_sq = sem("k_sq")
        k_st = sem("k_st")
        kT_ld = [sem(f"kT_ld{g}") for g in range(4)]
        go_mm = sem("go_mm")
        go_th = sem("go_th")
        k_ok = sem("k_ok")
        ks_mm = sem("ks_mm")
        lo_mm = sem("lo_mm")
        lo_s = sem("lo_s")
        lo_g = sem("lo_g")
        x2_ok = sem("x2_ok")
        x2_mm = sem("x2_mm")
        x2_cp = [sem("x2_cp0"), sem("x2_cp1")]
        out_st = sem("out_st")

        LZ, LV, LA = 7, 4, 2
        NZ_MASKS, NZ_Z = 15, 3
        WTS, WTS2 = 16 * 32, 16 * 48

        def bcast(ap, axis, n):
            v = ap.unsqueeze(axis)
            return v.to_broadcast([n if i == axis else s for i, s in enumerate(v.shape)])

        block = ctx.enter_context(nc.Block())
        x_src = x.rearrange("n (f e) b c -> (n f) e (b c)", e=A2)
        out_dst = out.rearrange("n (f e) b c -> f n e (b c)", e=A2)

        def sp_slab(sp, j, par, half):
            sp.wait_ge(ln_z, LZ * (j + 1))
            sp.dma_start(zn_dram.rearrange("n f s e m -> (n f) s (e m)")[:, bass.ds(j, 1)],
                         zn_tok[:, par].rearrange("p e d b k -> p (e d b k)").unsqueeze(1)).then_inc(zn_st, 16)
            sp.wait_ge(zT_ok, j + 1)
            for e in range(A2):
                rows = slice(D * e, D * e + D)
                sp.dma_start(zbd[rows, e], znT[rows]).then_inc(zbd_ld, 16)
            sp.wait_ge(zn_st, 16 * (j + 1))
            for copy in range(2):
                for e in range(A2):
                    r0 = 64 * copy + N * e
                    sp.dma_start(Z[r0:r0 + N, par, :, e].rearrange("p f d b k -> p f (d b k)"),
                                 zn_dram[:, :, bass.ds(j, 1), e].rearrange("n f s m -> n (f s) m")
                                 ).then_inc(Z_ld[par], 16)

        @block.sync
        def _(sp):
            for e in range(A2):
                sp.dma_start(x_tok[:, e].rearrange("p b d -> p (b d)"), x_src[:, e]).then_inc(x_in[e], 16)
            for m, w in enumerate((W_ga, W_gb, W_la, W_lb)):
                for g in range(A2):
                    sp.dma_start(w1_in[D * m:D * m + D, g], w).then_inc(wts2_in, 16)
            for m, w in enumerate((W_go, W_lo)):
                for g in range(A2):
                    sp.dma_start(w2_in[D * m:D * m + D, g], w).then_inc(wts2_in, 16)
            sp.wait_ge(zeros_w, 3)
            for r in range(3):
                for m, b in enumerate((b_ga, b_gb, b_la, b_lb)):
                    sp.dma_start(b1_in[32 * r:32 * r + 1, m // 2, m % 2], b.unsqueeze(0)).then_inc(wts2_in, 16)
            for g in range(A2):
                sp.dma_start(col[D * g:D * g + D, Bgo:Bgo + 1], b_go.unsqueeze(1)).then_inc(wts2_in, 16)
                sp.dma_start(col[D * g:D * g + D, Blo:Blo + 1], b_lo.unsqueeze(1)).then_inc(wts2_in, 16)
            for k, v in ((Ain, al_in), (Bin, be_in), (Aout, al_o), (Bout, be_o)):
                sp.dma_start(col[:, k:k + 1], v.partition_broadcast(128)).then_inc(wts2_in, 16)

            sp.wait_ge(zeros_z, NZ_MASKS + NZ_Z)
            sp_slab(sp, 0, 0, 0)
            sp_slab(sp, 1, 1, 0)
            with sp.Fori(0, (NS - 2) // 2) as it:
                for par in range(2):
                    sp_slab(sp, 2 * it + 2 + par, par, it + 1)

            def bbd_load(g):
                sp.wait_ge(pj_ok, 16 * (g + 1))
                if g == 0:
                    sp.wait_ge(bbd_z, 2)
                if g >= 2:
                    sp.wait_ge(k_mm, 2 * (g - 1))
                for n in range(4):
                    rows = slice(L * n, L * n + L)
                    sp.dma_start(bbd[g % 2][rows, n].rearrange("p j c -> p (j c)"),
                                 b_buf[g % 2][rows].rearrange("p j c -> p (j c)")).then_inc(bbd_ld[g % 2], 16)

            def k_move(g):
                sp.wait_ge(k_cp, 2 * (g + 1))
                sp.dma_start(k_dram.rearrange("(c8 c4) f e m -> c4 (f e) c8 m", c4=4)[:, :, :, 128 * g:128 * g + 128]
                             .rearrange("c4 i c8 m -> (c4 i) c8 m"),
                             k_sb.rearrange("p (h c m) -> p h c m", h=2, c=8)[:, g % 2]).then_inc(k_st, 16)
                sp.wait_ge(k_st, 16 * (g + 1))
                for e in range(A2):
                    sp.dma_start(kT.rearrange("p (f m) -> p f m", f=A4)[D * e:D * e + D, :, 128 * g:128 * g + 128],
                                 k_dram[:, :, e, 128 * g:128 * g + 128]).then_inc(kT_ld[g], 16)

            bbd_load(0)
            bbd_load(1)
            k_move(0)
            bbd_load(2)
            k_move(1)
            bbd_load(3)
            k_move(2)
            k_move(3)
            for i in range(NS):
                sp.wait_ge(x2_cp[i % 2], i // 2 + 1)
                for f in range(A4):
                    sp.dma_start(out_dst[f, :, :, SB * D * i:SB * D * (i + 1)],
                                 out_tok[N * f:N * f + N, :, SB * i:SB * (i + 1)].rearrange("p e b d -> p e (b d)")
                                 ).then_inc(out_st, 16)
            sp.wait_ge(out_st, 16 * NS * A4)

        def pool_ln_front(pool, j, par):
            z = zc[:, par].rearrange("p e b d -> p e (b d)").rearrange("p e (b d) -> p e b d", d=D)
            if not isinstance(j, int) or j >= 2:
                pool.wait_ge(ln_z, LZ * (j - 1))
            nc.gpsimd.tensor_tensor(z, x_tok[:, :, bass.ds(j * SB, SB), :],
                                    bcast(bcast(gn_r[:, :], 1, SB), 1, A2), ALU.mult).then_inc(ln_z, 1)
            pool.wait_ge(ln_z, LZ * j + 1)
            zf = zc[:, par].rearrange("p e b d -> p (e b) d")
            nc.gpsimd.tensor_tensor(zf, zf, bcast(gn_sh[:, :], 1, A2 * SB), ALU.add).then_inc(ln_z, 1)

        def pool_ln_back(pool, j, par):
            zf = zc[:, par].rearrange("p e b d -> p (e b) d")
            pool.wait_ge(ln_v, LV * (j + 1))
            nc.gpsimd.tensor_tensor(ln_rs[:, par], ln_ve[:, par], minus_half[:, 0:A2 * SB], ALU.pow).then_inc(ln_z, 1)
            pool.wait_ge(ln_z, LZ * j + 3)
            nc.gpsimd.tensor_tensor(zf, zf, bcast(ln_rs[:, par], 2, D), ALU.mult).then_inc(ln_z, 1)
            pool.wait_ge(ln_z, LZ * j + 4)
            nc.gpsimd.tensor_tensor(zf, zf, bcast(w_bc[:, :], 1, A2 * SB), ALU.mult).then_inc(ln_z, 1)
            pool.wait_ge(ln_z, LZ * j + 5)
            nc.gpsimd.tensor_tensor(zf, zf, bcast(b_bc[:, :], 1, A2 * SB), ALU.add).then_inc(ln_z, 1)
            pool.wait_ge(ln_a, LA * (j + 1))
            hl = zn_tok[:, par].rearrange("p e d b k -> p e b d k")
            nc.gpsimd.tensor_tensor(hl[:, :, :, :, LO], zc[:, par], hl[:, :, :, :, HI], ALU.subtract).then_inc(ln_z, 1)

        def pool_norm(pool, m, ks):
            if ks[0] == 0:
                pool.wait_ge(p_rec, m + 1)
            for k in ks:
                P = S_sb[:, 8 * k:8 * k + 8].rearrange("p q a n -> p (q a) n")
                nc.gpsimd.tensor_tensor(P, P, bcast(rden[:, 32 * k:32 * k + 32], 2, N), ALU.mult).then_inc(p_nrm, 1)

        def pool_plo(pool, m, ks):
            for k in ks:
                P = S_sb[:, 8 * k:8 * k + 8].rearrange("p q a n -> p q (a n)")
                pool.wait_ge(p_hi, 4 * m + k + 1)
                nc.gpsimd.tensor_tensor(P2[:, 8 * k:8 * k + 8, LO], P, P2[:, 8 * k:8 * k + 8, HI],
                                        ALU.subtract).then_inc(p_lo, 1)

        def pool_period(pool, j, par, tail=True, B=True, A=True):
            if A:
                pool_ln_front(pool, j, par)
            if tail:
                pool_norm(pool, j - 1, (0, 1))
            if A:
                pool_ln_back(pool, j, par)
            if tail:
                pool_norm(pool, j - 1, (2, 3))
                pool_plo(pool, j - 1, (0, 1, 2, 3))
            if B:
                pool_sqx(pool, j - 2)

        def pool_sqx(pool, s):
            pool.wait_ge(x1_ok, s + 1)
            if not isinstance(s, int) or s >= 1:
                pool.wait_ge(x1_st, 2 * s)
            v = xT[:, bass.ds(s * COLS, COLS)]
            nc.gpsimd.tensor_tensor(sqx[:, :], v, v, ALU.mult).then_inc(x1_sq, 1)

        @block.gpsimd
        def _(pool):
            def rsqrt(sem_in, n, dst, src):
                pool.wait_ge(sem_in, n)
                nc.gpsimd.tensor_tensor(dst, src, minus_half[:, 0:dst.shape[-1]], ALU.pow).then_inc(rsq, 1)

            nc.gpsimd.memset(minus_half[:, :], -0.5).then_inc(zeros_z, 1)
            seq = seqsum[:, :].rearrange("p (n f) -> p n f", f=A4)
            chn = chsum[:, :].rearrange("p (e c) -> p e c", c=D)
            nc.gpsimd.memset(ident[:, :], 0.0).then_inc(zeros_z, 1)
            nc.gpsimd.memset(seqsum[:, :], 1.0 / (L * L)).then_inc(zeros_z, 1)
            nc.gpsimd.memset(headmask[:, :], 1.0).then_inc(zeros_z, 1)
            nc.gpsimd.memset(chsum[:, :], 0.0).then_inc(zeros_z, 1)
            pool.wait_ge(zeros_z, 5)
            nc.gpsimd.affine_select(out=ident[:, :], in_=ident[:, :], compare_op=ALU.not_equal, fill=1.0, base=0,
                                    pattern=[[-1, 128]], channel_multiplier=1).then_inc(zeros_z, 1)
            nc.gpsimd.affine_select(out=seq, in_=seq, compare_op=ALU.is_ge, fill=0.0, base=0,
                                    pattern=[[-A4, N], [0, A4]], channel_multiplier=1).then_inc(zeros_z, 1)
            nc.gpsimd.affine_select(out=headmask[:, :], in_=headmask[:, :], compare_op=ALU.is_ge, fill=0.0, base=0,
                                    pattern=[[-C, H]], channel_multiplier=1).then_inc(zeros_z, 1)
            pool.wait_ge(zeros_z, 8)
            nc.gpsimd.affine_select(out=seq, in_=seq, compare_op=ALU.is_ge, fill=0.0, base=A4 - 1,
                                    pattern=[[A4, N], [0, A4]], channel_multiplier=-1).then_inc(zeros_z, 1)
            nc.gpsimd.affine_select(out=headmask[:, :], in_=headmask[:, :], compare_op=ALU.is_ge, fill=0.0, base=C - 1,
                                    pattern=[[C, H]], channel_multiplier=-1).then_inc(zeros_z, 1)
            for k in range(A2):
                if k:
                    pool.wait_ge(zeros_z, 10 + k)
                nc.gpsimd.affine_select(out=chn, in_=chn, compare_op=ALU.not_equal, fill=1.0 / (L * L), base=-D * k,
                                        pattern=[[0, A2], [-1, D]], channel_multiplier=1).then_inc(zeros_z, 1)
            nc.gpsimd.tensor_copy(ident16[:, :], ident[:, :]).then_inc(zeros_z, 1)
            nc.gpsimd.memset(zbd[:, :, :, :].rearrange("p e k c -> p (e k c)").bitcast(f32), 0.0).then_inc(zeros_z, 1)
            for k in range(2):
                nc.gpsimd.memset(Z[:, k].rearrange("p f e d b k -> p (f e d b k)").bitcast(f32), 0.0).then_inc(zeros_z, 1)
            rsqrt(gn_ok, 8, gn_r[:, :], gn_tmp[:, 1])
            pool.wait_ge(gn_ok, 9)
            pool.wait_ge(wts_in, WTS)
            for j in range(2):
                pool_period(pool, j, j % 2, tail=j >= 1, B=False)
            with pool.Fori(0, (NS - 2) // 2) as it:
                for par in range(2):
                    pool_period(pool, 2 * it + 2 + par, par)
            pool_period(pool, NS, 0, A=False)
            nc.gpsimd.memset(bbd[1].rearrange("p n j c -> p (n j c)"), 0.0).then_inc(bbd_z, 1)
            pool.wait_ge(u_mm, 8 * NS)
            nc.gpsimd.memset(bbd[0].rearrange("p n j c -> p (n j c)"), 0.0).then_inc(bbd_z, 1)
            pool_period(pool, NS + 1, 1, tail=False, A=False)
            rsqrt(g2_ok, 5, g2[:, 6], g2[:, 5])
            rsqrt(g2_ok, 9, col[:, T0:T0 + 1], col[:, RV:RV + 1])
            for f in range(A4):
                pool.wait_ge(z1_m, f + 1)
                v = z1f[f % 2].rearrange("p (n b) -> p n b", n=N)
                nc.gpsimd.tensor_tensor(v, v, bcast(g2[:, 11], 2, L), ALU.add).then_inc(z1_b, 1)
            rsqrt(k_ok, 5, col[:, KR:KR + 1], col[:, RV:RV + 1])
            for f in range(A4):
                pool.wait_ge(lo_g, f + 1)
                v = x2[:, 512 * f:512 * f + 512].rearrange("p (n b) -> p n b", n=N)
                nc.gpsimd.tensor_tensor(v, v, xT[:, :].rearrange("p (b f n) -> p f n b", f=A4, n=N)[:, f],
                                        ALU.add).then_inc(x2_ok, 1)

        def act_period(act, j, par, tail=True, B=True, A=True):
            s, m = j - 2, j - 1
            if A:
                act.wait_ge(ln_v, LV * j + 2)
                nc.scalar.activation(sq[:, 0:512], zc[:, par].rearrange("p e b d -> p (e b d)"),
                                     ACT.Square).then_inc(ln_a, 1)

            def u_copies(ks):
                for k in ks:
                    act.wait_ge(u_mm, 8 * s + k + 1)
                    nc.scalar.copy(u_sb[:, :, 4 * k:4 * k + 4].rearrange("p h q i -> p q h i"),
                                   bank_b(k)[:, :].rearrange("p (q h i) -> p q h i", q=4, h=H)).then_inc(u_ok, 1)
            if B:
                u_copies(range(4))
            if A:
                act.wait_ge(ln_z, LZ * j + 6)
                if not isinstance(j, int) or j >= 2:
                    act.wait_ge(zn_st, 16 * (j - 1))
                nc.scalar.copy(zn_tok[:, par].rearrange("p e d b k -> p e b d k")[:, :, :, :, HI],
                               zc[:, par]).then_inc(ln_a, 1)
            if B:
                u_copies(range(4, 8))
            if tail:
                for k in range(4):
                    act.wait_ge(p_nrm, 4 * m + k + 1)
                    if not isinstance(m, int) or m >= 1:
                        act.wait_ge(pt_mm, 4 * (m - 1) + k + 1)
                    nc.scalar.copy(P2[:, 8 * k:8 * k + 8, HI],
                                   S_sb[:, 8 * k:8 * k + 8].rearrange("p q a n -> p q (a n)")).then_inc(p_hi, 1)
            if A:
                act.wait_ge(zT_mm, j + 1)
                src = bank_w[:, :].bitcast(f16).rearrange("p (k n f) -> p k f n", f=A4, n=N)
                dst = znT[:, :, :].rearrange("p k c -> p (k c)").rearrange("p (k f n) -> p k f n", f=A4, n=N)
                nc.scalar.copy(dst, src).then_inc(zT_ok, 1)
                for h in range(H):
                    act.wait_ge(t_mm, H * j + h + 1)
                    nc.scalar.copy(t_sb[:, HI, :, h], bank_tg(h)[:, :].rearrange("p (q i) -> p q i", i=N)).then_inc(t_hi, 1)
                for k in range(HP):
                    act.wait_ge(g_mm, HP * j + k + 1)
                    nc.scalar.activation(th[:, par, k], bank_tg(H + k)[:, :], ACT.Tanh, bias=bg_h[:, k:k + 1],
                                         scale=0.5).then_inc(g_th, 1)
                for k in range(4):
                    act.wait_ge(s_sub, 4 * j + k + 1)
                    v = S_sb[:, 8 * k:8 * k + 8].rearrange("p q a n -> p (q a n)")
                    nc.scalar.activation(v, v, ACT.Exp).then_inc(s_exp, 1)

        @block.scalar
        def _(act):
            for k, w in enumerate((Wq, Wk)):
                act.dma_start(wq_in[:, k], w).then_inc(wts_in, 16)
            for g in range(A2):
                rows = slice(D * g, D * g + D)
                act.dma_start(wg_in[rows].rearrange("p h c -> p (h c)"), Wg).then_inc(wts_in, 16)
                act.dma_start(wv_in[rows].rearrange("p h c -> p (h c)"), Wv).then_inc(wts_in, 16)
                act.dma_start(bo_col[rows], bo.unsqueeze(1)).then_inc(wts_in, 16)
            act.wait_ge(zeros_w, 2)
            for r in range(2):
                for e in range(A2):
                    rows = slice(64 * r + C * e, 64 * r + C * e + C)
                    act.dma_start(Wo_bd[rows, :, e],
                                  Wo.rearrange("(k r c) d -> r c k d", k=HP, r=2)[r]).then_inc(wts_in, 16)
                    act.dma_start(bg_in[rows], bg[r]).then_inc(wts_in, 16)
            act.dma_start(w_bc[:, :], ln_w.partition_broadcast(128)).then_inc(wts_in, 16)
            act.dma_start(b_bc[:, :], ln_b.partition_broadcast(128)).then_inc(wts_in, 16)
            for e in range(A2):
                act.wait_ge(x_in[e], 16)
                if e >= 1:
                    act.wait_ge(sqred, e)
                nc.scalar.activation(sq[:, :], x_tok[:, e].rearrange("p b d -> p (b d)"), ACT.Square).then_inc(sq_ok, 1)
                nc.scalar.copy(x_perm[:, :, e], x_tok[:, e]).then_inc(xp_ok, 1)
            act.wait_ge(wts_in, WTS)
            nc.scalar.mul(bg_h[:, :], bg_in[:, :], 0.5)
            nc.scalar.mul(Wo_h[:, :, :, :].rearrange("p k e d -> p (k e d)"),
                          Wo_bd[:, :, :, :].rearrange("p k e d -> p (k e d)"), 0.5).then_inc(wprep_a, 1)
            act.wait_ge(wT_mm, 2)
            for g in range(A2):
                rows = slice(D * g, D * g + D)
                nc.scalar.mul(A_bd[rows, HI, :, g], PS[1][rows, 0:256].rearrange("p (h d) -> p h d", h=H),
                              0.25).then_inc(wprep_a, 1)
            for g in range(A2):
                rows = slice(D * g, D * g + D)
                nc.scalar.copy(Wg_bd[rows, HI, :, g], wg_in[rows]).then_inc(wprep_a, 1)
            for g in range(A2):
                rows = slice(D * g, D * g + D)
                nc.scalar.copy(Wv_bd[rows, :, g], wv_in[rows]).then_inc(wprep_a, 1)
            for i in range(NS):
                act.wait_ge(xT_mm, i + 1)
                nc.scalar.copy(xT[:, COLS * i:COLS * i + COLS].rearrange("p (b f n) -> p b f n", f=A4, n=N),
                               PS[2 + i % 2][:, :].rearrange("p (b n f) -> p b f n", f=A4, n=N)).then_inc(xT_ok, 1)
            for j in range(2):
                act_period(act, j, j % 2, tail=j >= 1, B=False)
            with act.Fori(0, (NS - 2) // 2) as it:
                for par in range(2):
                    act_period(act, 2 * it + 2 + par, par)
            act_period(act, NS, 0, A=False)
            act_period(act, NS + 1, 1, tail=False, A=False)
            for f in range(A4):
                act.wait_ge(z1_b, f + 1)
                nc.scalar.copy(z1[HI][:, f].rearrange("p n b -> p (n b)"), z1f[f % 2]).then_inc(z1_h, 1)

            def gates(g):
                for f in range(A4):
                    i = A4 * g + f
                    act.wait_ge(pj_mm, i + 1)
                    if i >= 3:
                        act.wait_ge(pj_ok, 2 * (i - 2))
                    nc.scalar.activation(gt[i % 3].rearrange("p a m c -> p (a m c)"), PS[i % 3][:, 0:256],
                                         ACT.Tanh, scale=0.5).then_inc(pj_th, 1)

            def k_copies(g):
                for h in range(2):
                    i = 2 * g + h
                    act.wait_ge(k_mm, i + 1)
                    if h == 0 and g >= 2:
                        act.wait_ge(k_st, 16 * (g - 1))
                    dst = k_sb.rearrange("p (s c m) -> p s c m", s=2, c=8)[:, g % 2, 4 * h:4 * h + 4]
                    nc.scalar.activation(dst.rearrange("p c m -> p (c m)"), PS[3 + i % 4][:, :], ACT.Identity,
                                         accum_out=ksum[:, 0, i:i + 1]).then_inc(k_cp, 1)
                    nc.scalar.activation(sq[:, 512 * h:512 * h + 512], PS[3 + i % 4][:, :], ACT.Square,
                                         accum_out=ksum[:, 1, i:i + 1]).then_inc(k_sq, 1)

            gates(0)
            gates(1)
            k_copies(0)
            gates(2)
            k_copies(1)
            gates(3)
            k_copies(2)
            act.wait_ge(g2_ok, 14)
            for f in range(A4):
                act.wait_ge(go_mm, f + 1)
                nc.scalar.activation(tg[:, 512 * f:512 * f + 512], PS[f % 3][:, :], ACT.Tanh,
                                     bias=col[:, BGH:BGH + 1], scale=0.5).then_inc(go_th, 1)
            k_copies(3)
            for i in range(0, NS, 2):
                act.wait_ge(x2_mm, i + 1)
                nc.scalar.copy(out_tok[:, :, SB * i:SB * i + SB].rearrange("p e b d -> p b e d"),
                               PS[5 + i % 3][:, :].rearrange("p (b e d) -> p b e d", b=SB, e=A2)).then_inc(x2_cp[0], 1)

        def dve_ln_centre(dve, j, par):
            z = zc[:, par].rearrange("p e b d -> p (e b) d")
            dve.wait_ge(ln_z, LZ * j + 2)
            nc.vector.tensor_reduce(ln_mu[:, par], z, op=ALU.add, axis=AX.X).then_inc(ln_v, 1)
            dve.wait_ge(ln_v, LV * j + 1)
            nc.vector.scalar_tensor_tensor(out=z, in0=bcast(ln_mu[:, par], 2, D), scalar=-1.0 / D, in1=z,
                                           op0=ALU.mult, op1=ALU.add).then_inc(ln_v, 1)

        def dve_ln_rstd(dve, j, par):
            dve.wait_ge(ln_a, LA * j + 1)
            nc.vector.tensor_reduce(ln_var[:, par], sq[:, 0:512].rearrange("p (t d) -> p t d", d=D), op=ALU.add,
                                    axis=AX.X).then_inc(ln_v, 1)
            dve.wait_ge(ln_v, LV * j + 3)
            nc.vector.tensor_scalar(ln_ve[:, par], ln_var[:, par], 1.0 / D, EPS, ALU.mult, ALU.add).then_inc(ln_v, 1)

        def dve_sums(dve, m):
            for k in range(4):
                dve.wait_ge(s_exp, 4 * m + k + 1)
                nc.vector.tensor_reduce(sums[:, 32 * k:32 * k + 32], S_sb[:, 8 * k:8 * k + 8]
                                        .rearrange("p q a n -> p (q a) n"), op=ALU.add, axis=AX.X).then_inc(p_sum, 1)
            dve.wait_ge(p_sum, 4 * (m + 1))
            if not isinstance(m, int) or m >= 1:
                dve.wait_ge(p_nrm, 4 * m)
            nc.vector.reciprocal(rden[:, :], sums[:, :]).then_inc(p_rec, 1)

        def dve_period(dve, j, par, tail=True, B=True, A=True):
            s, m = j - 2, j - 1
            if A:
                dve_ln_centre(dve, j, par)
            if tail:
                dve_sums(dve, m)
            if B:
                for k in range(4):
                    dve.wait_ge(pt_mm, 4 * s + k + 1)
                    nc.vector.tensor_copy(PT[:, 8 * k:8 * k + 8].rearrange("p q m -> p (q m)"),
                                          bank_b(k)[:, :].bitcast(f16)).then_inc(pt_ok, 1)
            if A:
                dve_ln_rstd(dve, j, par)
            if B:
                for k in range(HP):
                    dve.wait_ge(o_mm, HP * s + k + 1)
                    dve.wait_ge(g_th, HP * s + k + 1)
                    nc.vector.scalar_tensor_tensor(out=og[:, k], in0=th[:, par, k], scalar=1.0, in1=bank_b(k)[:, :],
                                                   op0=ALU.add, op1=ALU.mult).then_inc(o_ok, 1)
                dve.wait_ge(w_mm, s + 1)
                v = xT[:, bass.ds(s * COLS, COLS)]
                nc.vector.scalar_tensor_tensor(out=v, in0=bank_w[:, :], scalar=bo_col[:, 0:1], in1=v,
                                               op0=ALU.add, op1=ALU.add).then_inc(x1_ok, 1)
            if A:
                for h in range(H):
                    dve.wait_ge(t_hi, H * j + h + 1)
                    nc.vector.tensor_tensor(t_sb[:, LO, :, h], bank_tg(h)[:, :].rearrange("p (q i) -> p q i", i=N),
                                            t_sb[:, HI, :, h], ALU.subtract).then_inc(t_lo, 1)
                for k in range(4):
                    S = bank_s(k)[:, :].rearrange("p (r n) -> p r n", n=N)
                    dve.wait_ge(s_mm, 4 * j + k + 1)
                    nc.vector.tensor_reduce(nmax[:, k % 2], S, op=ALU.max, axis=AX.X).then_inc(s_max, 1)
                    if tail:
                        dve.wait_ge(p_lo, 4 * m + k + 1)
                    dve.wait_ge(s_max, 4 * j + k + 1)
                    nc.vector.tensor_tensor(S_sb[:, 8 * k:8 * k + 8].rearrange("p q a n -> p (q a) n"), S,
                                            bcast(nmax[:, k % 2], 2, N), ALU.subtract).then_inc(s_sub, 1)
            if B:
                dve.wait_ge(x1_ok, s + 1)
                nc.vector.tensor_reduce(st1[:, 0, bass.ds(s, 1)].rearrange("p s n -> p (s n)"),
                                        xT[:, bass.ds(s * COLS, COLS)].rearrange("p (q n) -> p n q", n=N),
                                        op=ALU.add, axis=AX.X).then_inc(x1_st, 1)
                dve.wait_ge(x1_sq, s + 1)
                nc.vector.tensor_reduce(st1[:, 1, bass.ds(s, 1)].rearrange("p s n -> p (s n)"),
                                        sqx[:, :].rearrange("p (q n) -> p n q", n=N),
                                        op=ALU.add, axis=AX.X).then_inc(x1_st, 1)

        def dve_weights2(dve):
            dve.wait_ge(wT_mm, 4)
            for g in range(A2):
                rows = slice(D * g, D * g + D)
                for kind, scale in ((0, 1.0), (1, 0.5)):
                    nc.vector.tensor_scalar(W1_bd[rows, HI, kind, g].rearrange("p m d -> p (m d)"),
                                            PS[6][rows, 64 * kind:64 * kind + 64], scale, None,
                                            ALU.mult).then_inc(wprep, 1)
                nc.vector.tensor_copy(Wgo_bd[rows, HI, g], PS[6][rows, 128:160]).then_inc(wprep, 1)
                nc.vector.tensor_copy(Wlo_bd[rows, g], PS[6][rows, 160:192]).then_inc(wprep, 1)
            dve.wait_ge(wprep, 11 + 16)
            for g in range(A2):
                rows = slice(D * g, D * g + D)
                for kind, scale in ((0, 1.0), (1, 0.5)):
                    nc.vector.scalar_tensor_tensor(out=W1_bd[rows, LO, kind, g].rearrange("p m d -> p (m d)"),
                                                   in0=PS[6][rows, 64 * kind:64 * kind + 64], scalar=scale,
                                                   in1=W1_bd[rows, HI, kind, g].rearrange("p m d -> p (m d)"),
                                                   op0=ALU.mult, op1=ALU.subtract).then_inc(wprep, 1)
                nc.vector.tensor_tensor(Wgo_bd[rows, LO, g], PS[6][rows, 128:160], Wgo_bd[rows, HI, g],
                                        ALU.subtract).then_inc(wprep, 1)
            dve.wait_ge(wts2_in, WTS2)
            nc.vector.tensor_scalar(b1_in[:, 1], b1_in[:, 1], 0.5, None, ALU.mult).then_inc(wprep, 1)
            n = 11 + 16 + 12 + 1
            rest = b1_in
            for r in range(3):
                dve.wait_ge(wprep, n)
                nc.vector.tensor_copy(b1_s[:, r], rest if r else b1_in[:, :, :, :]).then_inc(wprep, 1)
                n += 1
                dve.wait_ge(wprep, n)
                if r < 2:
                    nc.vector.tensor_tensor(b1_r[:, r], rest if r else b1_in[:, :, :, :], b1_s[:, r],
                                            ALU.subtract).then_inc(wprep, 1)
                    n += 1
                    rest = b1_r[:, r]
            for r in range(3):
                row = slice(32 * r, 32 * r + 1)
                nc.vector.tensor_copy(B1[row, :, :, :, :].rearrange("p k e m d -> p k e (m d)"),
                                      bcast(b1_s[row, r].rearrange("p k m d -> p k (m d)"), 2, A2)).then_inc(wprep, 1)
            n += 3
            return n

        WPREP = 11 + 16 + 12 + 1 + 5 + 3

        @block.vector
        def _(dve):
            def zero(v):
                return nc.vector.memset(v, 0.0)
            zero(A_bd[:, :, :, :, :].rearrange("p k h e d -> p (k h e d)").bitcast(f32))
            zero(Wg_bd[:, :, :, :, :].rearrange("p k h e c -> p (k h e c)").bitcast(f32))
            zero(Wv_bd[:, :, :, :].rearrange("p h e c -> p (h e c)")).then_inc(zeros_w, 1)
            zero(Wo_bd[:, :, :, :].rearrange("p k e d -> p (k e d)")).then_inc(zeros_w, 1)
            zero(b1_in[:, :, :, :].rearrange("p k m d -> p (k m d)")).then_inc(zeros_w, 1)
            zero(B1[:, :, :, :, :].rearrange("p k e m d -> p (k e m d)").bitcast(f32))
            zero(W1_bd[:, :, :, :, :, :].rearrange("p l k e m d -> p (l k e m d)").bitcast(f32))
            zero(Wgo_bd[:, :, :, :].rearrange("p l e d -> p (l e d)").bitcast(f32))
            zero(Wlo_bd[:, :, :].rearrange("p e d -> p (e d)"))
            nc.vector.memset(ones_bf[:, :], 1.0)
            nc.vector.memset(ones_col[:, :], 1.0)
            nc.vector.memset(allsum[:, 0], 1.0 / (A2 * N * D))
            nc.vector.memset(allsum[:, 1], 1.0 / (N * L * L * D)).then_inc(zeros_w, 1)
            for e in range(A2):
                dve.wait_ge(x_in[e], 16)
                nc.vector.tensor_reduce(gn_part[:, 0, :, e], x_tok[:, e].rearrange("p b d -> p d b"), op=ALU.add,
                                        axis=AX.X).then_inc(gn_ok, 1)
                dve.wait_ge(sq_ok, e + 1)
                nc.vector.tensor_reduce(gn_part[:, 1, :, e], sq[:, :].rearrange("p (b d) -> p d b", d=D), op=ALU.add,
                                        axis=AX.X).then_inc(sqred, 1)
            dve.wait_ge(gn_ok, 4)
            dve.wait_ge(sqred, 4)
            nc.vector.tensor_reduce(gn_sum[:, :, :], gn_part[:, :, :, :], op=ALU.add, axis=AX.X).then_inc(gn_ok, 1)
            dve.wait_ge(gn_mm, 1)
            nc.vector.tensor_copy(gn_mv[:, :, :].rearrange("p k d -> p (k d)"), PS[0][:, 0:2 * D]).then_inc(gn_ok, 1)
            dve.wait_ge(gn_ok, 6)
            nc.vector.tensor_tensor(gn_tmp[:, 0], gn_mv[:, 0], gn_mv[:, 0], ALU.mult).then_inc(gn_ok, 1)
            dve.wait_ge(gn_ok, 7)
            nc.vector.scalar_tensor_tensor(out=gn_tmp[:, 1], in0=gn_mv[:, 1], scalar=EPS, in1=gn_tmp[:, 0],
                                           op0=ALU.add, op1=ALU.subtract).then_inc(gn_ok, 1)
            dve.wait_ge(rsq, 1)
            nc.vector.scalar_tensor_tensor(out=gn_sh[:, :], in0=gn_mv[:, 0], scalar=-1.0, in1=gn_r[:, :],
                                           op0=ALU.mult, op1=ALU.mult).then_inc(gn_ok, 1)
            dve.wait_ge(wT_mm, 1)
            nc.vector.tensor_copy(wqT[:, :, :], bcast(PS[4][:, 0:D], 1, A2)).then_inc(wprep, 1)
            nc.vector.tensor_copy(wkT[:, :], PS[4][:, D:2 * D]).then_inc(wprep, 1)
            dve.wait_ge(wprep, 1)
            dve.wait_ge(zeros_z, NZ_MASKS)
            nc.vector.tensor_tensor(wqTm, bcast(wqT[:, :, :].rearrange("p e d -> p (e d)"), 1, H),
                                    bcast(headmask[:, :], 2, 128), ALU.mult).then_inc(wprep, 1)
            dve.wait_ge(wprep_a, 5)
            for g in range(A2):
                rows = slice(D * g, D * g + D)
                nc.vector.scalar_tensor_tensor(out=A_bd[rows, LO, :, g], in0=PS[1][rows, 0:256]
                                               .rearrange("p (h d) -> p h d", h=H), scalar=0.25,
                                               in1=A_bd[rows, HI, :, g], op0=ALU.mult,
                                               op1=ALU.subtract).then_inc(wprep, 1)
            dve.wait_ge(wprep_a, 9)
            for g in range(A2):
                rows = slice(D * g, D * g + D)
                nc.vector.tensor_tensor(Wg_bd[rows, LO, :, g], wg_in[rows], Wg_bd[rows, HI, :, g],
                                        ALU.subtract).then_inc(wprep, 1)
            for j in range(2):
                dve_period(dve, j, j % 2, tail=j >= 1, B=False)
                if j == 0:
                    assert dve_weights2(dve) == WPREP
            with dve.Fori(0, (NS - 2) // 2) as it:
                for par in range(2):
                    dve_period(dve, 2 * it + 2 + par, par)
            dve_period(dve, NS, 0, A=False)
            dve_period(dve, NS + 1, 1, tail=False, A=False)

            def step(n, ins):
                ins.then_inc(g2_ok, 1)
                dve.wait_ge(g2_ok, n)
            dve.wait_ge(x1_st, 2 * NS)
            step(1, nc.vector.tensor_reduce(g2[:, 0:2], st1[:, :, :, :].rearrange("p k s n -> p k n s"),
                                            op=ALU.add, axis=AX.X))
            dve.wait_ge(g2_mm, 1)
            step(2, nc.vector.tensor_copy(g2[:, 2:4].rearrange("p k n -> p (k n)"), PS[0][:, 0:2 * N]))
            step(3, nc.vector.tensor_tensor(g2[:, 4], g2[:, 2], g2[:, 2], ALU.mult))
            step(4, nc.vector.tensor_tensor(g2[:, 8], g2[:, 3], g2[:, 4], ALU.subtract))
            step(5, nc.vector.tensor_scalar(g2[:, 5], g2[:, 8], EPS, None, ALU.add))
            dve.wait_ge(rsq, 2)
            step(6, nc.vector.tensor_tensor(g2[:, 7], g2[:, 8], g2[:, 6], ALU.mult))
            step(7, nc.vector.tensor_tensor(g2[:, 9], g2[:, 7], g2[:, 6], ALU.mult))
            step(8, nc.vector.tensor_reduce(col[:, V:V + 1], g2[:, 9], op=ALU.add, axis=AX.X))
            dve.wait_ge(g2_mm, 2)
            step(9, nc.vector.tensor_scalar(col[:, RV:RV + 1], PS[1][:, 0:1], EPS, None, ALU.add))
            dve.wait_ge(rsq, 3)
            step(10, nc.vector.tensor_tensor(col[:, SC:SC + 1], col[:, T0:T0 + 1], col[:, Ain:Ain + 1], ALU.mult))
            step(11, nc.vector.tensor_scalar(g2[:, 10], g2[:, 6], col[:, SC:SC + 1], None, ALU.mult))
            step(12, nc.vector.scalar_tensor_tensor(out=g2[:, 4], in0=g2[:, 2], scalar=-1.0, in1=g2[:, 10],
                                                    op0=ALU.mult, op1=ALU.mult))
            step(13, nc.vector.tensor_scalar(g2[:, 11], g2[:, 4], col[:, Bin:Bin + 1], None, ALU.add))
            step(14, nc.vector.tensor_scalar(col[:, BGH:BGH + 1], col[:, Bgo:Bgo + 1], 0.5, None, ALU.mult))
            dve.wait_ge(g2_mm, 3)
            step(15, nc.vector.tensor_copy(col[:, RW:RW + 1], PS[2][:, 0:1]))

            def z1_low(f):
                dve.wait_ge(z1_h, f + 1)
                nc.vector.tensor_tensor(z1[LO][:, f].rearrange("p n b -> p (n b)"), z1f[f % 2],
                                        z1[HI][:, f].rearrange("p n b -> p (n b)"), ALU.subtract).then_inc(z1_l, 1)
            for f in range(A4):
                if f >= 2:
                    dve.wait_ge(z1_l, f - 1)
                nc.vector.tensor_tensor(z1f[f % 2].rearrange("p (n b) -> p n b", n=N),
                                        xT[:, :].rearrange("p (b f n) -> p f n b", f=A4, n=N)[:, f],
                                        bcast(g2[:, 10], 2, L), ALU.mult).then_inc(z1_m, 1)
                if f:
                    z1_low(f - 1)
            z1_low(A4 - 1)

            for i in range(4 * A4):
                g, f = divmod(i, A4)
                if f == 0 and g >= 2:
                    dve.wait_ge(k_mm, 2 * (g - 1))
                    dve.wait_ge(bbd_ld[g % 2], 64 * (g // 2))
                dve.wait_ge(pj_th, i + 1)
                lin = PS[i % 3][:, 256:512].rearrange("p (a m c) -> p a m c", a=A2, m=2)
                for m, dst in ((0, a_buf), (1, b_buf)):
                    nc.vector.scalar_tensor_tensor(out=dst[g % 2][:, A2 * f:A2 * f + A2], in0=gt[i % 3][:, :, m],
                                                   scalar=1.0, in1=lin[:, :, m], op0=ALU.add,
                                                   op1=ALU.mult).then_inc(pj_ok, 1)

            def kstep(n, ins):
                ins.then_inc(k_ok, 1)
                dve.wait_ge(k_ok, n)
            dve.wait_ge(k_cp, 8)
            dve.wait_ge(k_sq, 8)
            kstep(1, nc.vector.tensor_reduce(ksum2[:, :], ksum[:, :, :], op=ALU.add, axis=AX.X))
            dve.wait_ge(ks_mm, 1)
            kstep(2, nc.vector.tensor_copy(g2[:, 0, 0:2], PS[0][:, 0:2]))
            kstep(3, nc.vector.tensor_tensor(col[:, T0:T0 + 1], g2[:, 0, 0:1], g2[:, 0, 0:1], ALU.mult))
            kstep(4, nc.vector.tensor_tensor(col[:, V:V + 1], g2[:, 0, 1:2], col[:, T0:T0 + 1], ALU.subtract))
            kstep(5, nc.vector.tensor_scalar(col[:, RV:RV + 1], col[:, V:V + 1], EPS, None, ALU.add))
            dve.wait_ge(rsq, 4)
            kstep(6, nc.vector.tensor_tensor(col[:, SC:SC + 1], col[:, KR:KR + 1], col[:, Aout:Aout + 1], ALU.mult))
            kstep(7, nc.vector.scalar_tensor_tensor(out=col[:, T0:T0 + 1], in0=g2[:, 0, 0:1], scalar=-1.0,
                                                    in1=col[:, SC:SC + 1], op0=ALU.mult, op1=ALU.mult))
            kstep(8, nc.vector.tensor_tensor(col[:, KT:KT + 1], col[:, T0:T0 + 1], col[:, Bout:Bout + 1], ALU.add))
            kstep(9, nc.vector.tensor_tensor(col[:, V:V + 1], col[:, KT:KT + 1], col[:, RW:RW + 1], ALU.mult))
            kstep(10, nc.vector.tensor_tensor(col[:, T0:T0 + 1], col[:, V:V + 1], col[:, Blo:Blo + 1], ALU.add))
            kstep(11, nc.vector.tensor_scalar(col[:, CV:CV + 1], col[:, T0:T0 + 1], 0.5, None, ALU.mult))
            kstep(12, nc.vector.tensor_scalar(col[:, KS:KS + 1], col[:, SC:SC + 1], 0.5, None, ALU.mult))
            for f in range(A4):
                v = x2[:, 512 * f:512 * f + 512]
                dve.wait_ge(lo_mm, f + 1)
                nc.vector.tensor_scalar(v, PS[3 + f % 2][:, :], col[:, KS:KS + 1], col[:, CV:CV + 1], ALU.mult,
                                        ALU.add).then_inc(lo_s, 1)
                dve.wait_ge(lo_s, f + 1)
                dve.wait_ge(go_th, f + 1)
                nc.vector.scalar_tensor_tensor(out=v, in0=tg[:, 512 * f:512 * f + 512], scalar=1.0, in1=v,
                                               op0=ALU.add, op1=ALU.mult).then_inc(lo_g, 1)
            for i in range(1, NS, 2):
                dve.wait_ge(x2_mm, i + 1)
                nc.vector.tensor_copy(out_tok[:, :, SB * i:SB * i + SB].rearrange("p e b d -> p b e d"),
                                      PS[5 + i % 3][:, :].rearrange("p (b e d) -> p b e d", b=SB, e=A2)
                                      ).then_inc(x2_cp[1], 1)

        def mm(o, l, r, start=True, stop=True):
            return nc.tensor.matmul(o, l, r, start=start, stop=stop)

        def split_mm(o, wt, mv):
            mm(o, wt[HI], mv[HI], True, False)
            mm(o, wt[LO], mv[HI], False, False)
            return mm(o, wt[HI], mv[LO], False, True)

        def pe_A(pe, j, par):
            pe.wait_ge(ln_z, LZ * (j + 1))
            if not isinstance(j, int) or j >= 2:
                pe.wait_ge(x1_ok, j - 1)
            zt = bank_w[:, :].bitcast(f16)
            tok = zn_tok[:, par].rearrange("p e d b k -> p (e d) b k")
            for k in (HI, LO):
                for b in range(SB):
                    at = 128 * (SB * k + b)
                    last = nc.tensor.transpose(zt[:, at:at + 128], tok[:, :, b, k], ident16[:, :])
            last.then_inc(zT_mm, 1)
            pe.wait_ge(zT_ok, j + 1)
            for h in range(H):
                if h >= 3:
                    pe.wait_ge(t_lo, H * j + h - 2)
                elif not isinstance(j, int) or j >= 1:
                    pe.wait_ge(g_th, HP * (j - 1) + h + 2)
                split_mm(bank_tg(h)[:, :], [A_bd[:, k, h].rearrange("p e d -> p (e d)") for k in (HI, LO)],
                         [znT[:, k] for k in (HI, LO)]).then_inc(t_mm, 1)
            for k in range(HP):
                if k < 3:
                    pe.wait_ge(t_lo, H * j + H - 2 + k)
                else:
                    pe.wait_ge(g_th, HP * j + 1)
                split_mm(bank_tg(H + k)[:, :],
                         [Wg_bd[:, p, 2 * k:2 * k + 2].rearrange("p h e c -> p (h e c)") for p in (HI, LO)],
                         [znT[:, p] for p in (HI, LO)]).then_inc(g_mm, 1)
            pe.wait_ge(zbd_ld, 64 * (j + 1))
            for k in range(4):
                if k >= 2:
                    pe.wait_ge(s_sub, 4 * j + k - 1)
                elif not isinstance(j, int) or j >= 1:
                    pe.wait_ge(s_sub, 4 * (j - 1) + k + 3)
                for q in range(8 * k, 8 * k + 8):
                    last = split_mm(bank_s(k)[:, 64 * (q % 8):64 * (q % 8) + 64],
                                    [t_sb[:, p, q].rearrange("p h i -> p (h i)") for p in (HI, LO)],
                                    [zbd[:, :, p, N * q:N * q + N] for p in (HI, LO)])
                last.then_inc(s_mm, 1)

        def pe_B(pe, s, par, half):
            for k in range(4):
                pe.wait_ge(p_lo, 4 * s + k + 1)
                if k >= 2:
                    pe.wait_ge(pt_ok, 4 * s + k - 1)
                for q in range(8 * k, 8 * k + 8):
                    last = nc.tensor.transpose(bank_b(k)[:, :].bitcast(f16)[:, 128 * (q % 8):128 * (q % 8) + 128],
                                               P2[:, q].rearrange("p k m -> p (k m)"), ident16[:, :])
                last.then_inc(pt_mm, 1)
            pe.wait_ge(Z_ld[par], 128 * (half + 1))
            for k in range(8):
                if k < 2:
                    pe.wait_ge(pt_ok, 4 * s + k + 3)
                else:
                    pe.wait_ge(u_ok, 8 * s + k - 1)
                for q in range(4 * k, 4 * k + 4):
                    b, f = divmod(q, A4)
                    o = bank_b(k)[:, 128 * (q % 4):128 * (q % 4) + 128]
                    Zq = Z[:, par, f].rearrange("p e d b k -> p (e d) b k")[:, :, b]
                    mm(o, Zq[:, :, HI], PT[:, q], True, False)
                    last = mm(o, Zq[:, :, LO], PT[:, q], False, True)
                last.then_inc(u_mm, 1)
            pe.wait_ge(u_ok, 8 * (s + 1))
            for k in range(HP):
                if k >= 2:
                    pe.wait_ge(o_ok, HP * s + k - 1)
                for r in range(2):
                    last = mm(bank_b(k)[64 * r:64 * r + 64], Wv_bd[:, 2 * k + r].rearrange("p e c -> p (e c)"),
                              u_sb[:, 2 * k + r].rearrange("p q i -> p (q i)"))
                last.then_inc(o_mm, 1)
            for k in range(HP):
                pe.wait_ge(o_ok, HP * s + k + 1)
                last = mm(bank_w[:, :], Wo_h[:, k].rearrange("p e d -> p (e d)"), og[:, k], k == 0, k == HP - 1)
            last.then_inc(w_mm, 1)

        @block.tensor
        def _(pe):
            pe.wait_ge(wts_in, WTS)
            pe.wait_ge(zeros_z, NZ_MASKS)
            for k in range(2):
                last = nc.tensor.transpose(PS[4][:, D * k:D * k + D], wq_in[:, k], ident[0:D, 0:D])
            last.then_inc(wT_mm, 1)
            pe.wait_ge(xp_ok, A2)
            for i in range(NS):
                if i >= 2:
                    pe.wait_ge(xT_ok, i - 1)
                for b in range(SB):
                    last = nc.tensor.transpose(PS[2 + i % 2][:, 128 * b:128 * b + 128], x_perm[:, SB * i + b].rearrange("p e d -> p (e d)"), ident[:, :])
                last.then_inc(xT_mm, 1)
                if i == 1:
                    pe.wait_ge(gn_ok, 5)
                    mm(PS[0][:, 0:2 * D], seqsum[:, :], gn_sum[:, :, :].rearrange("p k d -> p (k d)")
                       ).then_inc(gn_mm, 1)
                    pe.wait_ge(wprep, 3)
                    for h in range(H):
                        last = mm(PS[1][:, D * h:D * h + D], wqTm[:, h], wkT[:, :])
                    last.then_inc(wT_mm, 1)
                    pe.wait_ge(wts2_in, WTS2)
                    nc.tensor.transpose(PS[6][:, 0:128], w1_in[:, :, :].rearrange("p g d -> p (g d)"),
                                        ident[:, :]).then_inc(wT_mm, 1)
                    nc.tensor.transpose(PS[6][:, 128:192], w2_in[:, :, :].rearrange("p g d -> p (g d)"),
                                        ident[0:64, 0:64]).then_inc(wT_mm, 1)
            pe.wait_ge(xT_ok, NS)
            pe.wait_ge(wprep, 11)
            pe.wait_ge(wprep_a, 13)
            for j in range(2):
                pe_A(pe, j, j % 2)
            pe.wait_ge(wprep, WPREP)
            with pe.Fori(0, (NS - 2) // 2) as it:
                for par in range(2):
                    pe_B(pe, 2 * it + par, par, it)
                    pe_A(pe, 2 * it + 2 + par, par)
            pe_B(pe, NS - 2, 0, (NS - 2) // 2)
            pe_B(pe, NS - 1, 1, (NS - 2) // 2)

            pe.wait_ge(g2_ok, 1)
            mm(PS[0][:, 0:2 * N], chsum[:, :], g2[:, 0:2].rearrange("p k n -> p (k n)")).then_inc(g2_mm, 1)
            pe.wait_ge(g2_ok, 8)
            mm(PS[1][:, 0:1], allsum[:, 0], col[:, V:V + 1]).then_inc(g2_mm, 1)
            mm(PS[2][:, 0:1], Wlo_bd[:, :, :].rearrange("p e d -> p (e d)"), ones_col[:, :]).then_inc(g2_mm, 1)
            pe.wait_ge(g2_ok, 15)

            def project(g):
                for f in range(A4):
                    i = A4 * g + f
                    if g == 0:
                        pe.wait_ge(z1_l, f + 1)
                    if i >= 3:
                        pe.wait_ge(pj_ok, 2 * (i - 2))
                    o = PS[i % 3][:, :]
                    zz = [z1[p][:, f, 4 * g:4 * g + 4].rearrange("p n b -> p (n b)") for p in (HI, LO)]
                    W = [W1_bd[:, p].rearrange("p k e m d -> p (k e m d)") for p in (HI, LO)]
                    mm(o, ones_bf[:, :], B1[:, :, :, :, :].rearrange("p k e m d -> p (k e m d)"), True, False)
                    mm(o, zz[HI], W[HI], False, False)
                    mm(o, zz[LO], W[HI], False, False)
                    mm(o, zz[HI], W[LO], False, True).then_inc(pj_mm, 1)

            def triangle(g):
                pe.wait_ge(bbd_ld[g % 2], 64 * (g // 2 + 1))
                for h in range(2):
                    i = 2 * g + h
                    if i >= 4:
                        pe.wait_ge(k_sq, i - 3)
                    for c in range(16 * h, 16 * h + 16):
                        c8, c4 = divmod(c, 4)
                        last = mm(PS[3 + i % 4][L * c4:L * c4 + L, 128 * (c8 % 4):128 * (c8 % 4) + 128],
                                  a_buf[g % 2][:, :, c], bbd[g % 2][:, :, :, c])
                    last.then_inc(k_mm, 1)

            project(0)
            project(1)
            triangle(0)
            project(2)
            triangle(1)
            project(3)
            triangle(2)
            for f in range(A4):
                if f < 3:
                    pe.wait_ge(pj_ok, 64)
                else:
                    pe.wait_ge(go_th, f - 2)
                split_mm(PS[f % 3][:, :], [Wgo_bd[:, p].rearrange("p e d -> p (e d)") for p in (HI, LO)],
                         [z1[p][:, f].rearrange("p n b -> p (n b)") for p in (HI, LO)]).then_inc(go_mm, 1)
            triangle(3)
            pe.wait_ge(go_th, A4)
            pe.wait_ge(k_ok, 1)
            mm(PS[0][:, 0:2], allsum[:, 1], ksum2[:, :]).then_inc(ks_mm, 1)
            for g in range(4):
                pe.wait_ge(kT_ld[g], 64)
            for f in range(A4):
                if f >= 2:
                    pe.wait_ge(lo_s, f - 1)
                mm(PS[3 + f % 2][:, :], Wlo_bd[:, :, :].rearrange("p e d -> p (e d)"),
                   kT[:, 512 * f:512 * f + 512]).then_inc(lo_mm, 1)
            pe.wait_ge(x2_ok, A4)
            for i in range(NS):
                if i >= 3:
                    pe.wait_ge(x2_cp[(i - 3) % 2], (i - 3) // 2 + 1)
                for b in range(SB):
                    last = nc.tensor.transpose(PS[5 + i % 3][:, 128 * b:128 * b + 128],
                                               x2.rearrange("p (m b) -> p m b", b=L)[:, :, SB * i + b],
                                               ident[:, :])
                last.then_inc(x2_mm, 1)


_INS = ["x", "L0_conv_ln_w", "L0_conv_ln_b", "L0_conv_Wq", "L0_conv_Wk", "L0_conv_Wv", "L0_conv_Wg", "L0_conv_bg",
        "L0_conv_Wo", "L0_conv_bo", "L1_conv_alpha_in", "L1_conv_beta_in", "L1_conv_W_la", "L1_conv_b_la",
        "L1_conv_W_ga", "L1_conv_b_ga", "L1_conv_W_lb", "L1_conv_b_lb", "L1_conv_W_gb", "L1_conv_b_gb",
        "L1_conv_alpha_o", "L1_conv_beta_o", "L1_conv_W_go", "L1_conv_b_go", "L1_conv_W_lo", "L1_conv_b_lo"]


def kernel(**inputs):
    import numpy as _np
    import concourse.bacc as _bacc
    from concourse.bass_utils import run_bass_kernel_spmd as _run

    nc = _bacc.Bacc("TRN2", target_bir_lowering=False, num_devices=1)
    arrays, args = {}, []
    for name in _INS:
        a = _np.ascontiguousarray(inputs[name])
        if name == "L0_conv_bg":
            a = _np.ascontiguousarray(a.reshape(HP, 2, C).transpose(1, 2, 0))
        arrays[f"in_{name}"] = a
        args.append(nc.dram_tensor(f"in_{name}", a.shape, mybir.dt.from_np(a.dtype), kind="ExternalInput").ap())
    out = nc.dram_tensor("out_x", (N, L, L, D), f32, kind="ExternalOutput").ap()
    build(nc, *args, out)
    r = _run(nc, [arrays], core_ids=[0])
    return r.results[0]["out_x"]
```

```python
import concourse.bass as bass
from concourse import mybir
from contextlib import ExitStack

f32 = mybir.dt.float32
f16 = mybir.dt.float16
bf16 = mybir.dt.bfloat16
ACT = mybir.ActivationFunctionType
ALU = mybir.AluOpType
AX = mybir.AxisListType

N, L, D, H, C = 16, 32, 32, 8, 16
A2, A4 = 4, 8
SB = 4
NS = L // SB
QS = SB * A4
COLS = QS * N
HP = H // 2
EPS = 1e-5
HI, LO = 0, 1


def build(nc, x, ln_w, ln_b, Wq, Wk, Wv, Wg, bg, Wo, bo, al_in, be_in, W_la, b_la, W_ga, b_ga,
          W_lb, b_lb, W_gb, b_gb, al_o, be_o, W_go, b_go, W_lo, b_lo, out):
    ctx = ExitStack()
    with ctx:
        def sb(name, shape, dt=f32):
            return ctx.enter_context(nc.sbuf_tensor(name, shape, dt))

        sem_names = {}

        def sem(name):
            s = ctx.enter_context(nc.semaphore(name))
            sem_names[name] = s
            return s

        x_tok = sb("x_tok", [128, A2, L, D])
        xT = sb("xT", [128, NS * COLS])
        zc = sb("zc", [128, 2, A2, SB, D])
        sq = sb("sq", [128, 1024])
        sqx = sb("sqx", [128, COLS])
        zn_tok = sb("zn_tok", [128, 2, A2, D, SB, 2], f16)
        znT = sb("znT", [128, 2, COLS], f16)
        zbd = sb("zbd", [128, A2, 2, COLS], f16)
        Z = sb("Z", [128, 2, A4, A2, D, SB, 2], f16)
        t_sb = sb("t_sb", [128, 2, QS, H, N], f16)
        S_sb = sb("S_sb", [128, QS, A2, N])
        PP = sb("PP", [128, 2, QS, 128], f16)
        P2 = PP[:, 0].rearrange("p q (k m) -> p q k m", k=2)
        PT = PP[:, 1]
        u_sb = sb("u_sb", [128, H, QS, N])
        th = sb("th", [128, 2, HP, COLS])
        og = sb("og", [128, HP, COLS])
        sums = sb("sums", [128, QS * A2])
        rden = sb("rden", [128, QS * A2])
        nmax = sb("nmax", [128, 2, 32])

        ident = sb("ident", [128, 128])
        ident16 = sb("ident16", [128, 128], f16)
        seqsum = sb("seqsum", [128, 128])
        chsum = sb("chsum", [128, 128])
        allsum = sb("allsum", [128, 2, 128])
        headmask = sb("headmask", [128, H])
        wq_in = sb("wq_in", [D, 2, H * C])
        wqT = sb("wqT", [128, A2, D])
        wkT = sb("wkT", [128, D])
        wqTm = S_sb[:, 0:16].rearrange("p q a n -> p (q a n)").rearrange("p (h m) -> p h m", h=H)
        A_bd = sb("A_bd", [128, 2, H, A2, D], f16)
        wg_in = sb("wg_in", [128, H, C])
        Wg_bd = sb("Wg_bd", [128, 2, H, A2, C], f16)
        wv_in = sb("wv_in", [128, H, C])
        Wv_bd = sb("Wv_bd", [128, H, A2, C])
        Wo_bd = sb("Wo_bd", [128, HP, A2, D])
        Wo_h = sb("Wo_h", [128, HP, A2, D])
        bg_in = sb("bg_in", [128, HP])
        bg_h = sb("bg_h", [128, HP])
        w_bc = sb("w_bc", [128, D])
        b_bc = sb("b_bc", [128, D])
        bo_col = sb("bo_col", [128, 1])
        gn_part = sb("gn_part", [128, 2, D, A2])
        gn_sum = sb("gn_sum", [128, 2, D])
        gn_mv = sb("gn_mv", [128, 2, D])
        gn_tmp = sb("gn_tmp", [128, 3, D])
        gn_r = sb("gn_r", [128, D])
        gn_sh = sb("gn_sh", [128, D])
        minus_half = sb("minus_half", [128, D])
        ln_mu = sb("ln_mu", [128, 2, A2 * SB])
        ln_var = sb("ln_var", [128, 2, A2 * SB])
        ln_ve = sb("ln_ve", [128, 2, A2 * SB])
        ln_rs = sb("ln_rs", [128, 2, A2 * SB])
        st1 = sb("st1", [128, 2, NS, N])
        w1_in = sb("w1_in", [128, A2, D])
        w2_in = sb("w2_in", [64, A2, D])
        W1_f = sb("W1_f", [128, 2, 2, D])
        W1_bd = sb("W1_bd", [128, 2, 2, A2, 2, D], f16)
        W2_f = sb("W2_f", [128, 2, D])
        Wgo_bd = sb("Wgo_bd", [128, 2, A2, D], f16)
        Wlo_bd = sb("Wlo_bd", [128, A2, D])
        b1_in = sb("b1_in", [128, 2, 2, D])
        b1_r = sb("b1_r", [128, 2, 2, 2, D])
        b1_s = sb("b1_s", [128, 3, 2, 2, D], bf16)
        B1 = sb("B1", [128, 2, A2, 2, D], bf16)
        ones_bf = sb("ones_bf", [128, 128], bf16)
        ones_col = sb("ones_col", [128, 1])
        col = sb("col", [128, 16])
        g2 = sb("g2", [128, 12, N])
        ksum = sb("ksum", [128, 2, 8])
        ksum2 = sb("ksum2", [128, 2])
        (Bgo, Blo, Ain, Bin, Aout, Bout, V, RV, SC, KR, KS, KT, CV, T0, BGH, RW) = range(16)

        z1 = [t_sb[:, k].rearrange("p q h i -> p (q h i)").rearrange("p (a n b) -> p a n b", a=A4, n=N)
              for k in (HI, LO)]
        z1f = [zc[:, k].rearrange("p a b d -> p (a b d)") for k in (0, 1)]
        a_buf = [u_sb[:, 2 * k:2 * k + 2].rearrange("p h q i -> p (h q i)")
                 .rearrange("p (i c) -> p i c", c=D) for k in (0, 1)]
        b_buf = [u_sb[:, 4 + 2 * k:6 + 2 * k].rearrange("p h q i -> p (h q i)")
                 .rearrange("p (i c) -> p i c", c=D) for k in (0, 1)]
        x_perm = u_sb[:, :, :, :].rearrange("p h q i -> p (h q i)").rearrange("p (b e d) -> p b e d", b=L, e=A2)
        bbd = [PP[:, :, :, :].rearrange("p k q m -> p (k q m)").bitcast(f32)
               .rearrange("p (n j c) -> p n j c", n=4, j=L), x_tok[:, :, :, :]]
        gt = [S_sb[:, 4 * k:4 * k + 4].rearrange("p q a n -> p (q a n)")
              .rearrange("p (a m c) -> p a m c", a=A2, m=2) for k in range(3)]
        k_sb = og[:, :, :].rearrange("p h c -> p (h c)")
        kT = th[:, :, :, :].rearrange("p k h c -> p (k h c)")
        tg = Z[:, :, :, :, :, :, :].rearrange("p r f e d b k -> p (r f e d b k)").bitcast(f32)
        x2 = tg[:, 4096:8192]
        tg = tg[:, 0:4096]
        out_tok = u_sb[:, :, :, :].rearrange("p h q i -> p (h q i)").rearrange("p (a b d) -> p a b d", a=A2, b=L)

        zn_dram = nc.dram_tensor("zn_dram", [N, A4, NS, A2, D * SB * 2], f16, kind="Internal").ap()
        k_dram = nc.dram_tensor("k_dram", [D, A4, A2, N * L], f32, kind="Internal").ap()

        PS = [ctx.enter_context(nc.psum_tensor(f"PS{i}", [128, 512], f32)) for i in range(8)]
        bank_tg = lambda i: PS[i % 3]
        bank_s = lambda i: PS[3 + i % 2]
        bank_b = lambda i: PS[5 + i % 2]
        bank_u = lambda i: PS[(5, 6, 3, 4)[i % 4]]
        bank_w = PS[7]

        x_in = [sem(f"x_in{i}") for i in range(A2)]
        wts_in = sem("wts_in")
        wts2_in = sem("wts2_in")
        zeros_w = sem("zeros_w")
        zeros_z = sem("zeros_z")
        sq_ok = sem("sq_ok")
        sqred = sem("sqred")
        gn_ok = sem("gn_ok")
        rsq = sem("rsq")
        gn_mm = sem("gn_mm")
        wT_mm = sem("wT_mm")
        wprep = sem("wprep")
        wprep_a = sem("wprep_a")
        xp_ok = sem("xp_ok")
        xT_mm = sem("xT_mm")
        xT_ok = sem("xT_ok")
        ln_z = sem("ln_z")
        ln_v = sem("ln_v")
        ln_a = sem("ln_a")
        zn_st = [sem("zn_st0"), sem("zn_st1")]
        Z_ld = [sem("Z_ld0"), sem("Z_ld1")]
        zbd_ld = sem("zbd_ld")
        zT_mm = sem("zT_mm")
        zT_ok = sem("zT_ok")
        t_mm = sem("t_mm")
        t_hi = sem("t_hi")
        t_lo = sem("t_lo")
        g_mm = sem("g_mm")
        g_th = sem("g_th")
        s_mm = sem("s_mm")
        s_max = sem("s_max")
        s_sub = sem("s_sub")
        s_exp = sem("s_exp")
        p_sum = sem("p_sum")
        p_rec = sem("p_rec")
        p_nrm = sem("p_nrm")
        p_hi = sem("p_hi")
        p_lo = sem("p_lo")
        pt_mm = sem("pt_mm")
        pt_ok = [sem("pt_ok0"), sem("pt_ok1")]
        u_mm = sem("u_mm")
        u_ok = sem("u_ok")
        o_mm = sem("o_mm")
        o_ok = sem("o_ok")
        w_mm = sem("w_mm")
        x1_ok = sem("x1_ok")
        x1_sq = sem("x1_sq")
        x1_st = sem("x1_st")
        g2_ok = sem("g2_ok")
        g2_mm = sem("g2_mm")
        bbd_z = sem("bbd_z")
        z1_m = sem("z1_m")
        z1_b = sem("z1_b")
        z1_h = sem("z1_h")
        z1_l = sem("z1_l")
        pj_mm = sem("pj_mm")
        pj_th = sem("pj_th")
        pj_ok = sem("pj_ok")
        bbd_ld = [sem("bbd_ld0"), sem("bbd_ld1")]
        k_mm = sem("k_mm")
        k_cp = sem("k_cp")
        k_sq = sem("k_sq")
        k_st = sem("k_st")
        kT_ld = [sem(f"kT_ld{g}") for g in range(4)]
        go_mm = sem("go_mm")
        go_th = sem("go_th")
        k_ok = sem("k_ok")
        ks_mm = sem("ks_mm")
        lo_mm = sem("lo_mm")
        lo_s = sem("lo_s")
        lo_g = sem("lo_g")
        x2_ok = sem("x2_ok")
        x2_mm = sem("x2_mm")
        x2_cp = [sem("x2_cp0"), sem("x2_cp1")]
        out_st = sem("out_st")

        LZ, LV, LA = 7, 4, 2
        LOOPS = (NS - 4) // 2
        NZ_MASKS, NZ_Z = 15, 3
        WTS, WTS2 = 16 * 32, 16 * 48

        def bcast(ap, axis, n):
            v = ap.unsqueeze(axis)
            return v.to_broadcast([n if i == axis else s for i, s in enumerate(v.shape)])

        block = ctx.enter_context(nc.Block())
        x_src = x.rearrange("n (f e) b c -> (n f) e (b c)", e=A2)
        out_dst = out.rearrange("n (f e) b c -> f n e (b c)", e=A2)

        def sp_store(sp, j, par):
            sp.wait_ge(ln_z, LZ * (j + 1))
            sp.dma_start(zn_dram.rearrange("n f s e m -> (n f) s (e m)")[:, bass.ds(j, 1)],
                         zn_tok[:, par].rearrange("p e d b k -> p (e d b k)").unsqueeze(1)).then_inc(zn_st[par], 16)

        def sp_period(sp, j, par, half, last=False):
            sp.wait_ge(zT_ok, j + 1)
            for e in range(A2):
                rows = slice(D * e, D * e + D)
                sp.dma_start(zbd[rows, e], znT[rows]).then_inc(zbd_ld, 16)
            if not last:
                sp_store(sp, j + 1, 1 - par)
            else:
                sp.wait_ge(u_mm, 8 * (j - 1))
            sp.wait_ge(zn_st[par], 16 * (half + 1))
            for copy in range(2):
                for e in range(A2):
                    r0 = 64 * copy + N * e
                    sp.dma_start(Z[r0:r0 + N, par, :, e].rearrange("p f d b k -> p f (d b k)"),
                                 zn_dram[:, :, bass.ds(j, 1), e].rearrange("n f s m -> n (f s) m")
                                 ).then_inc(Z_ld[par], 16)

        @block.sync
        def _(sp):
            for e in range(A2):
                sp.dma_start(x_tok[:, e].rearrange("p b d -> p (b d)"), x_src[:, e]).then_inc(x_in[e], 16)
            for m, w in enumerate((W_ga, W_gb, W_la, W_lb)):
                for g in range(A2):
                    sp.dma_start(w1_in[D * m:D * m + D, g], w).then_inc(wts2_in, 16)
            for m, w in enumerate((W_go, W_lo)):
                for g in range(A2):
                    sp.dma_start(w2_in[D * m:D * m + D, g], w).then_inc(wts2_in, 16)
            sp.wait_ge(zeros_w, 3)
            for r in range(3):
                for m, b in enumerate((b_ga, b_gb, b_la, b_lb)):
                    sp.dma_start(b1_in[32 * r:32 * r + 1, m // 2, m % 2], b.unsqueeze(0)).then_inc(wts2_in, 16)
            for g in range(A2):
                sp.dma_start(col[D * g:D * g + D, Bgo:Bgo + 1], b_go.unsqueeze(1)).then_inc(wts2_in, 16)
                sp.dma_start(col[D * g:D * g + D, Blo:Blo + 1], b_lo.unsqueeze(1)).then_inc(wts2_in, 16)
            for k, v in ((Ain, al_in), (Bin, be_in), (Aout, al_o), (Bout, be_o)):
                sp.dma_start(col[:, k:k + 1], v.partition_broadcast(128)).then_inc(wts2_in, 16)

            sp.wait_ge(zeros_z, NZ_MASKS + NZ_Z)
            sp_store(sp, 0, 0)
            for j in range(3):
                sp_period(sp, j, j % 2, j // 2)
            with sp.Fori(0, LOOPS) as it:
                for i in range(2):
                    sp_period(sp, 2 * it + 3 + i, 1 - i, it + 1 + i)
            sp_period(sp, NS - 1, 1, NS // 2 - 1, last=True)

            def bbd_load(g):
                sp.wait_ge(pj_ok, 16 * (g + 1))
                if g == 0:
                    sp.wait_ge(bbd_z, 2)
                if g >= 2:
                    sp.wait_ge(k_mm, 2 * (g - 1))
                for n in range(4):
                    rows = slice(L * n, L * n + L)
                    sp.dma_start(bbd[g % 2][rows, n].rearrange("p j c -> p (j c)"),
                                 b_buf[g % 2][rows].rearrange("p j c -> p (j c)")).then_inc(bbd_ld[g % 2], 16)

            def k_move(g):
                sp.wait_ge(k_cp, 2 * (g + 1))
                sp.dma_start(k_dram.rearrange("(c8 c4) f e m -> c4 (f e) c8 m", c4=4)[:, :, :, 128 * g:128 * g + 128]
                             .rearrange("c4 i c8 m -> (c4 i) c8 m"),
                             k_sb.rearrange("p (h c m) -> p h c m", h=2, c=8)[:, g % 2]).then_inc(k_st, 16)
                sp.wait_ge(k_st, 16 * (g + 1))
                for e in range(A2):
                    sp.dma_start(kT.rearrange("p (f m) -> p f m", f=A4)[D * e:D * e + D, :, 128 * g:128 * g + 128],
                                 k_dram[:, :, e, 128 * g:128 * g + 128]).then_inc(kT_ld[g], 16)

            bbd_load(0)
            bbd_load(1)
            k_move(0)
            bbd_load(2)
            k_move(1)
            bbd_load(3)
            k_move(2)
            k_move(3)
            for i in range(NS):
                sp.wait_ge(x2_cp[i % 2], i // 2 + 1)
                for f in range(A4):
                    sp.dma_start(out_dst[f, :, :, SB * D * i:SB * D * (i + 1)],
                                 out_tok[N * f:N * f + N, :, SB * i:SB * (i + 1)].rearrange("p e b d -> p e (b d)")
                                 ).then_inc(out_st, 16)
            sp.wait_ge(out_st, 16 * NS * A4)

        def pool_ln_front(pool, j, par):
            z = zc[:, par].rearrange("p e b d -> p e (b d)").rearrange("p e (b d) -> p e b d", d=D)
            if not isinstance(j, int) or j >= 2:
                pool.wait_ge(ln_z, LZ * (j - 1))
            nc.gpsimd.tensor_tensor(z, x_tok[:, :, bass.ds(j * SB, SB), :],
                                    bcast(bcast(gn_r[:, :], 1, SB), 1, A2), ALU.mult).then_inc(ln_z, 1)
            pool.wait_ge(ln_z, LZ * j + 1)
            zf = zc[:, par].rearrange("p e b d -> p (e b) d")
            nc.gpsimd.tensor_tensor(zf, zf, bcast(gn_sh[:, :], 1, A2 * SB), ALU.add).then_inc(ln_z, 1)

        def pool_ln_back(pool, j, par):
            zf = zc[:, par].rearrange("p e b d -> p (e b) d")
            pool.wait_ge(ln_v, LV * (j + 1))
            nc.gpsimd.tensor_tensor(ln_rs[:, par], ln_ve[:, par], minus_half[:, 0:A2 * SB], ALU.pow).then_inc(ln_z, 1)
            pool.wait_ge(ln_z, LZ * j + 3)
            nc.gpsimd.tensor_tensor(zf, zf, bcast(ln_rs[:, par], 2, D), ALU.mult).then_inc(ln_z, 1)
            pool.wait_ge(ln_z, LZ * j + 4)
            nc.gpsimd.tensor_tensor(zf, zf, bcast(w_bc[:, :], 1, A2 * SB), ALU.mult).then_inc(ln_z, 1)
            pool.wait_ge(ln_z, LZ * j + 5)
            nc.gpsimd.tensor_tensor(zf, zf, bcast(b_bc[:, :], 1, A2 * SB), ALU.add).then_inc(ln_z, 1)

        def pool_ln_low(pool, j, par):
            pool.wait_ge(ln_a, LA * (j + 1))
            hl = zn_tok[:, par].rearrange("p e d b k -> p e b d k")
            nc.gpsimd.tensor_tensor(hl[:, :, :, :, LO], zc[:, par], hl[:, :, :, :, HI], ALU.subtract).then_inc(ln_z, 1)

        def pool_norm(pool, m, ks):
            pool.wait_ge(p_rec, 2 * m + ks[0] // 2 + 1)
            for k in ks:
                P = S_sb[:, 8 * k:8 * k + 8].rearrange("p q a n -> p (q a) n")
                nc.gpsimd.tensor_tensor(P, P, bcast(rden[:, 32 * k:32 * k + 32], 2, N), ALU.mult).then_inc(p_nrm, 1)

        def pool_plo(pool, m, ks):
            for k in ks:
                P = S_sb[:, 8 * k:8 * k + 8].rearrange("p q a n -> p q (a n)")
                pool.wait_ge(p_hi, 4 * m + k + 1)
                nc.gpsimd.tensor_tensor(P2[:, 8 * k:8 * k + 8, LO], P, P2[:, 8 * k:8 * k + 8, HI],
                                        ALU.subtract).then_inc(p_lo, 1)

        def pool_sqx(pool, s):
            pool.wait_ge(x1_ok, s + 1)
            v = xT[:, bass.ds(s * COLS, COLS)]
            nc.gpsimd.tensor_tensor(sqx[:, :], v, v, ALU.mult).then_inc(x1_sq, 1)

        def pool_period(pool, j, par, tail=True, LN=True, stats=True):
            if LN:
                pool_ln_front(pool, j + 1, 1 - par)
            if tail:
                pool_norm(pool, j - 1, (0, 1))
            if stats:
                pool_sqx(pool, j - 3)
            if tail:
                pool_norm(pool, j - 1, (2, 3))
            if LN:
                pool_ln_back(pool, j + 1, 1 - par)
                pool_ln_low(pool, j + 1, 1 - par)
            if tail:
                pool_plo(pool, j - 1, (0, 1, 2, 3))

        @block.gpsimd
        def _(pool):
            def rsqrt(sem_in, n, dst, src):
                pool.wait_ge(sem_in, n)
                nc.gpsimd.tensor_tensor(dst, src, minus_half[:, 0:dst.shape[-1]], ALU.pow).then_inc(rsq, 1)

            nc.gpsimd.memset(minus_half[:, :], -0.5).then_inc(zeros_z, 1)
            seq = seqsum[:, :].rearrange("p (n f) -> p n f", f=A4)
            chn = chsum[:, :].rearrange("p (e c) -> p e c", c=D)
            nc.gpsimd.memset(ident[:, :], 0.0).then_inc(zeros_z, 1)
            nc.gpsimd.memset(seqsum[:, :], 1.0 / (L * L)).then_inc(zeros_z, 1)
            nc.gpsimd.memset(headmask[:, :], 1.0).then_inc(zeros_z, 1)
            nc.gpsimd.memset(chsum[:, :], 0.0).then_inc(zeros_z, 1)
            pool.wait_ge(zeros_z, 5)
            nc.gpsimd.affine_select(out=ident[:, :], in_=ident[:, :], compare_op=ALU.not_equal, fill=1.0, base=0,
                                    pattern=[[-1, 128]], channel_multiplier=1).then_inc(zeros_z, 1)
            nc.gpsimd.affine_select(out=seq, in_=seq, compare_op=ALU.is_ge, fill=0.0, base=0,
                                    pattern=[[-A4, N], [0, A4]], channel_multiplier=1).then_inc(zeros_z, 1)
            nc.gpsimd.affine_select(out=headmask[:, :], in_=headmask[:, :], compare_op=ALU.is_ge, fill=0.0, base=0,
                                    pattern=[[-C, H]], channel_multiplier=1).then_inc(zeros_z, 1)
            pool.wait_ge(zeros_z, 8)
            nc.gpsimd.affine_select(out=seq, in_=seq, compare_op=ALU.is_ge, fill=0.0, base=A4 - 1,
                                    pattern=[[A4, N], [0, A4]], channel_multiplier=-1).then_inc(zeros_z, 1)
            nc.gpsimd.affine_select(out=headmask[:, :], in_=headmask[:, :], compare_op=ALU.is_ge, fill=0.0, base=C - 1,
                                    pattern=[[C, H]], channel_multiplier=-1).then_inc(zeros_z, 1)
            for k in range(A2):
                if k:
                    pool.wait_ge(zeros_z, 10 + k)
                nc.gpsimd.affine_select(out=chn, in_=chn, compare_op=ALU.not_equal, fill=1.0 / (L * L), base=-D * k,
                                        pattern=[[0, A2], [-1, D]], channel_multiplier=1).then_inc(zeros_z, 1)
            nc.gpsimd.tensor_copy(ident16[:, :], ident[:, :]).then_inc(zeros_z, 1)
            nc.gpsimd.memset(zbd[:, :, :, :].rearrange("p e k c -> p (e k c)").bitcast(f32), 0.0).then_inc(zeros_z, 1)
            for k in range(2):
                nc.gpsimd.memset(Z[:, k].rearrange("p f e d b k -> p (f e d b k)").bitcast(f32), 0.0).then_inc(zeros_z, 1)
            rsqrt(gn_ok, 8, gn_r[:, :], gn_tmp[:, 1])
            pool.wait_ge(gn_ok, 9)
            pool.wait_ge(wts_in, WTS)
            pool_ln_front(pool, 0, 0)
            pool_ln_back(pool, 0, 0)
            pool_ln_low(pool, 0, 0)
            for j in range(3):
                pool_period(pool, j, j % 2, tail=j >= 1, stats=False)
            with pool.Fori(0, LOOPS) as it:
                for i in range(2):
                    pool_period(pool, 2 * it + 3 + i, 1 - i)
            for j in range(NS - 1, NS + 2):
                pool_period(pool, j, j % 2, tail=j <= NS, LN=j < NS - 1)
            nc.gpsimd.memset(bbd[1].rearrange("p n j c -> p (n j c)"), 0.0).then_inc(bbd_z, 1)
            pool.wait_ge(u_mm, 8 * NS)
            nc.gpsimd.memset(bbd[0].rearrange("p n j c -> p (n j c)"), 0.0).then_inc(bbd_z, 1)
            pool_sqx(pool, NS - 1)
            rsqrt(g2_ok, 5, g2[:, 6], g2[:, 5])
            rsqrt(g2_ok, 9, col[:, T0:T0 + 1], col[:, RV:RV + 1])
            for f in range(A4):
                pool.wait_ge(z1_m, f + 1)
                v = z1f[f % 2].rearrange("p (n b) -> p n b", n=N)
                nc.gpsimd.tensor_tensor(v, v, bcast(g2[:, 11], 2, L), ALU.add).then_inc(z1_b, 1)
            rsqrt(k_ok, 5, col[:, KR:KR + 1], col[:, RV:RV + 1])
            for f in range(A4):
                pool.wait_ge(lo_g, f + 1)
                v = x2[:, 512 * f:512 * f + 512].rearrange("p (n b) -> p n b", n=N)
                nc.gpsimd.tensor_tensor(v, v, xT[:, :].rearrange("p (b f n) -> p f n b", f=A4, n=N)[:, f],
                                        ALU.add).then_inc(x2_ok, 1)

        def act_ln_square(act, j, par):
            act.wait_ge(ln_v, LV * j + 2)
            nc.scalar.activation(sq[:, 0:512], zc[:, par].rearrange("p e b d -> p (e b d)"),
                                 ACT.Square).then_inc(ln_a, 1)

        def act_ln_high(act, j, par, half):
            act.wait_ge(ln_z, LZ * j + 6)
            if not isinstance(j, int) or j >= 2:
                act.wait_ge(zn_st[par], 16 * half)
            nc.scalar.copy(zn_tok[:, par].rearrange("p e d b k -> p e b d k")[:, :, :, :, HI],
                           zc[:, par]).then_inc(ln_a, 1)

        def act_period(act, j, par, half, tail=True, B=True, A=True, LN=True):
            s, m = j - 2, j - 1

            def u_copies(ks):
                for k in ks:
                    act.wait_ge(u_mm, 8 * s + k + 1)
                    nc.scalar.copy(u_sb[:, :, 4 * k:4 * k + 4].rearrange("p h q i -> p q h i"),
                                   bank_u(k)[:, :].rearrange("p (q h i) -> p q h i", q=4, h=H)).then_inc(u_ok, 1)

            def p_high(ks):
                for k in ks:
                    act.wait_ge(p_nrm, 4 * m + k + 1)
                    if not isinstance(m, int) or m >= 1:
                        act.wait_ge(pt_mm, 4 * (m - 1) + k + 1)
                    nc.scalar.copy(P2[:, 8 * k:8 * k + 8, HI],
                                   S_sb[:, 8 * k:8 * k + 8].rearrange("p q a n -> p q (a n)")).then_inc(p_hi, 1)

            def t_high(hs):
                for h in hs:
                    act.wait_ge(t_mm, H * j + h + 1)
                    nc.scalar.copy(t_sb[:, HI, :, h], bank_tg(h)[:, :].rearrange("p (q i) -> p q i", i=N)).then_inc(t_hi, 1)

            def exps(ks):
                for k in ks:
                    act.wait_ge(s_sub, 4 * j + k + 1)
                    v = S_sb[:, 8 * k:8 * k + 8].rearrange("p q a n -> p (q a n)")
                    nc.scalar.activation(v, v, ACT.Exp).then_inc(s_exp, 1)

            def gates(ks):
                for k in ks:
                    act.wait_ge(g_mm, HP * j + k + 1)
                    nc.scalar.activation(th[:, par, k], bank_tg(H + k)[:, :], ACT.Tanh, bias=bg_h[:, k:k + 1],
                                         scale=0.5).then_inc(g_th, 1)

            def PT_copy(k):
                act.wait_ge(pt_mm, 4 * s + k + 1)
                nc.scalar.copy(PT[:, 8 * k:8 * k + 8].rearrange("p q m -> p (q m)"),
                               bank_b(k)[:, :].bitcast(f16)).then_inc(pt_ok[1], 1)

            if B:
                PT_copy(1)
            if A:
                act.wait_ge(zT_mm, j + 1)
                src = bank_w[:, :].bitcast(f16).rearrange("p (k n f) -> p k f n", f=A4, n=N)
                dst = znT[:, :, :].rearrange("p k c -> p (k c)").rearrange("p (k f n) -> p k f n", f=A4, n=N)
                nc.scalar.copy(dst, src).then_inc(zT_ok, 1)
            if B:
                PT_copy(3)
                u_copies(range(4))
            if LN:
                act_ln_square(act, j + 1, 1 - par)
            if B:
                u_copies(range(4, 8))
            if A:
                t_high(range(H))
            if LN:
                act_ln_high(act, j + 1, 1 - par, half + par)
            if tail:
                p_high(range(4))
            if A:
                exps((0,))
                gates((0, 1))
                exps((1, 2))
                gates((2,))
                exps((3,))
                gates((3,))

        @block.scalar
        def _(act):
            for k, w in enumerate((Wq, Wk)):
                act.dma_start(wq_in[:, k], w).then_inc(wts_in, 16)
            for g in range(A2):
                rows = slice(D * g, D * g + D)
                act.dma_start(wg_in[rows].rearrange("p h c -> p (h c)"), Wg).then_inc(wts_in, 16)
                act.dma_start(wv_in[rows].rearrange("p h c -> p (h c)"), Wv).then_inc(wts_in, 16)
                act.dma_start(bo_col[rows], bo.unsqueeze(1)).then_inc(wts_in, 16)
            act.wait_ge(zeros_w, 2)
            for r in range(2):
                for e in range(A2):
                    rows = slice(64 * r + C * e, 64 * r + C * e + C)
                    act.dma_start(Wo_bd[rows, :, e],
                                  Wo.rearrange("(k r c) d -> r c k d", k=HP, r=2)[r]).then_inc(wts_in, 16)
                    act.dma_start(bg_in[rows], bg[r]).then_inc(wts_in, 16)
            act.dma_start(w_bc[:, :], ln_w.partition_broadcast(128)).then_inc(wts_in, 16)
            act.dma_start(b_bc[:, :], ln_b.partition_broadcast(128)).then_inc(wts_in, 16)
            for e in range(A2):
                act.wait_ge(x_in[e], 16)
                if e >= 1:
                    act.wait_ge(sqred, e)
                nc.scalar.activation(sq[:, :], x_tok[:, e].rearrange("p b d -> p (b d)"), ACT.Square).then_inc(sq_ok, 1)
                nc.scalar.copy(x_perm[:, :, e], x_tok[:, e]).then_inc(xp_ok, 1)
            act.wait_ge(wts_in, WTS)
            nc.scalar.mul(bg_h[:, :], bg_in[:, :], 0.5)
            nc.scalar.mul(Wo_h[:, :, :, :].rearrange("p k e d -> p (k e d)"),
                          Wo_bd[:, :, :, :].rearrange("p k e d -> p (k e d)"), 0.5).then_inc(wprep_a, 1)
            act.wait_ge(wT_mm, 2)
            for g in range(A2):
                rows = slice(D * g, D * g + D)
                nc.scalar.mul(A_bd[rows, HI, :, g], PS[1][rows, 0:256].rearrange("p (h d) -> p h d", h=H),
                              0.25).then_inc(wprep_a, 1)
            for g in range(A2):
                rows = slice(D * g, D * g + D)
                nc.scalar.copy(Wg_bd[rows, HI, :, g], wg_in[rows]).then_inc(wprep_a, 1)
            for g in range(A2):
                rows = slice(D * g, D * g + D)
                nc.scalar.copy(Wv_bd[rows, :, g], wv_in[rows]).then_inc(wprep_a, 1)
            for i in range(NS):
                act.wait_ge(xT_mm, i + 1)
                nc.scalar.copy(xT[:, COLS * i:COLS * i + COLS].rearrange("p (b f n) -> p b f n", f=A4, n=N),
                               PS[2 + i % 2][:, :].rearrange("p (b n f) -> p b f n", f=A4, n=N)).then_inc(xT_ok, 1)
            act_ln_square(act, 0, 0)
            act_ln_high(act, 0, 0, 0)
            for j in range(3):
                act_period(act, j, j % 2, j // 2, tail=j >= 1, B=j >= 2)
            with act.Fori(0, LOOPS) as it:
                for i in range(2):
                    act_period(act, 2 * it + 3 + i, 1 - i, it + 1 + i)
            for j in range(NS - 1, NS + 2):
                act_period(act, j, j % 2, j // 2, tail=j <= NS, A=j < NS, LN=j < NS - 1)
            for f in range(A4):
                act.wait_ge(z1_b, f + 1)
                nc.scalar.copy(z1[HI][:, f].rearrange("p n b -> p (n b)"), z1f[f % 2]).then_inc(z1_h, 1)

            def gates(g):
                for f in range(A4):
                    i = A4 * g + f
                    act.wait_ge(pj_mm, i + 1)
                    if i >= 3:
                        act.wait_ge(pj_ok, 2 * (i - 2))
                    nc.scalar.activation(gt[i % 3].rearrange("p a m c -> p (a m c)"), PS[i % 3][:, 0:256],
                                         ACT.Tanh, scale=0.5).then_inc(pj_th, 1)

            def k_copies(g):
                for h in range(2):
                    i = 2 * g + h
                    act.wait_ge(k_mm, i + 1)
                    if h == 0 and g >= 2:
                        act.wait_ge(k_st, 16 * (g - 1))
                    dst = k_sb.rearrange("p (s c m) -> p s c m", s=2, c=8)[:, g % 2, 4 * h:4 * h + 4]
                    nc.scalar.activation(dst.rearrange("p c m -> p (c m)"), PS[3 + i % 4][:, :], ACT.Identity,
                                         accum_out=ksum[:, 0, i:i + 1]).then_inc(k_cp, 1)
                    nc.scalar.activation(sq[:, 512 * h:512 * h + 512], PS[3 + i % 4][:, :], ACT.Square,
                                         accum_out=ksum[:, 1, i:i + 1]).then_inc(k_sq, 1)

            gates(0)
            gates(1)
            k_copies(0)
            gates(2)
            k_copies(1)
            gates(3)
            k_copies(2)
            act.wait_ge(g2_ok, 14)
            for f in range(A4):
                act.wait_ge(go_mm, f + 1)
                nc.scalar.activation(tg[:, 512 * f:512 * f + 512], PS[f % 3][:, :], ACT.Tanh,
                                     bias=col[:, BGH:BGH + 1], scale=0.5).then_inc(go_th, 1)
            k_copies(3)
            for i in range(0, NS, 2):
                act.wait_ge(x2_mm, i + 1)
                nc.scalar.copy(out_tok[:, :, SB * i:SB * i + SB].rearrange("p e b d -> p b e d"),
                               PS[5 + i % 3][:, :].rearrange("p (b e d) -> p b e d", b=SB, e=A2)).then_inc(x2_cp[0], 1)

        def dve_ln_centre(dve, j, par):
            z = zc[:, par].rearrange("p e b d -> p (e b) d")
            dve.wait_ge(ln_z, LZ * j + 2)
            nc.vector.tensor_reduce(ln_mu[:, par], z, op=ALU.add, axis=AX.X).then_inc(ln_v, 1)
            dve.wait_ge(ln_v, LV * j + 1)
            nc.vector.scalar_tensor_tensor(out=z, in0=bcast(ln_mu[:, par], 2, D), scalar=-1.0 / D, in1=z,
                                           op0=ALU.mult, op1=ALU.add).then_inc(ln_v, 1)

        def dve_ln_rstd(dve, j, par):
            dve.wait_ge(ln_a, LA * j + 1)
            nc.vector.tensor_reduce(ln_var[:, par], sq[:, 0:512].rearrange("p (t d) -> p t d", d=D), op=ALU.add,
                                    axis=AX.X).then_inc(ln_v, 1)
            dve.wait_ge(ln_v, LV * j + 3)
            nc.vector.tensor_scalar(ln_ve[:, par], ln_var[:, par], 1.0 / D, EPS, ALU.mult, ALU.add).then_inc(ln_v, 1)

        def dve_sums(dve, m, ks):
            for k in ks:
                dve.wait_ge(s_exp, 4 * m + k + 1)
                nc.vector.tensor_reduce(sums[:, 32 * k:32 * k + 32], S_sb[:, 8 * k:8 * k + 8]
                                        .rearrange("p q a n -> p (q a) n"), op=ALU.add, axis=AX.X).then_inc(p_sum, 1)

        def dve_stats(dve, s):
            dve.wait_ge(x1_ok, s + 1)
            nc.vector.tensor_reduce(st1[:, 0, bass.ds(s, 1)].rearrange("p s n -> p (s n)"),
                                    xT[:, bass.ds(s * COLS, COLS)].rearrange("p (q n) -> p n q", n=N),
                                    op=ALU.add, axis=AX.X).then_inc(x1_st, 1)
            dve.wait_ge(x1_sq, s + 1)
            nc.vector.tensor_reduce(st1[:, 1, bass.ds(s, 1)].rearrange("p s n -> p (s n)"),
                                    sqx[:, :].rearrange("p (q n) -> p n q", n=N),
                                    op=ALU.add, axis=AX.X).then_inc(x1_st, 1)

        def dve_reciprocal(dve, m, half):
            dve.wait_ge(p_sum, 4 * m + 2 * half + 2)
            if not isinstance(m, int) or m >= 1:
                dve.wait_ge(p_nrm, 4 * m)
            nc.vector.reciprocal(rden[:, 64 * half:64 * half + 64], sums[:, 64 * half:64 * half + 64]).then_inc(p_rec, 1)

        def dve_period(dve, j, par, tail=True, B=True, A=True, LN=True, stats=True):
            s, m = j - 2, j - 1
            for i, k in enumerate((0, 2)):
                if B:
                    dve.wait_ge(pt_mm, 4 * s + k + 1)
                    nc.vector.tensor_copy(PT[:, 8 * k:8 * k + 8].rearrange("p q m -> p (q m)"),
                                          bank_b(k)[:, :].bitcast(f16)).then_inc(pt_ok[0], 1)
                if tail:
                    dve_sums(dve, m, (2 + i,))
            if tail:
                dve_reciprocal(dve, m, 1)
            if LN:
                dve_ln_centre(dve, j + 1, 1 - par)
                dve_ln_rstd(dve, j + 1, 1 - par)
            if stats:
                dve_stats(dve, s - 1)
            for h in range(H if A else 0):
                dve.wait_ge(t_hi, H * j + h + 1)
                nc.vector.tensor_tensor(t_sb[:, LO, :, h], bank_tg(h)[:, :].rearrange("p (q i) -> p q i", i=N),
                                        t_sb[:, HI, :, h], ALU.subtract).then_inc(t_lo, 1)
            for k in range(HP if B else 0):
                dve.wait_ge(o_mm, HP * s + k + 1)
                dve.wait_ge(g_th, HP * s + k + 1)
                nc.vector.scalar_tensor_tensor(out=og[:, k], in0=th[:, par, k], scalar=1.0, in1=bank_b(k)[:, :],
                                               op0=ALU.add, op1=ALU.mult).then_inc(o_ok, 1)
            for k in range(4 if A else 0):
                S = bank_s(k)[:, :].rearrange("p (r n) -> p r n", n=N)
                dve.wait_ge(s_mm, 4 * j + k + 1)
                nc.vector.tensor_reduce(nmax[:, k % 2], S, op=ALU.max, axis=AX.X).then_inc(s_max, 1)
                if tail:
                    dve.wait_ge(p_lo, 4 * m + k + 1)
                dve.wait_ge(s_max, 4 * j + k + 1)
                nc.vector.tensor_tensor(S_sb[:, 8 * k:8 * k + 8].rearrange("p q a n -> p (q a) n"), S,
                                        bcast(nmax[:, k % 2], 2, N), ALU.subtract).then_inc(s_sub, 1)
                if k in (1, 2):
                    dve_sums(dve, j, (k - 1,))
                if k == 2:
                    dve_reciprocal(dve, j, 0)
            if B:
                dve.wait_ge(w_mm, s + 1)
                v = xT[:, bass.ds(s * COLS, COLS)]
                nc.vector.scalar_tensor_tensor(out=v, in0=bank_w[:, :], scalar=bo_col[:, 0:1], in1=v,
                                               op0=ALU.add, op1=ALU.add).then_inc(x1_ok, 1)

        def dve_weights2(dve):
            dve.wait_ge(wT_mm, 4)
            for g in range(A2):
                rows = slice(D * g, D * g + D)
                for kind, scale in ((0, 1.0), (1, 0.5)):
                    nc.vector.tensor_scalar(W1_bd[rows, HI, kind, g].rearrange("p m d -> p (m d)"),
                                            PS[6][rows, 64 * kind:64 * kind + 64], scale, None,
                                            ALU.mult).then_inc(wprep, 1)
                nc.vector.tensor_copy(Wgo_bd[rows, HI, g], PS[6][rows, 128:160]).then_inc(wprep, 1)
                nc.vector.tensor_copy(Wlo_bd[rows, g], PS[6][rows, 160:192]).then_inc(wprep, 1)
            dve.wait_ge(wprep, 11 + 16)
            for g in range(A2):
                rows = slice(D * g, D * g + D)
                for kind, scale in ((0, 1.0), (1, 0.5)):
                    nc.vector.scalar_tensor_tensor(out=W1_bd[rows, LO, kind, g].rearrange("p m d -> p (m d)"),
                                                   in0=PS[6][rows, 64 * kind:64 * kind + 64], scalar=scale,
                                                   in1=W1_bd[rows, HI, kind, g].rearrange("p m d -> p (m d)"),
                                                   op0=ALU.mult, op1=ALU.subtract).then_inc(wprep, 1)
                nc.vector.tensor_tensor(Wgo_bd[rows, LO, g], PS[6][rows, 128:160], Wgo_bd[rows, HI, g],
                                        ALU.subtract).then_inc(wprep, 1)
            dve.wait_ge(wts2_in, WTS2)
            nc.vector.tensor_scalar(b1_in[:, 1], b1_in[:, 1], 0.5, None, ALU.mult).then_inc(wprep, 1)
            n = 11 + 16 + 12 + 1
            rest = b1_in
            for r in range(3):
                dve.wait_ge(wprep, n)
                nc.vector.tensor_copy(b1_s[:, r], rest if r else b1_in[:, :, :, :]).then_inc(wprep, 1)
                n += 1
                dve.wait_ge(wprep, n)
                if r < 2:
                    nc.vector.tensor_tensor(b1_r[:, r], rest if r else b1_in[:, :, :, :], b1_s[:, r],
                                            ALU.subtract).then_inc(wprep, 1)
                    n += 1
                    rest = b1_r[:, r]
            for r in range(3):
                row = slice(32 * r, 32 * r + 1)
                nc.vector.tensor_copy(B1[row, :, :, :, :].rearrange("p k e m d -> p k e (m d)"),
                                      bcast(b1_s[row, r].rearrange("p k m d -> p k (m d)"), 2, A2)).then_inc(wprep, 1)
            n += 3
            return n

        WPREP = 11 + 16 + 12 + 1 + 5 + 3

        @block.vector
        def _(dve):
            def zero(v):
                return nc.vector.memset(v, 0.0)
            zero(A_bd[:, :, :, :, :].rearrange("p k h e d -> p (k h e d)").bitcast(f32))
            zero(Wg_bd[:, :, :, :, :].rearrange("p k h e c -> p (k h e c)").bitcast(f32))
            zero(Wv_bd[:, :, :, :].rearrange("p h e c -> p (h e c)")).then_inc(zeros_w, 1)
            zero(Wo_bd[:, :, :, :].rearrange("p k e d -> p (k e d)")).then_inc(zeros_w, 1)
            zero(b1_in[:, :, :, :].rearrange("p k m d -> p (k m d)")).then_inc(zeros_w, 1)
            zero(B1[:, :, :, :, :].rearrange("p k e m d -> p (k e m d)").bitcast(f32))
            zero(W1_bd[:, :, :, :, :, :].rearrange("p l k e m d -> p (l k e m d)").bitcast(f32))
            zero(Wgo_bd[:, :, :, :].rearrange("p l e d -> p (l e d)").bitcast(f32))
            zero(Wlo_bd[:, :, :].rearrange("p e d -> p (e d)"))
            nc.vector.memset(ones_bf[:, :], 1.0)
            nc.vector.memset(ones_col[:, :], 1.0)
            nc.vector.memset(allsum[:, 0], 1.0 / (A2 * N * D))
            nc.vector.memset(allsum[:, 1], 1.0 / (N * L * L * D)).then_inc(zeros_w, 1)
            for e in range(A2):
                dve.wait_ge(x_in[e], 16)
                nc.vector.tensor_reduce(gn_part[:, 0, :, e], x_tok[:, e].rearrange("p b d -> p d b"), op=ALU.add,
                                        axis=AX.X).then_inc(gn_ok, 1)
                dve.wait_ge(sq_ok, e + 1)
                nc.vector.tensor_reduce(gn_part[:, 1, :, e], sq[:, :].rearrange("p (b d) -> p d b", d=D), op=ALU.add,
                                        axis=AX.X).then_inc(sqred, 1)
            dve.wait_ge(gn_ok, 4)
            dve.wait_ge(sqred, 4)
            nc.vector.tensor_reduce(gn_sum[:, :, :], gn_part[:, :, :, :], op=ALU.add, axis=AX.X).then_inc(gn_ok, 1)
            dve.wait_ge(gn_mm, 1)
            nc.vector.tensor_copy(gn_mv[:, :, :].rearrange("p k d -> p (k d)"), PS[0][:, 0:2 * D]).then_inc(gn_ok, 1)
            dve.wait_ge(gn_ok, 6)
            nc.vector.tensor_tensor(gn_tmp[:, 0], gn_mv[:, 0], gn_mv[:, 0], ALU.mult).then_inc(gn_ok, 1)
            dve.wait_ge(gn_ok, 7)
            nc.vector.scalar_tensor_tensor(out=gn_tmp[:, 1], in0=gn_mv[:, 1], scalar=EPS, in1=gn_tmp[:, 0],
                                           op0=ALU.add, op1=ALU.subtract).then_inc(gn_ok, 1)
            dve.wait_ge(rsq, 1)
            nc.vector.scalar_tensor_tensor(out=gn_sh[:, :], in0=gn_mv[:, 0], scalar=-1.0, in1=gn_r[:, :],
                                           op0=ALU.mult, op1=ALU.mult).then_inc(gn_ok, 1)
            dve.wait_ge(wT_mm, 1)
            nc.vector.tensor_copy(wqT[:, :, :], bcast(PS[4][:, 0:D], 1, A2)).then_inc(wprep, 1)
            nc.vector.tensor_copy(wkT[:, :], PS[4][:, D:2 * D]).then_inc(wprep, 1)
            dve.wait_ge(wprep, 1)
            dve.wait_ge(zeros_z, NZ_MASKS)
            nc.vector.tensor_tensor(wqTm, bcast(wqT[:, :, :].rearrange("p e d -> p (e d)"), 1, H),
                                    bcast(headmask[:, :], 2, 128), ALU.mult).then_inc(wprep, 1)
            dve.wait_ge(wprep_a, 5)
            for g in range(A2):
                rows = slice(D * g, D * g + D)
                nc.vector.scalar_tensor_tensor(out=A_bd[rows, LO, :, g], in0=PS[1][rows, 0:256]
                                               .rearrange("p (h d) -> p h d", h=H), scalar=0.25,
                                               in1=A_bd[rows, HI, :, g], op0=ALU.mult,
                                               op1=ALU.subtract).then_inc(wprep, 1)
            dve.wait_ge(wprep_a, 9)
            for g in range(A2):
                rows = slice(D * g, D * g + D)
                nc.vector.tensor_tensor(Wg_bd[rows, LO, :, g], wg_in[rows], Wg_bd[rows, HI, :, g],
                                        ALU.subtract).then_inc(wprep, 1)
            dve_ln_centre(dve, 0, 0)
            dve_ln_rstd(dve, 0, 0)
            for j in range(3):
                dve_period(dve, j, j % 2, tail=j >= 1, B=j >= 2, stats=False)
                if j == 0:
                    assert dve_weights2(dve) == WPREP
            with dve.Fori(0, LOOPS) as it:
                for i in range(2):
                    dve_period(dve, 2 * it + 3 + i, 1 - i)
            for j in range(NS - 1, NS + 2):
                dve_period(dve, j, j % 2, tail=j <= NS, A=j < NS, LN=j < NS - 1)
            dve_stats(dve, NS - 1)

            def step(n, ins):
                ins.then_inc(g2_ok, 1)
                dve.wait_ge(g2_ok, n)
            dve.wait_ge(x1_st, 2 * NS)
            step(1, nc.vector.tensor_reduce(g2[:, 0:2], st1[:, :, :, :].rearrange("p k s n -> p k n s"),
                                            op=ALU.add, axis=AX.X))
            dve.wait_ge(g2_mm, 1)
            step(2, nc.vector.tensor_copy(g2[:, 2:4].rearrange("p k n -> p (k n)"), PS[0][:, 0:2 * N]))
            step(3, nc.vector.tensor_tensor(g2[:, 4], g2[:, 2], g2[:, 2], ALU.mult))
            step(4, nc.vector.tensor_tensor(g2[:, 8], g2[:, 3], g2[:, 4], ALU.subtract))
            step(5, nc.vector.tensor_scalar(g2[:, 5], g2[:, 8], EPS, None, ALU.add))
            dve.wait_ge(rsq, 2)
            step(6, nc.vector.tensor_tensor(g2[:, 7], g2[:, 8], g2[:, 6], ALU.mult))
            step(7, nc.vector.tensor_tensor(g2[:, 9], g2[:, 7], g2[:, 6], ALU.mult))
            step(8, nc.vector.tensor_reduce(col[:, V:V + 1], g2[:, 9], op=ALU.add, axis=AX.X))
            dve.wait_ge(g2_mm, 2)
            step(9, nc.vector.tensor_scalar(col[:, RV:RV + 1], PS[1][:, 0:1], EPS, None, ALU.add))
            dve.wait_ge(rsq, 3)
            step(10, nc.vector.tensor_tensor(col[:, SC:SC + 1], col[:, T0:T0 + 1], col[:, Ain:Ain + 1], ALU.mult))
            step(11, nc.vector.tensor_scalar(g2[:, 10], g2[:, 6], col[:, SC:SC + 1], None, ALU.mult))
            step(12, nc.vector.scalar_tensor_tensor(out=g2[:, 4], in0=g2[:, 2], scalar=-1.0, in1=g2[:, 10],
                                                    op0=ALU.mult, op1=ALU.mult))
            step(13, nc.vector.tensor_scalar(g2[:, 11], g2[:, 4], col[:, Bin:Bin + 1], None, ALU.add))
            step(14, nc.vector.tensor_scalar(col[:, BGH:BGH + 1], col[:, Bgo:Bgo + 1], 0.5, None, ALU.mult))
            dve.wait_ge(g2_mm, 3)
            step(15, nc.vector.tensor_copy(col[:, RW:RW + 1], PS[2][:, 0:1]))

            def z1_low(f):
                dve.wait_ge(z1_h, f + 1)
                nc.vector.tensor_tensor(z1[LO][:, f].rearrange("p n b -> p (n b)"), z1f[f % 2],
                                        z1[HI][:, f].rearrange("p n b -> p (n b)"), ALU.subtract).then_inc(z1_l, 1)
            for f in range(A4):
                if f >= 2:
                    dve.wait_ge(z1_l, f - 1)
                nc.vector.tensor_tensor(z1f[f % 2].rearrange("p (n b) -> p n b", n=N),
                                        xT[:, :].rearrange("p (b f n) -> p f n b", f=A4, n=N)[:, f],
                                        bcast(g2[:, 10], 2, L), ALU.mult).then_inc(z1_m, 1)
                if f:
                    z1_low(f - 1)
            z1_low(A4 - 1)

            for i in range(4 * A4):
                g, f = divmod(i, A4)
                if f == 0 and g >= 2:
                    dve.wait_ge(k_mm, 2 * (g - 1))
                    dve.wait_ge(bbd_ld[g % 2], 64 * (g // 2))
                dve.wait_ge(pj_th, i + 1)
                lin = PS[i % 3][:, 256:512].rearrange("p (a m c) -> p a m c", a=A2, m=2)
                for m, dst in ((0, a_buf), (1, b_buf)):
                    nc.vector.scalar_tensor_tensor(out=dst[g % 2][:, A2 * f:A2 * f + A2], in0=gt[i % 3][:, :, m],
                                                   scalar=1.0, in1=lin[:, :, m], op0=ALU.add,
                                                   op1=ALU.mult).then_inc(pj_ok, 1)

            def kstep(n, ins):
                ins.then_inc(k_ok, 1)
                dve.wait_ge(k_ok, n)
            dve.wait_ge(k_cp, 8)
            dve.wait_ge(k_sq, 8)
            kstep(1, nc.vector.tensor_reduce(ksum2[:, :], ksum[:, :, :], op=ALU.add, axis=AX.X))
            dve.wait_ge(ks_mm, 1)
            kstep(2, nc.vector.tensor_copy(g2[:, 0, 0:2], PS[0][:, 0:2]))
            kstep(3, nc.vector.tensor_tensor(col[:, T0:T0 + 1], g2[:, 0, 0:1], g2[:, 0, 0:1], ALU.mult))
            kstep(4, nc.vector.tensor_tensor(col[:, V:V + 1], g2[:, 0, 1:2], col[:, T0:T0 + 1], ALU.subtract))
            kstep(5, nc.vector.tensor_scalar(col[:, RV:RV + 1], col[:, V:V + 1], EPS, None, ALU.add))
            dve.wait_ge(rsq, 4)
            kstep(6, nc.vector.tensor_tensor(col[:, SC:SC + 1], col[:, KR:KR + 1], col[:, Aout:Aout + 1], ALU.mult))
            kstep(7, nc.vector.scalar_tensor_tensor(out=col[:, T0:T0 + 1], in0=g2[:, 0, 0:1], scalar=-1.0,
                                                    in1=col[:, SC:SC + 1], op0=ALU.mult, op1=ALU.mult))
            kstep(8, nc.vector.tensor_tensor(col[:, KT:KT + 1], col[:, T0:T0 + 1], col[:, Bout:Bout + 1], ALU.add))
            kstep(9, nc.vector.tensor_tensor(col[:, V:V + 1], col[:, KT:KT + 1], col[:, RW:RW + 1], ALU.mult))
            kstep(10, nc.vector.tensor_tensor(col[:, T0:T0 + 1], col[:, V:V + 1], col[:, Blo:Blo + 1], ALU.add))
            kstep(11, nc.vector.tensor_scalar(col[:, CV:CV + 1], col[:, T0:T0 + 1], 0.5, None, ALU.mult))
            kstep(12, nc.vector.tensor_scalar(col[:, KS:KS + 1], col[:, SC:SC + 1], 0.5, None, ALU.mult))
            for f in range(A4):
                v = x2[:, 512 * f:512 * f + 512]
                dve.wait_ge(lo_mm, f + 1)
                nc.vector.tensor_scalar(v, PS[3 + f % 2][:, :], col[:, KS:KS + 1], col[:, CV:CV + 1], ALU.mult,
                                        ALU.add).then_inc(lo_s, 1)
                dve.wait_ge(lo_s, f + 1)
                dve.wait_ge(go_th, f + 1)
                nc.vector.scalar_tensor_tensor(out=v, in0=tg[:, 512 * f:512 * f + 512], scalar=1.0, in1=v,
                                               op0=ALU.add, op1=ALU.mult).then_inc(lo_g, 1)
            for i in range(1, NS, 2):
                dve.wait_ge(x2_mm, i + 1)
                nc.vector.tensor_copy(out_tok[:, :, SB * i:SB * i + SB].rearrange("p e b d -> p b e d"),
                                      PS[5 + i % 3][:, :].rearrange("p (b e d) -> p b e d", b=SB, e=A2)
                                      ).then_inc(x2_cp[1], 1)

        def mm(o, l, r, start=True, stop=True):
            return nc.tensor.matmul(o, l, r, start=start, stop=stop)

        def split_mm(o, wt, mv):
            mm(o, wt[HI], mv[HI], True, False)
            mm(o, wt[LO], mv[HI], False, False)
            return mm(o, wt[HI], mv[LO], False, True)

        def pe_znT(pe, j, par):
            pe.wait_ge(ln_z, LZ * (j + 1))
            if not isinstance(j, int) or j >= 3:
                pe.wait_ge(x1_ok, j - 2)
            zt = bank_w[:, :].bitcast(f16)
            tok = zn_tok[:, par].rearrange("p e d b k -> p (e d) b k")
            for k in (HI, LO):
                for b in range(SB):
                    at = 128 * (SB * k + b)
                    last = nc.tensor.transpose(zt[:, at:at + 128], tok[:, :, b, k], ident16[:, :])
            last.then_inc(zT_mm, 1)

        def pe_t(pe, j):
            pe.wait_ge(zT_ok, j + 1)
            for h in range(H):
                if h >= 3:
                    pe.wait_ge(t_lo, H * j + h - 2)
                elif not isinstance(j, int) or j >= 1:
                    pe.wait_ge(g_th, HP * (j - 1) + h + 2)
                split_mm(bank_tg(h)[:, :], [A_bd[:, k, h].rearrange("p e d -> p (e d)") for k in (HI, LO)],
                         [znT[:, k] for k in (HI, LO)]).then_inc(t_mm, 1)

        def pe_gate(pe, j, ks):
            for k in ks:
                if k < 3:
                    pe.wait_ge(t_lo, H * j + H - 2 + k)
                else:
                    pe.wait_ge(g_th, HP * j + 1)
                split_mm(bank_tg(H + k)[:, :],
                         [Wg_bd[:, p, 2 * k:2 * k + 2].rearrange("p h e c -> p (h e c)") for p in (HI, LO)],
                         [znT[:, p] for p in (HI, LO)]).then_inc(g_mm, 1)

        def pe_scores(pe, j, ks):
            if ks[0] == 0:
                pe.wait_ge(t_lo, H * (j + 1))
                pe.wait_ge(zbd_ld, 64 * (j + 1))
            for k in ks:
                if k >= 2:
                    pe.wait_ge(s_sub, 4 * j + k - 1)
                elif not isinstance(j, int) or j >= 1:
                    pe.wait_ge(s_sub, 4 * (j - 1) + k + 3)
                for q in range(8 * k, 8 * k + 8):
                    last = split_mm(bank_s(k)[:, 64 * (q % 8):64 * (q % 8) + 64],
                                    [t_sb[:, p, q].rearrange("p h i -> p (h i)") for p in (HI, LO)],
                                    [zbd[:, :, p, N * q:N * q + N] for p in (HI, LO)])
                last.then_inc(s_mm, 1)

        def pe_PT(pe, s, ks):
            for k in ks:
                pe.wait_ge(p_lo, 4 * s + k + 1)
                if k >= 2:
                    pe.wait_ge(pt_ok[k % 2], 2 * s + 1)
                for q in range(8 * k, 8 * k + 8):
                    last = nc.tensor.transpose(bank_b(k)[:, :].bitcast(f16)[:, 128 * (q % 8):128 * (q % 8) + 128],
                                               P2[:, q].rearrange("p k m -> p (k m)"), ident16[:, :])
                last.then_inc(pt_mm, 1)

        def pe_u(pe, s, par, half):
            pe.wait_ge(Z_ld[par], 128 * (half + 1))
            for k in range(8):
                if k < 2:
                    pe.wait_ge(pt_ok[k], 2 * (s + 1))
                elif k >= 4:
                    pe.wait_ge(u_ok, 8 * s + k - 3)
                for q in range(4 * k, 4 * k + 4):
                    b, f = divmod(q, A4)
                    o = bank_u(k)[:, 128 * (q % 4):128 * (q % 4) + 128]
                    Zq = Z[:, par, f].rearrange("p e d b k -> p (e d) b k")[:, :, b]
                    mm(o, Zq[:, :, HI], PT[:, q], True, False)
                    last = mm(o, Zq[:, :, LO], PT[:, q], False, True)
                last.then_inc(u_mm, 1)

        def pe_o(pe, s):
            pe.wait_ge(u_ok, 8 * (s + 1))
            for k in range(HP):
                if k >= 2:
                    pe.wait_ge(o_ok, HP * s + k - 1)
                for r in range(2):
                    last = mm(bank_b(k)[64 * r:64 * r + 64], Wv_bd[:, 2 * k + r].rearrange("p e c -> p (e c)"),
                              u_sb[:, 2 * k + r].rearrange("p q i -> p (q i)"))
                last.then_inc(o_mm, 1)

        def pe_out(pe, s, ks):
            for k in ks:
                pe.wait_ge(o_ok, HP * s + k + 1)
                last = mm(bank_w[:, :], Wo_h[:, k].rearrange("p e d -> p (e d)"), og[:, k], k == 0, k == HP - 1)
            if ks[-1] == HP - 1:
                last.then_inc(w_mm, 1)

        def pe_period(pe, j, par, half, B=True, A=True):
            s = j - 2
            if B:
                pe_PT(pe, s, (0, 1))
            if A:
                pe_znT(pe, j, par)
            if B:
                pe_PT(pe, s, (2, 3))
                pe_u(pe, s, par, half)
            if A:
                pe_t(pe, j)
            if B:
                pe_o(pe, s)
            for scores, gate, proj in (((0, 1), (0, 1), (0,)), ((2,), (), (1, 2)), ((3,), (2, 3), (3,))):
                if A:
                    pe_scores(pe, j, scores)
                if A and gate == (0, 1):
                    pe_gate(pe, j, gate)
                if B:
                    pe_out(pe, s, proj)
                if A and gate == (2, 3):
                    pe_gate(pe, j, gate)

        @block.tensor
        def _(pe):
            pe.wait_ge(wts_in, WTS)
            pe.wait_ge(zeros_z, NZ_MASKS)
            for k in range(2):
                last = nc.tensor.transpose(PS[4][:, D * k:D * k + D], wq_in[:, k], ident[0:D, 0:D])
            last.then_inc(wT_mm, 1)
            pe.wait_ge(xp_ok, A2)
            for i in range(NS):
                if i >= 2:
                    pe.wait_ge(xT_ok, i - 1)
                for b in range(SB):
                    last = nc.tensor.transpose(PS[2 + i % 2][:, 128 * b:128 * b + 128], x_perm[:, SB * i + b].rearrange("p e d -> p (e d)"), ident[:, :])
                last.then_inc(xT_mm, 1)
                if i == 1:
                    pe.wait_ge(gn_ok, 5)
                    mm(PS[0][:, 0:2 * D], seqsum[:, :], gn_sum[:, :, :].rearrange("p k d -> p (k d)")
                       ).then_inc(gn_mm, 1)
                    pe.wait_ge(wprep, 3)
                    for h in range(H):
                        last = mm(PS[1][:, D * h:D * h + D], wqTm[:, h], wkT[:, :])
                    last.then_inc(wT_mm, 1)
                    pe.wait_ge(wts2_in, WTS2)
                    nc.tensor.transpose(PS[6][:, 0:128], w1_in[:, :, :].rearrange("p g d -> p (g d)"),
                                        ident[:, :]).then_inc(wT_mm, 1)
                    nc.tensor.transpose(PS[6][:, 128:192], w2_in[:, :, :].rearrange("p g d -> p (g d)"),
                                        ident[0:64, 0:64]).then_inc(wT_mm, 1)
            pe.wait_ge(xT_ok, NS)
            pe.wait_ge(wprep, 11)
            pe.wait_ge(wprep_a, 13)
            for j in range(3):
                if j == 2:
                    pe.wait_ge(wprep, WPREP)
                pe_period(pe, j, j % 2, 0, B=j == 2)
            with pe.Fori(0, LOOPS) as it:
                for i in range(2):
                    pe_period(pe, 2 * it + 3 + i, 1 - i, it + i)
            for j in range(NS - 1, NS + 2):
                pe_period(pe, j, j % 2, j // 2 - 1, A=j < NS)

            pe.wait_ge(g2_ok, 1)
            mm(PS[0][:, 0:2 * N], chsum[:, :], g2[:, 0:2].rearrange("p k n -> p (k n)")).then_inc(g2_mm, 1)
            pe.wait_ge(g2_ok, 8)
            mm(PS[1][:, 0:1], allsum[:, 0], col[:, V:V + 1]).then_inc(g2_mm, 1)
            mm(PS[2][:, 0:1], Wlo_bd[:, :, :].rearrange("p e d -> p (e d)"), ones_col[:, :]).then_inc(g2_mm, 1)
            pe.wait_ge(g2_ok, 15)

            def project(g):
                for f in range(A4):
                    i = A4 * g + f
                    if g == 0:
                        pe.wait_ge(z1_l, f + 1)
                    if i >= 3:
                        pe.wait_ge(pj_ok, 2 * (i - 2))
                    o = PS[i % 3][:, :]
                    zz = [z1[p][:, f, 4 * g:4 * g + 4].rearrange("p n b -> p (n b)") for p in (HI, LO)]
                    W = [W1_bd[:, p].rearrange("p k e m d -> p (k e m d)") for p in (HI, LO)]
                    mm(o, ones_bf[:, :], B1[:, :, :, :, :].rearrange("p k e m d -> p (k e m d)"), True, False)
                    mm(o, zz[HI], W[HI], False, False)
                    mm(o, zz[LO], W[HI], False, False)
                    mm(o, zz[HI], W[LO], False, True).then_inc(pj_mm, 1)

            def triangle(g):
                pe.wait_ge(bbd_ld[g % 2], 64 * (g // 2 + 1))
                for h in range(2):
                    i = 2 * g + h
                    if i >= 4:
                        pe.wait_ge(k_sq, i - 3)
                    for c in range(16 * h, 16 * h + 16):
                        c8, c4 = divmod(c, 4)
                        last = mm(PS[3 + i % 4][L * c4:L * c4 + L, 128 * (c8 % 4):128 * (c8 % 4) + 128],
                                  a_buf[g % 2][:, :, c], bbd[g % 2][:, :, :, c])
                    last.then_inc(k_mm, 1)

            project(0)
            project(1)
            triangle(0)
            project(2)
            triangle(1)
            project(3)
            triangle(2)
            for f in range(A4):
                if f < 3:
                    pe.wait_ge(pj_ok, 64)
                else:
                    pe.wait_ge(go_th, f - 2)
                split_mm(PS[f % 3][:, :], [Wgo_bd[:, p].rearrange("p e d -> p (e d)") for p in (HI, LO)],
                         [z1[p][:, f].rearrange("p n b -> p (n b)") for p in (HI, LO)]).then_inc(go_mm, 1)
            triangle(3)
            pe.wait_ge(go_th, A4)
            pe.wait_ge(k_ok, 1)
            mm(PS[0][:, 0:2], allsum[:, 1], ksum2[:, :]).then_inc(ks_mm, 1)
            for g in range(4):
                pe.wait_ge(kT_ld[g], 64)
            for f in range(A4):
                if f >= 2:
                    pe.wait_ge(lo_s, f - 1)
                mm(PS[3 + f % 2][:, :], Wlo_bd[:, :, :].rearrange("p e d -> p (e d)"),
                   kT[:, 512 * f:512 * f + 512]).then_inc(lo_mm, 1)
            pe.wait_ge(x2_ok, A4)
            for i in range(NS):
                if i >= 3:
                    pe.wait_ge(x2_cp[(i - 3) % 2], (i - 3) // 2 + 1)
                for b in range(SB):
                    last = nc.tensor.transpose(PS[5 + i % 3][:, 128 * b:128 * b + 128],
                                               x2.rearrange("p (m b) -> p m b", b=L)[:, :, SB * i + b],
                                               ident[:, :])
                last.then_inc(x2_mm, 1)


_INS = ["x", "L0_conv_ln_w", "L0_conv_ln_b", "L0_conv_Wq", "L0_conv_Wk", "L0_conv_Wv", "L0_conv_Wg", "L0_conv_bg",
        "L0_conv_Wo", "L0_conv_bo", "L1_conv_alpha_in", "L1_conv_beta_in", "L1_conv_W_la", "L1_conv_b_la",
        "L1_conv_W_ga", "L1_conv_b_ga", "L1_conv_W_lb", "L1_conv_b_lb", "L1_conv_W_gb", "L1_conv_b_gb",
        "L1_conv_alpha_o", "L1_conv_beta_o", "L1_conv_W_go", "L1_conv_b_go", "L1_conv_W_lo", "L1_conv_b_lo"]


def kernel(**inputs):
    import numpy as _np
    import concourse.bacc as _bacc
    from concourse.bass_utils import run_bass_kernel_spmd as _run

    nc = _bacc.Bacc("TRN2", target_bir_lowering=False, num_devices=1)
    arrays, args = {}, []
    for name in _INS:
        a = _np.ascontiguousarray(inputs[name])
        if name == "L0_conv_bg":
            a = _np.ascontiguousarray(a.reshape(HP, 2, C).transpose(1, 2, 0))
        arrays[f"in_{name}"] = a
        args.append(nc.dram_tensor(f"in_{name}", a.shape, mybir.dt.from_np(a.dtype), kind="ExternalInput").ap())
    out = nc.dram_tensor("out_x", (N, L, L, D), f32, kind="ExternalOutput").ap()
    build(nc, *args, out)
    r = _run(nc, [arrays], core_ids=[0])
    return r.results[0]["out_x"]
```

```python
import concourse.bass as bass
from concourse import mybir
from contextlib import ExitStack

f32 = mybir.dt.float32
f16 = mybir.dt.float16
bf16 = mybir.dt.bfloat16
ACT = mybir.ActivationFunctionType
ALU = mybir.AluOpType
AX = mybir.AxisListType

N, L, D, H, C = 16, 32, 32, 8, 16
A2, A4 = 4, 8
SB = 4
NS = L // SB
QS = SB * A4
COLS = QS * N
HP = H // 2
EPS = 1e-5
HI, LO = 0, 1


def build(nc, x, ln_w, ln_b, Wq, Wk, Wv, Wg, bg, Wo, bo, al_in, be_in, W_la, b_la, W_ga, b_ga,
          W_lb, b_lb, W_gb, b_gb, al_o, be_o, W_go, b_go, W_lo, b_lo, out):
    ctx = ExitStack()
    with ctx:
        def sb(name, shape, dt=f32):
            return ctx.enter_context(nc.sbuf_tensor(name, shape, dt))

        sem_names = {}

        def sem(name):
            s = ctx.enter_context(nc.semaphore(name))
            sem_names[name] = s
            return s

        x_tok = sb("x_tok", [128, A2, L, D])
        xT = sb("xT", [128, NS * COLS])
        zc = sb("zc", [128, 2, A2, SB, D])
        sq = sb("sq", [128, 1024])
        sqx = sb("sqx", [128, COLS])
        zn_tok = sb("zn_tok", [128, 2, A2, D, SB, 2], f16)
        znT = sb("znT", [128, 2, COLS], f16)
        zbd = sb("zbd", [128, A2, 2, COLS], f16)
        Z = sb("Z", [128, 2, A4, A2, D, SB, 2], f16)
        t_sb = sb("t_sb", [128, 2, QS, H, N], f16)
        S_sb = sb("S_sb", [128, QS, A2, N])
        PP = sb("PP", [128, 2, QS, 128], f16)
        P2 = PP[:, 0].rearrange("p q (k m) -> p q k m", k=2)
        PT = PP[:, 1]
        u_sb = sb("u_sb", [128, H, QS, N])
        th = sb("th", [128, 2, HP, COLS])
        og = sb("og", [128, HP, COLS])
        sums = sb("sums", [128, QS * A2])
        rden = sb("rden", [128, QS * A2])
        nmax = sb("nmax", [128, 2, 32])

        ident = sb("ident", [128, 128])
        ident16 = sb("ident16", [128, 128], f16)
        seqsum = sb("seqsum", [128, 128])
        chsum = sb("chsum", [128, 128])
        allsum = sb("allsum", [128, 2, 128])
        headmask = sb("headmask", [128, H])
        wq_in = sb("wq_in", [D, 2, H * C])
        wqT = sb("wqT", [128, A2, D])
        wkT = sb("wkT", [128, D])
        wqTm = S_sb[:, 0:16].rearrange("p q a n -> p (q a n)").rearrange("p (h m) -> p h m", h=H)
        A_bd = sb("A_bd", [128, 2, H, A2, D], f16)
        wg_in = sb("wg_in", [128, H, C])
        Wg_bd = sb("Wg_bd", [128, 2, H, A2, C], f16)
        wv_in = sb("wv_in", [128, H, C])
        Wv_bd = sb("Wv_bd", [128, H, A2, C])
        wo_in = sb("wo_in", [128, HP, D])
        a2mask = sb("a2mask", [128, A2])
        Wo_h = sb("Wo_h", [128, HP, A2, D])
        bg_in = sb("bg_in", [128, HP])
        bg_h = sb("bg_h", [128, HP])
        w_bc = sb("w_bc", [128, D])
        b_bc = sb("b_bc", [128, D])
        bo_col = sb("bo_col", [128, 1])
        gn_part = sb("gn_part", [128, 2, D, A2])
        gn_sum = sb("gn_sum", [128, 2, D])
        gn_mv = sb("gn_mv", [128, 2, D])
        gn_tmp = sb("gn_tmp", [128, 3, D])
        gn_r = sb("gn_r", [128, D])
        gn_sh = sb("gn_sh", [128, D])
        scrap = sb("scrap", [128, 1])
        minus_half = sb("minus_half", [128, D])
        ln_inv = sb("ln_inv", [128, A2 * SB])
        ln_mu = sb("ln_mu", [128, 2, A2 * SB])
        ln_var = sb("ln_var", [128, 2, A2 * SB])
        ln_ve = sb("ln_ve", [128, 2, A2 * SB])
        ln_rs = sb("ln_rs", [128, 2, A2 * SB])
        st1 = sb("st1", [128, 2, NS, N])
        w1_in = sb("w1_in", [128, A2, D])
        w2_in = sb("w2_in", [64, A2, D])
        w12_f = sb("w12_f", [128, 192])
        W1_bd = sb("W1_bd", [128, 2, 2, A2, 2, D], f16)
        Wgo_bd = sb("Wgo_bd", [128, 2, A2, D], f16)
        Wlo_bd = sb("Wlo_bd", [128, A2, D])
        b1_in = sb("b1_in", [128, 2, 2, D])
        b1_r = sb("b1_r", [128, 2, 2, 2, D])
        b1_s = sb("b1_s", [128, 3, 2, 2, D], bf16)
        B1 = sb("B1", [128, 2, A2, 2, D], bf16)
        ones_bf = sb("ones_bf", [128, 128], bf16)
        ones_col = sb("ones_col", [128, 1])
        col = sb("col", [128, 17])
        g2 = sb("g2", [128, 12, N])
        ksum = sb("ksum", [128, 2, 8])
        ksum2 = sb("ksum2", [128, 2])
        (Bgo, Blo, Ain, Bin, Aout, Bout, V, RV, KR, KS, KT, CV, T0, BGH, RW, BOH, BLH) = range(17)

        gn_sq = th[:, :, :, :].rearrange("p k h c -> p (k h c)").rearrange("p (e m) -> p e m", e=A2)
        gn_x = [S_sb[:, 16 * k:16 * k + 16].rearrange("p q a n -> p (q a n)") for k in (0, 1)]
        z1 = [t_sb[:, k].rearrange("p q h i -> p (q h i)").rearrange("p (a n b) -> p a n b", a=A4, n=N)
              for k in (HI, LO)]
        z1f = [v.rearrange("p (f n b) -> p f n b", f=A4, n=4)
               for v in (zc[:, :, :, :, :].rearrange("p k a b d -> p (k a b d)"), sq[:, :])]
        a_buf = [u_sb[:, 2 * k:2 * k + 2].rearrange("p h q i -> p (h q i)")
                 .rearrange("p (i c) -> p i c", c=D) for k in (0, 1)]
        b_buf = [u_sb[:, 4 + 2 * k:6 + 2 * k].rearrange("p h q i -> p (h q i)")
                 .rearrange("p (i c) -> p i c", c=D) for k in (0, 1)]
        x_perm = u_sb[:, :, :, :].rearrange("p h q i -> p (h q i)").rearrange("p (b e d) -> p b e d", b=L, e=A2)
        bbd = [PP[:, :, :, :].rearrange("p k q m -> p (k q m)").bitcast(f32)
               .rearrange("p (n j c) -> p n j c", n=4, j=L), x_tok[:, :, :, :]]
        gt = [S_sb[:, 4 * k:4 * k + 4].rearrange("p q a n -> p (q a n)")
              .rearrange("p (a m c) -> p a m c", a=A2, m=2) for k in range(3)]
        x1_nfb = xT[:, :].rearrange("p (b f n) -> p b n f", f=A4, n=N)
        k_sb = og[:, :, :].rearrange("p h c -> p (h c)")
        kT = th[:, :, :, :].rearrange("p k h c -> p (k h c)")
        tg = Z[:, :, :, :, :, :, :].rearrange("p r f e d b k -> p (r f e d b k)").bitcast(f32)
        x2 = tg[:, 4096:8192]
        tg = tg[:, 0:4096]
        half_n = lambda v, u: v[:, L // 2 * (u % 2):L // 2 * (u % 2) + L // 2, 4 * (u // 2):4 * (u // 2) + 4]
        unit = lambda v, u: half_n(v.rearrange("p (b n f) -> p b n f", n=N, f=A4), u).rearrange("p b n f -> p b (n f)")
        kT_bnf = kT.rearrange("p (f n b) -> p b n f", f=A4, n=N)
        bank_lo = lambda u: PS[(7, 0, 3, 4, 5, 6, 7, 0)[UNITS.index(u)]]
        out_tok = u_sb[:, :, :, :].rearrange("p h q i -> p (h q i)").rearrange("p (a b d) -> p a b d", a=A2, b=L)

        zn_dram = nc.dram_tensor("zn_dram", [N, A4, NS, A2, D * SB * 2], f16, kind="Internal").ap()
        k_dram = nc.dram_tensor("k_dram", [D, A4, A2, N * L], f32, kind="Internal").ap()

        PS = [ctx.enter_context(nc.psum_tensor(f"PS{i}", [128, 512], f32)) for i in range(8)]
        bank_tg = lambda i: PS[i % 3]
        bank_s = lambda i: PS[3 + i % 2]
        bank_b = lambda i: PS[5 + i % 2]
        bank_u = lambda i: PS[(5, 3, 4, 6)[i % 4]]
        bank_w = PS[7]

        x_in = [sem(f"x_in{i}") for i in range(A2)]
        wts_in = sem("wts_in")
        wts2_in = sem("wts2_in")
        zeros_w = sem("zeros_w")
        zeros_z = sem("zeros_z")
        sq_ok = sem("sq_ok")
        sqred = sem("sqred")
        gn_ok = sem("gn_ok")
        x_sum = sem("x_sum")
        rsq = sem("rsq")
        rsq_k = sem("rsq_k")
        gn_mm = sem("gn_mm")
        wT_mm = sem("wT_mm")
        wprep = sem("wprep")
        wprep_a = sem("wprep_a")
        zeros_w2 = sem("zeros_w2")
        wprep2 = sem("wprep2")
        xp_ok = sem("xp_ok")
        xT_mm = sem("xT_mm")
        xT_ok = sem("xT_ok")
        ln_v0 = sem("ln_v0")
        ln_0 = sem("ln_0")
        ln_z = sem("ln_z")
        ln_v = sem("ln_v")
        ln_q = sem("ln_q")
        ln_a = sem("ln_a")
        zn_st = [sem("zn_st0"), sem("zn_st1")]
        Z_ld = [sem("Z_ld0"), sem("Z_ld1")]
        zbd_ld = sem("zbd_ld")
        zT_mm = sem("zT_mm")
        zT_ok = sem("zT_ok")
        t_mm = sem("t_mm")
        t_hi = sem("t_hi")
        t_lo = sem("t_lo")
        g_mm = sem("g_mm")
        g_th = sem("g_th")
        s_mm = sem("s_mm")
        s_max = sem("s_max")
        s_sub = sem("s_sub")
        s_exp = sem("s_exp")
        p_sum = sem("p_sum")
        p_rec = sem("p_rec")
        p_nrm = sem("p_nrm")
        p_hi = sem("p_hi")
        p_lo = sem("p_lo")
        pt_mm = sem("pt_mm")
        pt_ok = [sem("pt_ok0"), sem("pt_ok1")]
        u_mm = sem("u_mm")
        u_ok = sem("u_ok")
        o_mm = sem("o_mm")
        o_ok = sem("o_ok")
        w_mm = sem("w_mm")
        x1_ok = sem("x1_ok")
        x1_sq = sem("x1_sq")
        x1_st = sem("x1_st")
        g2_ok = sem("g2_ok")
        g2_mm = sem("g2_mm")
        bbd_z = sem("bbd_z")
        z1_m = [sem("z1_m0"), sem("z1_m1")]
        z1_h = sem("z1_h")
        z1_l = [sem("z1_l0"), sem("z1_l1")]
        pj_mm = sem("pj_mm")
        pj_th = sem("pj_th")
        pj_ok = sem("pj_ok")
        bbd_ld = [sem("bbd_ld0"), sem("bbd_ld1")]
        k_mm = sem("k_mm")
        k_cp = sem("k_cp")
        k_sq = sem("k_sq")
        k_st = [sem("k_st0"), sem("k_st1")]
        kT_ld = [sem(f"kT_ld{g}") for g in range(4)]
        go_mm = sem("go_mm")
        go_th = sem("go_th")
        k_ok = sem("k_ok")
        ks_mm = sem("ks_mm")
        lo_mm = sem("lo_mm")
        lo_s = sem("lo_s")
        lo_g = sem("lo_g")
        x2_ok = [sem("x2_ok0"), sem("x2_ok1")]
        x2_mm = sem("x2_mm")
        x2_cp = [sem("x2_cp0"), sem("x2_cp1")]
        out_st = sem("out_st")

        LZ, LV = 7, 4
        LOOPS = (NS - 4) // 2
        UNITS = (0, 2, 4, 1, 3, 5, 6, 7)
        POOL_UNITS = (0, 2, 1, 3)
        NZ_MASKS, NZ_Z = 15, 3
        WTS, WTS2 = 16 * 11, 16 * 16

        def bcast(ap, axis, n):
            v = ap.unsqueeze(axis)
            return v.to_broadcast([n if i == axis else s for i, s in enumerate(v.shape)])

        def wait_zn(engine, j):
            if isinstance(j, int) and j == 0:
                engine.wait_ge(ln_0, LZ)
            else:
                engine.wait_ge(ln_z, LZ * j)

        block = ctx.enter_context(nc.Block())
        x_src = x.rearrange("n (f e) b c -> (n f) e (b c)", e=A2)
        out_dst = out.rearrange("n (f e) b c -> (n f) e (b c)", e=A2)

        def sp_store(sp, j, par):
            wait_zn(sp, j)
            sp.dma_start(zn_dram.rearrange("n f s e m -> (n f) s (e m)")[:, bass.ds(j, 1)],
                         zn_tok[:, par].rearrange("p e d b k -> p (e d b k)").unsqueeze(1)).then_inc(zn_st[par], 16)

        def sp_period(sp, j, par, half, last=False):
            sp.wait_ge(zT_ok, j + 1)
            if isinstance(j, int) and j == 1:
                sp.wait_ge(s_mm, 4)
            for e in range(A2):
                rows = slice(D * e, D * e + D)
                sp.dma_start(zbd[rows, e], znT[rows]).then_inc(zbd_ld, 16)
            if not last:
                sp_store(sp, j + 1, 1 - par)
            else:
                sp.wait_ge(u_mm, 8 * (j - 1))
            sp.wait_ge(zn_st[par], 16 * (half + 1))
            for copy in range(2):
                for e in range(A2):
                    r0 = 64 * copy + N * e
                    sp.dma_start(Z[r0:r0 + N, par, :, e].rearrange("p f d b k -> p f (d b k)"),
                                 zn_dram[:, :, bass.ds(j, 1), e].rearrange("n f s m -> n (f s) m")
                                 ).then_inc(Z_ld[par], 16)

        def k_store(engine, g):
            engine.wait_ge(k_cp, 2 * g + 2)
            src = k_sb.rearrange("p (s c m) -> p s c m", s=2, c=8)[:, g % 2]
            dst = k_dram[:, :, :, 128 * g:128 * g + 128]
            engine.dma_start(dst.rearrange("(c8 c4) f e m -> c4 (f e) c8 m", c4=4)
                             .rearrange("c4 i c8 m -> (c4 i) c8 m"), src).then_inc(k_st[g % 2], 16)

        def k_load(engine, g):
            engine.wait_ge(k_st[g % 2], 16 * (g // 2 + 1))
            for e in range(A2):
                engine.dma_start(kT.rearrange("p (f m) -> p f m", f=A4)[D * e:D * e + D, :, 128 * g:128 * g + 128],
                                 k_dram[:, :, e, 128 * g:128 * g + 128]).then_inc(kT_ld[g], 16)

        @block.sync
        def _(sp):
            for e in range(A2):
                sp.dma_start(x_tok[:, e].rearrange("p b d -> p (b d)"), x_src[:, e]).then_inc(x_in[e], 16)
            for k, w in enumerate((Wq, Wk)):
                sp.dma_start(wq_in[:, k], w).then_inc(wts_in, 16)
            sp.dma_start(wg_in[:, :, :].rearrange("p h c -> p (h c)"),
                         Wg.unsqueeze(0).to_broadcast([A2, D, H * C])).then_inc(wts_in, 16)
            sp.dma_start(wv_in[:, :, :].rearrange("p h c -> p (h c)"),
                         Wv.unsqueeze(0).to_broadcast([A2, D, H * C])).then_inc(wts_in, 16)
            sp.dma_start(w_bc[:, :], ln_w.partition_broadcast(128)).then_inc(wts_in, 16)
            sp.dma_start(b_bc[:, :], ln_b.partition_broadcast(128)).then_inc(wts_in, 16)
            for r in range(2):
                rows = slice(64 * r, 64 * r + 64)
                sp.dma_start(wo_in[rows].rearrange("p k d -> p (k d)"),
                             Wo[r].unsqueeze(0).to_broadcast([A2, C, HP * D])).then_inc(wts_in, 16)
                sp.dma_start(bg_in[rows], bg[r].unsqueeze(0).to_broadcast([A2, C, HP])).then_inc(wts_in, 16)
            sp.dma_start(bo_col[:, :], bo.unsqueeze(0).to_broadcast([A2, D]).unsqueeze(2)).then_inc(wts_in, 16)
            for m, w in enumerate((W_ga, W_gb, W_la, W_lb)):
                sp.dma_start(w1_in[D * m:D * m + D], w.unsqueeze(1).to_broadcast([D, A2, D])).then_inc(wts2_in, 16)
            for m, w in enumerate((W_go, W_lo)):
                sp.dma_start(w2_in[D * m:D * m + D], w.unsqueeze(1).to_broadcast([D, A2, D])).then_inc(wts2_in, 16)
            sp.wait_ge(zeros_w, 1)
            for m, b in enumerate((b_ga, b_gb, b_la, b_lb)):
                sp.dma_start(b1_in[0:65:32, m // 2, m % 2], b.partition_broadcast(3)).then_inc(wts2_in, 16)
            for k, b in ((Bgo, b_go), (Blo, b_lo)):
                sp.dma_start(col[:, k:k + 1], b.unsqueeze(0).to_broadcast([A2, D]).unsqueeze(2)).then_inc(wts2_in, 16)
            for k, v in ((Ain, al_in), (Bin, be_in), (Aout, al_o), (Bout, be_o)):
                sp.dma_start(col[:, k:k + 1], v.partition_broadcast(128)).then_inc(wts2_in, 16)

            sp.wait_ge(zeros_z, NZ_MASKS + NZ_Z)
            sp_store(sp, 0, 0)
            for j in range(3):
                sp_period(sp, j, j % 2, j // 2)
            with sp.Fori(0, LOOPS) as it:
                for i in range(2):
                    sp_period(sp, 2 * it + 3 + i, 1 - i, it + 1 + i)
            sp_period(sp, NS - 1, 1, NS // 2 - 1, last=True)

            def bbd_load(g):
                sp.wait_ge(pj_ok, 16 * (g + 1))
                if g == 0:
                    sp.wait_ge(bbd_z, 2)
                if g >= 2:
                    sp.wait_ge(k_mm, 2 * (g - 1))
                for n in range(4):
                    rows = slice(L * n, L * n + L)
                    sp.dma_start(bbd[g % 2][rows, n].rearrange("p j c -> p (j c)"),
                                 b_buf[g % 2][rows].rearrange("p j c -> p (j c)")).then_inc(bbd_ld[g % 2], 16)

            bbd_load(0)
            bbd_load(1)
            k_store(sp, 0)
            k_load(sp, 0)
            bbd_load(2)
            k_store(sp, 1)
            k_load(sp, 1)
            bbd_load(3)
            k_store(sp, 2)
            k_load(sp, 2)
            k_store(sp, 3)
            k_load(sp, 3)
            for i in range(0, NS, 2):
                for m in (i, i + 1):
                    sp.wait_ge(x2_cp[m % 2], m // 2 + 1)
                sp.dma_start(out_dst[:, :, SB * D * i:SB * D * (i + 2)],
                             out_tok[:, :, SB * i:SB * (i + 2)].rearrange("p e b d -> p e (b d)")).then_inc(out_st, 16)
            sp.wait_ge(out_st, 16 * (NS // 2))

        def pool_ln_front(pool, j, par):
            z = zc[:, par].rearrange("p e b d -> p e (b d)").rearrange("p e (b d) -> p e b d", d=D)
            if not isinstance(j, int) or j >= 2:
                wait_zn(pool, j - 2)
            nc.gpsimd.tensor_tensor(z, x_tok[:, :, bass.ds(j * SB, SB), :],
                                    bcast(bcast(gn_r[:, :], 1, SB), 1, A2), ALU.mult).then_inc(ln_z, 1)
            pool.wait_ge(ln_z, LZ * (j - 1) + 1)
            zf = zc[:, par].rearrange("p e b d -> p (e b) d")
            nc.gpsimd.tensor_tensor(zf, zf, bcast(gn_sh[:, :], 1, A2 * SB), ALU.add).then_inc(ln_z, 1)

        def pool_ln_back(pool, j, par):
            zf = zc[:, par].rearrange("p e b d -> p (e b) d")
            pool.wait_ge(ln_v, LV * (j + 1))
            nc.gpsimd.tensor_tensor(ln_rs[:, par], ln_ve[:, par], minus_half[:, 0:A2 * SB], ALU.pow).then_inc(ln_z, 1)
            pool.wait_ge(ln_z, LZ * (j - 1) + 3)
            nc.gpsimd.tensor_tensor(zf, zf, bcast(ln_rs[:, par], 2, D), ALU.mult).then_inc(ln_z, 1)
            pool.wait_ge(ln_z, LZ * (j - 1) + 4)
            nc.gpsimd.tensor_tensor(zf, zf, bcast(w_bc[:, :], 1, A2 * SB), ALU.mult).then_inc(ln_z, 1)
            pool.wait_ge(ln_z, LZ * (j - 1) + 5)
            nc.gpsimd.tensor_tensor(zf, zf, bcast(b_bc[:, :], 1, A2 * SB), ALU.add).then_inc(ln_z, 1)

        def pool_ln_low(pool, j, par):
            pool.wait_ge(ln_a, j + 1)
            hl = zn_tok[:, par].rearrange("p e d b k -> p e b d k")
            nc.gpsimd.tensor_tensor(hl[:, :, :, :, LO], zc[:, par], hl[:, :, :, :, HI], ALU.subtract).then_inc(ln_z, 1)

        def pool_norm(pool, m, ks):
            pool.wait_ge(p_rec, 2 * m + ks[0] // 2 + 1)
            for k in ks:
                P = S_sb[:, 8 * k:8 * k + 8].rearrange("p q a n -> p (q a) n")
                nc.gpsimd.tensor_tensor(P, P, bcast(rden[:, 32 * k:32 * k + 32], 2, N), ALU.mult).then_inc(p_nrm, 1)

        def p_low(engine, ops, m, ks):
            for k in ks:
                P = S_sb[:, 8 * k:8 * k + 8].rearrange("p q a n -> p q (a n)")
                engine.wait_ge(p_hi, 4 * m + k + 1)
                ops.tensor_tensor(P2[:, 8 * k:8 * k + 8, LO], P, P2[:, 8 * k:8 * k + 8, HI],
                                  ALU.subtract).then_inc(p_lo, 1)

        def pool_sqx(pool, s):
            pool.wait_ge(x1_ok, s + 1)
            v = xT[:, bass.ds(s * COLS, COLS)]
            nc.gpsimd.tensor_tensor(sqx[:, :], v, v, ALU.mult).then_inc(x1_sq, 1)

        def pool_period(pool, j, par, tail=True, LN=True, stats=True):
            if LN and not (isinstance(j, int) and j == 0):
                pool_ln_front(pool, j + 1, 1 - par)
            if tail:
                pool_norm(pool, j - 1, (0, 1))
            if stats:
                pool_sqx(pool, j - 3)
            if tail:
                pool_norm(pool, j - 1, (2, 3))
            if LN:
                pool_ln_back(pool, j + 1, 1 - par)
            own = tail and not (isinstance(j, int) and j == 1)
            if own:
                p_low(pool, nc.gpsimd, j - 1, (0, 1))
            if LN:
                pool_ln_low(pool, j + 1, 1 - par)
            if own:
                p_low(pool, nc.gpsimd, j - 1, (2, 3))

        def z1_norm(engine, ops, g, done):
            for n in range(4 * g, 4 * g + 4):
                ops.tensor_scalar(z1f[g % 2][:, :, n % 4], xT[:, :].rearrange("p (b f n) -> p f b n", f=A4, n=N)[:, :, :, n],
                                  g2[:, 10, n:n + 1], g2[:, 11, n:n + 1], ALU.mult, ALU.add).then_inc(done, 1)

        def z1_low(engine, ops, g, done):
            halves = 2 if g == 0 else 1
            for k in range(halves):
                fs = slice(A4 // halves * k, A4 // halves * (k + 1))
                engine.wait_ge(z1_h, g + k + 1 + (g > 0))
                ops.tensor_tensor(z1[LO][:, fs, 4 * g:4 * g + 4], z1f[g % 2][:, fs], z1[HI][:, fs, 4 * g:4 * g + 4],
                                  ALU.subtract).then_inc(done, 1)

        def pool_clear2():
            zeros = lambda v: nc.gpsimd.memset(v, 0.0)
            zeros(B1[:, :, :, :, :].rearrange("p k e m d -> p (k e m d)").bitcast(f32))
            zeros(W1_bd[:, :, :, :, :, :].rearrange("p l k e m d -> p (l k e m d)").bitcast(f32))
            zeros(Wgo_bd[:, :, :, :].rearrange("p l e d -> p (l e d)").bitcast(f32))
            zeros(Wlo_bd[:, :, :].rearrange("p e d -> p (e d)"))
            nc.gpsimd.memset(ones_bf[:, :], 1.0)
            nc.gpsimd.memset(ones_col[:, :], 1.0)
            nc.gpsimd.memset(allsum[:, 0], 1.0 / (A2 * N * D))
            nc.gpsimd.memset(allsum[:, 1], 1.0 / (N * L * L * D)).then_inc(zeros_w2, 1)

        @block.gpsimd
        def _(pool):
            nc.gpsimd.memset(minus_half[:, :], -0.5).then_inc(zeros_z, 1)
            seq = seqsum[:, :].rearrange("p (n f) -> p n f", f=A4)
            chn = chsum[:, :].rearrange("p (e c) -> p e c", c=D)
            nc.gpsimd.memset(ident[:, :], 0.0).then_inc(zeros_z, 1)
            nc.gpsimd.memset(seqsum[:, :], 1.0 / (L * L)).then_inc(zeros_z, 1)
            nc.gpsimd.memset(headmask[:, :], 1.0).then_inc(zeros_z, 1)
            nc.gpsimd.memset(chsum[:, :], 0.0).then_inc(zeros_z, 1)
            pool.wait_ge(zeros_z, 5)
            nc.gpsimd.affine_select(out=ident[:, :], in_=ident[:, :], compare_op=ALU.not_equal, fill=1.0, base=0,
                                    pattern=[[-1, 128]], channel_multiplier=1).then_inc(zeros_z, 1)
            nc.gpsimd.affine_select(out=seq, in_=seq, compare_op=ALU.is_ge, fill=0.0, base=0,
                                    pattern=[[-A4, N], [0, A4]], channel_multiplier=1).then_inc(zeros_z, 1)
            nc.gpsimd.affine_select(out=headmask[:, :], in_=headmask[:, :], compare_op=ALU.is_ge, fill=0.0, base=0,
                                    pattern=[[-C, H]], channel_multiplier=1).then_inc(zeros_z, 1)
            pool.wait_ge(zeros_z, 8)
            nc.gpsimd.affine_select(out=seq, in_=seq, compare_op=ALU.is_ge, fill=0.0, base=A4 - 1,
                                    pattern=[[A4, N], [0, A4]], channel_multiplier=-1).then_inc(zeros_z, 1)
            nc.gpsimd.affine_select(out=headmask[:, :], in_=headmask[:, :], compare_op=ALU.is_ge, fill=0.0, base=C - 1,
                                    pattern=[[C, H]], channel_multiplier=-1).then_inc(zeros_z, 1)
            for k in range(A2):
                if k:
                    pool.wait_ge(zeros_z, 10 + k)
                nc.gpsimd.affine_select(out=chn, in_=chn, compare_op=ALU.not_equal, fill=1.0 / (L * L), base=-D * k,
                                        pattern=[[0, A2], [-1, D]], channel_multiplier=1).then_inc(zeros_z, 1)
            nc.gpsimd.tensor_copy(ident16[:, :], ident[:, :]).then_inc(zeros_z, 1)
            chunk = lambda e: x_tok[:, e].rearrange("p b d -> p (b d)")
            for k in range(2):
                for e in (2 * k, 2 * k + 1):
                    pool.wait_ge(x_in[e], 16)
                nc.gpsimd.tensor_tensor(gn_x[k], chunk(2 * k), chunk(2 * k + 1), ALU.add).then_inc(x_sum, 1)
            nc.gpsimd.memset(zbd[:, :, :, :].rearrange("p e k c -> p (e k c)").bitcast(f32), 0.0).then_inc(zeros_z, 1)
            for k in range(2):
                nc.gpsimd.memset(Z[:, k].rearrange("p f e d b k -> p (f e d b k)").bitcast(f32), 0.0).then_inc(zeros_z, 1)
            pool.wait_ge(gn_ok, 9)
            pool.wait_ge(wts_in, WTS)
            pool_ln_front(pool, 1, 1)
            pool_clear2()
            for j in range(3):
                pool_period(pool, j, j % 2, tail=j >= 1, stats=False)
            with pool.Fori(0, LOOPS) as it:
                for i in range(2):
                    pool_period(pool, 2 * it + 3 + i, 1 - i)
            for j in range(NS - 1, NS + 2):
                pool_period(pool, j, j % 2, tail=j <= NS, LN=j < NS - 1)
            nc.gpsimd.memset(bbd[1].rearrange("p n j c -> p (n j c)"), 0.0).then_inc(bbd_z, 1)
            pool.wait_ge(u_mm, 8 * NS)
            nc.gpsimd.memset(bbd[0].rearrange("p n j c -> p (n j c)"), 0.0).then_inc(bbd_z, 1)
            pool.wait_ge(g2_ok, 15)
            z1_norm(pool, nc.gpsimd, 1, z1_m[1])
            pool.wait_ge(z1_l[0], 2)
            z1_norm(pool, nc.gpsimd, 2, z1_m[1])
            pool.wait_ge(z1_l[0], 3)
            z1_norm(pool, nc.gpsimd, 3, z1_m[1])
            z1_low(pool, nc.gpsimd, 2, z1_l[1])
            z1_low(pool, nc.gpsimd, 3, z1_l[1])
            pool.wait_ge(k_ok, 4)
            nc.gpsimd.tensor_tensor(col[:, KR:KR + 1], col[:, RV:RV + 1], minus_half[:, 0:1], ALU.pow).then_inc(rsq_k, 1)
            for u in POOL_UNITS:
                pool.wait_ge(lo_g, UNITS.index(u) + 1)
                v = half_n(x2.rearrange("p (b n f) -> p b n f", n=N, f=A4), u)
                nc.gpsimd.tensor_tensor(v, v, half_n(x1_nfb, u), ALU.add).then_inc(x2_ok[0], 1)

        def act_ln_square(act, j, par):
            act.wait_ge(ln_v, LV * j + 2)
            nc.scalar.activation(sq[:, 0:512], zc[:, par].rearrange("p e b d -> p (e b d)"),
                                 ACT.Square).then_inc(ln_q, 1)

        def act_ln_high(act, j, par, half):
            if isinstance(j, int) and j == 0:
                act.wait_ge(ln_0, 6)
            else:
                act.wait_ge(ln_z, LZ * (j - 1) + 6)
            if not isinstance(j, int) or j >= 2:
                act.wait_ge(zn_st[par], 16 * half)
            nc.scalar.copy(zn_tok[:, par].rearrange("p e d b k -> p e b d k")[:, :, :, :, HI],
                           zc[:, par]).then_inc(ln_a, 1)

        def act_znT(act, j):
            if isinstance(j, int) and j == 1:
                act.wait_ge(zbd_ld, 64)
            act.wait_ge(zT_mm, j + 1)
            src = bank_w[:, :].bitcast(f16).rearrange("p (k n f) -> p k f n", f=A4, n=N)
            dst = znT[:, :, :].rearrange("p k c -> p (k c)").rearrange("p (k f n) -> p k f n", f=A4, n=N)
            nc.scalar.copy(dst, src).then_inc(zT_ok, 1)

        def act_weights(act):
            for g in range(A2):
                rows = slice(D * g, D * g + D)
                nc.scalar.copy(Wv_bd[rows, :, g], wv_in[rows]).then_inc(wprep_a, 1)
            act.wait_ge(wT_mm, 4)
            nc.scalar.mul(w12_f[:, 64:128], PS[6][:, 64:128], 0.5)
            nc.scalar.copy(w12_f[:, 0:64], PS[6][:, 0:64])
            nc.scalar.copy(w12_f[:, 128:192], PS[6][:, 128:192]).then_inc(wprep_a, 1)

        def act_period(act, j, par, half, tail=True, B=True, A=True, LN=True):
            s, m = j - 2, j - 1
            early = isinstance(j, int) and j < 2

            def u_copies(ks):
                for k in ks:
                    act.wait_ge(u_mm, 8 * s + k + 1)
                    nc.scalar.copy(u_sb[:, :, 4 * k:4 * k + 4].rearrange("p h q i -> p q h i"),
                                   bank_u(k)[:, :].rearrange("p (q h i) -> p q h i", q=4, h=H)).then_inc(u_ok, 1)

            def p_high(ks):
                for k in ks:
                    act.wait_ge(p_nrm, 4 * m + k + 1)
                    if not isinstance(m, int) or m >= 1:
                        act.wait_ge(pt_mm, 4 * (m - 1) + k + 1)
                    nc.scalar.copy(P2[:, 8 * k:8 * k + 8, HI],
                                   S_sb[:, 8 * k:8 * k + 8].rearrange("p q a n -> p q (a n)")).then_inc(p_hi, 1)

            def t_high(hs):
                for h in hs:
                    act.wait_ge(t_mm, H * j + h + 1)
                    nc.scalar.copy(t_sb[:, HI, :, h], bank_tg(h)[:, :].rearrange("p (q i) -> p q i", i=N)).then_inc(t_hi, 1)

            def exps(ks):
                for k in ks:
                    act.wait_ge(s_sub, 4 * j + k + 1)
                    v = S_sb[:, 8 * k:8 * k + 8].rearrange("p q a n -> p (q a n)")
                    nc.scalar.activation(v, v, ACT.Exp).then_inc(s_exp, 1)

            def gates(ks):
                for k in ks:
                    act.wait_ge(g_mm, HP * j + k + 1)
                    nc.scalar.activation(th[:, par, k], bank_tg(H + k)[:, :], ACT.Tanh, bias=bg_h[:, k:k + 1],
                                         scale=0.5).then_inc(g_th, 1)

            def PT_copy(k):
                act.wait_ge(pt_mm, 4 * s + k + 1)
                nc.scalar.copy(PT[:, 8 * k:8 * k + 8].rearrange("p q m -> p (q m)"),
                               bank_b(k)[:, :].bitcast(f16)).then_inc(pt_ok[1], 1)

            if B:
                PT_copy(1)
            if A and not early:
                act_znT(act, j)
            if B:
                PT_copy(3)
                u_copies(range(4))
            if LN and not early:
                act_ln_square(act, j + 1, 1 - par)
            if B:
                u_copies(range(4, 8))
            if early:
                if j == 0:
                    t_high(range(H))
                    act_ln_high(act, 1, 1, 0)
                    nc.scalar.activation(scrap[:, 0:1], minus_half[:, 0:1], ACT.Tanh)
                    act_weights(act)
                else:
                    t_high((0, 1, 2))
                    p_high((0, 1))
                    t_high((3, 4))
                    p_high((2, 3))
                    act_ln_square(act, 2, 0)
                    t_high((5, 6, 7))
                exps((0,))
                gates((0, 1))
                exps((1,))
                gates((2, 3))
                if j == 0:
                    act_znT(act, 1)
                else:
                    act_ln_high(act, 2, 0, 1)
                exps((2, 3))
                return
            if A:
                t_high((0, 1, 2))
            if tail:
                p_high((0, 1, 2) if A else range(4))
            if A:
                t_high(range(3, H))
            if LN:
                act_ln_high(act, j + 1, 1 - par, half + par)
            if tail and A:
                p_high((3,))
            if A:
                exps((0,))
                gates((0, 1))
                exps((1,))
                gates((2,))
                exps((2, 3))
                gates((3,))

        @block.scalar
        def _(act):
            act.wait_ge(zeros_z, 1)
            nc.scalar.activation(scrap[:, 0:1], minus_half[:, 0:1], ACT.Sqrt, scale=-1.0)
            for e in range(A2):
                act.wait_ge(x_in[e], 16)
                nc.scalar.activation(gn_sq[:, e], x_tok[:, e].rearrange("p b d -> p (b d)"), ACT.Square).then_inc(sq_ok, 1)
            for e in range(A2):
                nc.scalar.copy(x_perm[:, :, e], x_tok[:, e]).then_inc(xp_ok, 1)
            def xT_copy(i):
                act.wait_ge(xT_mm, i + 1)
                nc.scalar.copy(xT[:, COLS * i:COLS * i + COLS].rearrange("p (b f n) -> p b f n", f=A4, n=N),
                               PS[2 + i % 2][:, :].rearrange("p (b n f) -> p b f n", f=A4, n=N)).then_inc(xT_ok, 1)
            xT_copy(0)
            act.wait_ge(gn_ok, 8)
            nc.scalar.activation(gn_r[:, :], gn_tmp[:, 2], ACT.Sqrt).then_inc(rsq, 1)
            xT_copy(1)
            xT_copy(2)
            act_ln_square(act, 0, 0)
            xT_copy(3)
            act.wait_ge(ln_v0, 1)
            nc.scalar.activation(ln_rs[:, 0], ln_inv[:, :], ACT.Sqrt).then_inc(ln_0, 1)
            xT_copy(4)
            act.wait_ge(wT_mm, 2)
            for g in range(A2):
                rows = slice(D * g, D * g + D)
                nc.scalar.mul(A_bd[rows, HI, :, g], PS[1][rows, 0:256].rearrange("p (h d) -> p h d", h=H),
                              0.25).then_inc(wprep_a, 1)
            act.wait_ge(wts_in, WTS)
            nc.scalar.mul(bg_h[:, :], bg_in[:, :], 0.5).then_inc(wprep_a, 1)
            act_ln_high(act, 0, 0, 0)
            xT_copy(5)
            act_znT(act, 0)
            xT_copy(6)
            xT_copy(7)
            act_ln_square(act, 1, 1)
            for g in range(A2):
                rows = slice(D * g, D * g + D)
                nc.scalar.copy(Wg_bd[rows, HI, :, g], wg_in[rows]).then_inc(wprep_a, 1)
            for j in range(3):
                act_period(act, j, j % 2, j // 2, tail=j >= 1, B=j >= 2)
            with act.Fori(0, LOOPS) as it:
                for i in range(2):
                    act_period(act, 2 * it + 3 + i, 1 - i, it + 1 + i)
            for j in range(NS - 1, NS + 2):
                act_period(act, j, j % 2, j // 2, tail=j <= NS, A=j < NS, LN=j < NS - 1)
            nc.scalar.activation(scrap[:, 0:1], minus_half[:, 0:1], ACT.Sqrt, scale=-1.0)
            act.wait_ge(x1_ok, NS)
            act.wait_ge(x1_st, 2 * (NS - 1))
            nc.scalar.activation(sqx[:, :], xT[:, (NS - 1) * COLS:], ACT.Square).then_inc(x1_sq, 1)

            act.wait_ge(g2_ok, 12)
            nc.scalar.activation(g2[:, 6], g2[:, 5], ACT.Sqrt).then_inc(rsq, 1)
            nc.scalar.activation(scrap[:, 0:1], minus_half[:, 0:1], ACT.Tanh)

            def z1_high(g):
                if g == 0:
                    act.wait_ge(z1_m[0], 4)
                else:
                    act.wait_ge(z1_m[1], 4 * g)
                halves = 2 if g == 0 else 1
                for k in range(halves):
                    fs = slice(A4 // halves * k, A4 // halves * (k + 1))
                    nc.scalar.copy(z1[HI][:, fs, 4 * g:4 * g + 4], z1f[g % 2][:, fs]).then_inc(z1_h, 1)
            z1_high(0)

            def gates(g):
                for f in range(A4):
                    if A4 * g + f in (2, 6, 13):
                        z1_high((2, 6, 13).index(A4 * g + f) + 1)
                    i = A4 * g + f
                    act.wait_ge(pj_mm, i + 1)
                    if i >= 3:
                        act.wait_ge(pj_ok, 2 * (i - 2))
                    nc.scalar.activation(gt[i % 3].rearrange("p a m c -> p (a m c)"), PS[i % 3][:, 0:256],
                                         ACT.Tanh, scale=0.5).then_inc(pj_th, 1)

            def k_copies(g):
                if g == 0:
                    act.wait_ge(z1_l[1], 2)
                for h in range(2):
                    i = 2 * g + h
                    act.wait_ge(k_mm, i + 1)
                    if g >= 2:
                        act.wait_ge(k_st[g % 2], 16)
                    dst = k_sb.rearrange("p (s c m) -> p s c m", s=2, c=8)[:, g % 2, 4 * h:4 * h + 4]
                    nc.scalar.activation(dst.rearrange("p c m -> p (c m)"), PS[3 + i % 4][:, :], ACT.Identity,
                                         accum_out=ksum[:, 0, i:i + 1]).then_inc(k_cp, 1)
                    nc.scalar.activation(sq[:, 512 * h:512 * h + 512], PS[3 + i % 4][:, :], ACT.Square,
                                         accum_out=ksum[:, 1, i:i + 1]).then_inc(k_sq, 1)

            gates(0)
            gates(1)
            k_copies(0)
            gates(2)
            k_copies(1)
            gates(3)
            k_copies(2)
            act.wait_ge(g2_ok, 9)

            def out_gates(js):
                for j in js:
                    act.wait_ge(go_mm, j + 1)
                    nc.scalar.activation(tg[:, 512 * j:512 * j + 512], PS[j % 3][:, :], ACT.Tanh,
                                         bias=col[:, BGH:BGH + 1], scale=0.5).then_inc(go_th, 1)
            out_gates(range(0, 6))
            k_copies(3)
            out_gates((6, 7))
            act.wait_ge(k_ok, 8)
            for u in UNITS:
                act.wait_ge(lo_mm, UNITS.index(u) + 1)
                nc.scalar.activation(unit(x2, u), bank_lo(u)[:, :].rearrange("p (b m) -> p b m", m=32),
                                     ACT.Identity, bias=col[:, CV:CV + 1], scale=col[:, KS:KS + 1]).then_inc(lo_s, 1)
            for i in range(0, NS, 2):
                act.wait_ge(x2_mm, i + 1)
                nc.scalar.copy(out_tok[:, :, SB * i:SB * i + SB].rearrange("p e b d -> p b e d"),
                               PS[1 + i % 3][:, :].rearrange("p (b e d) -> p b e d", b=SB, e=A2)).then_inc(x2_cp[0], 1)

        def dve_ln_centre(dve, j, par):
            z = zc[:, par].rearrange("p e b d -> p (e b) d")
            if isinstance(j, int) and j == 0:
                dve.wait_ge(ln_0, 2)
            else:
                dve.wait_ge(ln_z, LZ * (j - 1) + 2)
            nc.vector.tensor_reduce(ln_mu[:, par], z, op=ALU.add, axis=AX.X).then_inc(ln_v, 1)
            dve.wait_ge(ln_v, LV * j + 1)
            nc.vector.scalar_tensor_tensor(out=z, in0=bcast(ln_mu[:, par], 2, D), scalar=-1.0 / D, in1=z,
                                           op0=ALU.mult, op1=ALU.add).then_inc(ln_v, 1)

        def dve_ln_rstd(dve, j, par):
            dve.wait_ge(ln_q, j + 1)
            nc.vector.tensor_reduce(ln_var[:, par], sq[:, 0:512].rearrange("p (t d) -> p t d", d=D), op=ALU.add,
                                    axis=AX.X).then_inc(ln_v, 1)
            dve.wait_ge(ln_v, LV * j + 3)
            nc.vector.tensor_scalar(ln_ve[:, par], ln_var[:, par], 1.0 / D, EPS, ALU.mult, ALU.add).then_inc(ln_v, 1)

        def dve_sums(dve, m, ks):
            for k in ks:
                dve.wait_ge(s_exp, 4 * m + k + 1)
                nc.vector.tensor_reduce(sums[:, 32 * k:32 * k + 32], S_sb[:, 8 * k:8 * k + 8]
                                        .rearrange("p q a n -> p (q a) n"), op=ALU.add, axis=AX.X).then_inc(p_sum, 1)

        def dve_stats(dve, s):
            dve.wait_ge(x1_ok, s + 1)
            nc.vector.tensor_reduce(st1[:, 0, bass.ds(s, 1)].rearrange("p s n -> p (s n)"),
                                    xT[:, bass.ds(s * COLS, COLS)].rearrange("p (q n) -> p n q", n=N),
                                    op=ALU.add, axis=AX.X).then_inc(x1_st, 1)
            dve.wait_ge(x1_sq, s + 1)
            nc.vector.tensor_reduce(st1[:, 1, bass.ds(s, 1)].rearrange("p s n -> p (s n)"),
                                    sqx[:, :].rearrange("p (q n) -> p n q", n=N),
                                    op=ALU.add, axis=AX.X).then_inc(x1_st, 1)

        def dve_reciprocal(dve, m, half):
            dve.wait_ge(p_sum, 4 * m + 2 * half + 2)
            if not isinstance(m, int) or m >= 1:
                dve.wait_ge(p_nrm, 4 * m)
            nc.vector.reciprocal(rden[:, 64 * half:64 * half + 64], sums[:, 64 * half:64 * half + 64]).then_inc(p_rec, 1)

        def dve_gate_weights(dve):
            dve.wait_ge(wprep_a, 9)
            for g in range(A2):
                rows = slice(D * g, D * g + D)
                nc.vector.tensor_tensor(Wg_bd[rows, LO, :, g], wg_in[rows], Wg_bd[rows, HI, :, g],
                                        ALU.subtract).then_inc(wprep, 1)

        def dve_period(dve, j, par, tail=True, B=True, A=True, LN=True, stats=True):
            s, m = j - 2, j - 1
            for i, k in enumerate((0, 2)):
                if B:
                    dve.wait_ge(pt_mm, 4 * s + k + 1)
                    nc.vector.tensor_copy(PT[:, 8 * k:8 * k + 8].rearrange("p q m -> p (q m)"),
                                          bank_b(k)[:, :].bitcast(f16)).then_inc(pt_ok[0], 1)
                if tail:
                    dve_sums(dve, m, (2 + i,))
            if tail:
                dve_reciprocal(dve, m, 1)
            if LN and not (isinstance(j, int) and j < 2):
                dve_ln_centre(dve, j + 1, 1 - par)
                dve_ln_rstd(dve, j + 1, 1 - par)
            if stats:
                dve_stats(dve, s - 1)
            if isinstance(j, int) and j == NS:
                dve_weights2(dve)
            if isinstance(j, int) and j == NS + 1:
                dve_biases2(dve)
            def gate_o(ks):
                for k in ks:
                    dve.wait_ge(o_mm, HP * s + k + 1)
                    dve.wait_ge(g_th, HP * s + k + 1)
                    nc.vector.scalar_tensor_tensor(out=og[:, k], in0=th[:, par, k], scalar=1.0, in1=bank_b(k)[:, :],
                                                   op0=ALU.add, op1=ALU.mult).then_inc(o_ok, 1)

            for h in range(H if A else 0):
                if h == 3 and B:
                    gate_o((0, 1))
                dve.wait_ge(t_hi, H * j + h + 1)
                nc.vector.tensor_tensor(t_sb[:, LO, :, h], bank_tg(h)[:, :].rearrange("p (q i) -> p q i", i=N),
                                        t_sb[:, HI, :, h], ALU.subtract).then_inc(t_lo, 1)
                if isinstance(j, int) and j == 0 and h == 0:
                    dve_gate_weights(dve)
                if isinstance(j, int) and j == 1:
                    if h == 3:
                        dve_ln_centre(dve, 2, 0)
                    if h == 5:
                        dve_ln_rstd(dve, 2, 0)
                    if h in (2, 4):
                        p_low(dve, nc.vector, 0, (h - 2, h - 1))
            if B:
                gate_o((2, 3) if A else range(HP))
            for k in range(4 if A else 0):
                S = bank_s(k)[:, :].rearrange("p (r n) -> p r n", n=N)
                dve.wait_ge(s_mm, 4 * j + k + 1)
                nc.vector.tensor_reduce(nmax[:, k % 2], S, op=ALU.max, axis=AX.X).then_inc(s_max, 1)
                if tail:
                    dve.wait_ge(p_lo, 4 * m + k + 1)
                dve.wait_ge(s_max, 4 * j + k + 1)
                nc.vector.tensor_tensor(S_sb[:, 8 * k:8 * k + 8].rearrange("p q a n -> p (q a) n"), S,
                                        bcast(nmax[:, k % 2], 2, N), ALU.subtract).then_inc(s_sub, 1)
                if k in (1, 2):
                    dve_sums(dve, j, (k - 1,))
                if k == 2:
                    dve_reciprocal(dve, j, 0)
            if B:
                dve.wait_ge(w_mm, s + 1)
                v = xT[:, bass.ds(s * COLS, COLS)]
                nc.vector.scalar_tensor_tensor(out=v, in0=bank_w[:, :], scalar=bo_col[:, 0:1], in1=v,
                                               op0=ALU.add, op1=ALU.add).then_inc(x1_ok, 1)

        WP1 = 3 + 2 + 4 + 1 + 4
        WPREP2 = 16 + 12 + 1 + 5 + 3

        def dve_weights2(dve):
            dve.wait_ge(zeros_w2, 1)
            dve.wait_ge(wprep_a, 14)
            for g in range(A2):
                rows = slice(D * g, D * g + D)
                for kind in range(2):
                    nc.vector.tensor_copy(W1_bd[rows, HI, kind, g].rearrange("p m d -> p (m d)"),
                                          w12_f[rows, 64 * kind:64 * kind + 64]).then_inc(wprep2, 1)
                nc.vector.tensor_copy(Wgo_bd[rows, HI, g], w12_f[rows, 128:160]).then_inc(wprep2, 1)
                nc.vector.tensor_copy(Wlo_bd[rows, g], w12_f[rows, 160:192]).then_inc(wprep2, 1)
            dve.wait_ge(wprep2, 16)
            for g in range(A2):
                rows = slice(D * g, D * g + D)
                for kind in range(2):
                    nc.vector.tensor_tensor(W1_bd[rows, LO, kind, g].rearrange("p m d -> p (m d)"),
                                            w12_f[rows, 64 * kind:64 * kind + 64],
                                            W1_bd[rows, HI, kind, g].rearrange("p m d -> p (m d)"),
                                            ALU.subtract).then_inc(wprep2, 1)
                nc.vector.tensor_tensor(Wgo_bd[rows, LO, g], w12_f[rows, 128:160], Wgo_bd[rows, HI, g],
                                        ALU.subtract).then_inc(wprep2, 1)

        def dve_biases2(dve):
            dve.wait_ge(wts2_in, WTS2)
            nc.vector.tensor_scalar(b1_in[:, 1], b1_in[:, 1], 0.5, None, ALU.mult).then_inc(wprep2, 1)
            n = 16 + 12 + 1
            rest = b1_in[:, :, :, :]
            for r in range(3):
                dve.wait_ge(wprep2, n)
                nc.vector.tensor_copy(b1_s[:, r], rest).then_inc(wprep2, 1)
                n += 1
                dve.wait_ge(wprep2, n)
                if r < 2:
                    nc.vector.tensor_tensor(b1_r[:, r], rest, b1_s[:, r], ALU.subtract).then_inc(wprep2, 1)
                    n += 1
                    rest = b1_r[:, r]
            for r in range(3):
                row = slice(32 * r, 32 * r + 1)
                nc.vector.tensor_copy(B1[row, :, :, :, :].rearrange("p k e m d -> p k e (m d)"),
                                      bcast(b1_s[row, r].rearrange("p k m d -> p k (m d)"), 2, A2)).then_inc(wprep2, 1)
            assert n + 3 == WPREP2

        def zero(v):
            return nc.vector.memset(v, 0.0)

        @block.vector
        def _(dve):
            zero(A_bd[:, :, :, :, :].rearrange("p k h e d -> p (k h e d)").bitcast(f32))
            zero(Wg_bd[:, :, :, :, :].rearrange("p k h e c -> p (k h e c)").bitcast(f32))
            zero(Wv_bd[:, :, :, :].rearrange("p h e c -> p (h e c)"))
            zero(b1_in[:, :, :, :].rearrange("p k m d -> p (k m d)")).then_inc(zeros_w, 1)
            def gn_reduce(out, v):
                return nc.vector.tensor_reduce(out, v.rearrange("p (b d) -> p d b", d=D), op=ALU.add, axis=AX.X)
            for e in range(A2):
                dve.wait_ge(sq_ok, e + 1)
                gn_reduce(gn_part[:, 1, :, e], gn_sq[:, e]).then_inc(sqred, 1)
                if e == 1:
                    dve.wait_ge(x_sum, 1)
                    gn_reduce(gn_part[:, 0, :, 0], gn_x[0]).then_inc(gn_ok, 1)
            dve.wait_ge(sqred, 4)
            nc.vector.tensor_reduce(gn_sum[:, 1], gn_part[:, 1], op=ALU.add, axis=AX.X).then_inc(gn_ok, 1)
            dve.wait_ge(x_sum, 2)
            gn_reduce(gn_part[:, 0, :, 1], gn_x[1]).then_inc(gn_ok, 1)
            dve.wait_ge(gn_ok, 3)
            nc.vector.tensor_tensor(gn_sum[:, 0], gn_part[:, 0, :, 0], gn_part[:, 0, :, 1], ALU.add).then_inc(gn_ok, 1)
            dve.wait_ge(wT_mm, 1)
            nc.vector.tensor_copy(wqT[:, :, :], bcast(PS[4][:, 0:D], 1, A2)).then_inc(wprep, 1)
            nc.vector.tensor_copy(wkT[:, :], PS[4][:, D:2 * D]).then_inc(wprep, 1)
            dve.wait_ge(gn_mm, 1)
            nc.vector.tensor_copy(gn_mv[:, :, :].rearrange("p k d -> p (k d)"), PS[0][:, 0:2 * D]).then_inc(gn_ok, 1)
            dve.wait_ge(gn_ok, 5)
            nc.vector.tensor_tensor(gn_tmp[:, 0], gn_mv[:, 0], gn_mv[:, 0], ALU.mult).then_inc(gn_ok, 1)
            dve.wait_ge(gn_ok, 6)
            nc.vector.scalar_tensor_tensor(out=gn_tmp[:, 1], in0=gn_mv[:, 1], scalar=EPS, in1=gn_tmp[:, 0],
                                           op0=ALU.add, op1=ALU.subtract).then_inc(gn_ok, 1)
            dve.wait_ge(gn_ok, 7)
            nc.vector.reciprocal(gn_tmp[:, 2], gn_tmp[:, 1]).then_inc(gn_ok, 1)
            dve.wait_ge(rsq, 1)
            nc.vector.scalar_tensor_tensor(out=gn_sh[:, :], in0=gn_mv[:, 0], scalar=-1.0, in1=gn_r[:, :],
                                           op0=ALU.mult, op1=ALU.mult).then_inc(gn_ok, 1)
            zf = zc[:, 0].rearrange("p e b d -> p (e b) d")
            nc.vector.tensor_tensor(zc[:, 0], x_tok[:, :, 0:SB, :], bcast(bcast(gn_r[:, :], 1, SB), 1, A2),
                                    ALU.mult).then_inc(ln_0, 1)
            dve.wait_ge(ln_0, 1)
            dve.wait_ge(gn_ok, 9)
            nc.vector.tensor_tensor(zf, zf, bcast(gn_sh[:, :], 1, A2 * SB), ALU.add).then_inc(ln_0, 1)
            dve_ln_centre(dve, 0, 0)
            dve.wait_ge(wprep, 1)
            dve.wait_ge(zeros_z, NZ_MASKS)
            nc.vector.tensor_tensor(wqTm, bcast(wqT[:, :, :].rearrange("p e d -> p (e d)"), 1, H),
                                    bcast(headmask[:, :], 2, 128), ALU.mult).then_inc(wprep, 1)
            dve_ln_rstd(dve, 0, 0)
            dve.wait_ge(ln_v, LV)
            nc.vector.reciprocal(ln_inv[:, :], ln_ve[:, 0]).then_inc(ln_v0, 1)
            dve.wait_ge(ln_0, 3)
            for n, by in ((4, bcast(ln_rs[:, 0], 2, D)), (5, bcast(w_bc[:, :], 1, A2 * SB))):
                nc.vector.tensor_tensor(zf, zf, by, ALU.mult).then_inc(ln_0, 1)
                dve.wait_ge(ln_0, n)
            nc.vector.tensor_tensor(zf, zf, bcast(b_bc[:, :], 1, A2 * SB), ALU.add).then_inc(ln_0, 1)
            nc.vector.tensor_tensor(a2mask[:, :], headmask[:, 0:A2], headmask[:, A2:H], ALU.add).then_inc(wprep, 1)
            dve.wait_ge(wprep, 4)
            nc.vector.tensor_scalar(a2mask[:, :], a2mask[:, :], 0.5, None, ALU.mult).then_inc(wprep, 1)
            dve.wait_ge(ln_a, 1)
            hl = zn_tok[:, 0].rearrange("p e d b k -> p e b d k")
            nc.vector.tensor_tensor(hl[:, :, :, :, LO], zc[:, 0], hl[:, :, :, :, HI], ALU.subtract).then_inc(ln_0, 1)
            dve.wait_ge(wprep_a, 4)
            for g in range(A2):
                rows = slice(D * g, D * g + D)
                nc.vector.scalar_tensor_tensor(out=A_bd[rows, LO, :, g], in0=PS[1][rows, 0:256]
                                               .rearrange("p (h d) -> p h d", h=H), scalar=0.25,
                                               in1=A_bd[rows, HI, :, g], op0=ALU.mult,
                                               op1=ALU.subtract).then_inc(wprep, 1)
            dve_ln_centre(dve, 1, 1)
            dve.wait_ge(wts_in, WTS)
            dve.wait_ge(wprep, 5)
            nc.vector.tensor_tensor(Wo_h[:, :, :, :], bcast(wo_in[:, :, :], 2, A2),
                                    bcast(bcast(a2mask[:, :], 2, D), 1, HP), ALU.mult).then_inc(wprep, 1)
            dve_ln_rstd(dve, 1, 1)
            for j in range(3):
                dve_period(dve, j, j % 2, tail=j >= 1, B=j >= 2, stats=False)
            with dve.Fori(0, LOOPS) as it:
                for i in range(2):
                    dve_period(dve, 2 * it + 3 + i, 1 - i)
            for j in range(NS - 1, NS + 2):
                dve_period(dve, j, j % 2, tail=j <= NS, A=j < NS, LN=j < NS - 1)
            dve_stats(dve, NS - 1)

            def step(n, ins):
                ins.then_inc(g2_ok, 1)
                dve.wait_ge(g2_ok, n)
            dve.wait_ge(x1_st, 2 * NS)
            step(1, nc.vector.tensor_reduce(g2[:, 0:2], st1[:, :, :, :].rearrange("p k s n -> p k n s"),
                                            op=ALU.add, axis=AX.X))
            dve.wait_ge(g2_mm, 1)
            mean, mean_sq = PS[0][:, 0:N], PS[0][:, N:2 * N]
            step(2, nc.vector.tensor_copy(g2[:, 2], mean))
            step(3, nc.vector.tensor_tensor(g2[:, 4], g2[:, 2], g2[:, 2], ALU.mult))
            nc.vector.scalar_tensor_tensor(out=g2[:, 5], in0=mean_sq, scalar=EPS, in1=g2[:, 4],
                                           op0=ALU.add, op1=ALU.subtract).then_inc(g2_ok, 1)
            nc.vector.tensor_tensor(g2[:, 8], mean_sq, g2[:, 4], ALU.subtract).then_inc(g2_ok, 1)
            dve.wait_ge(g2_ok, 4)
            step(6, nc.vector.reciprocal(g2[:, 7], g2[:, 5]))
            step(7, nc.vector.tensor_tensor(g2[:, 9], g2[:, 8], g2[:, 7], ALU.mult))
            step(8, nc.vector.tensor_reduce(col[:, V:V + 1], g2[:, 9], op=ALU.add, axis=AX.X))
            nc.vector.tensor_scalar(col[:, BGH:BGH + 1], col[:, Bgo:Bgo + 1], 0.5, None, ALU.mult).then_inc(g2_ok, 1)
            dve.wait_ge(g2_mm, 2)
            step(10, nc.vector.tensor_scalar(col[:, RV:RV + 1], PS[1][:, 0:1], EPS, None, ALU.add))
            step(11, nc.vector.reciprocal(col[:, T0:T0 + 1], col[:, RV:RV + 1]))
            step(12, nc.vector.tensor_scalar(g2[:, 5], g2[:, 7], col[:, T0:T0 + 1], None, ALU.mult))
            dve.wait_ge(rsq, 2)
            step(13, nc.vector.tensor_scalar(g2[:, 10], g2[:, 6], col[:, Ain:Ain + 1], None, ALU.mult))
            step(14, nc.vector.scalar_tensor_tensor(out=g2[:, 4], in0=g2[:, 2], scalar=-1.0, in1=g2[:, 10],
                                                    op0=ALU.mult, op1=ALU.mult))
            step(15, nc.vector.tensor_scalar(g2[:, 11], g2[:, 4], col[:, Bin:Bin + 1], None, ALU.add))
            z1_norm(dve, nc.vector, 0, z1_m[0])
            z1_low(dve, nc.vector, 0, z1_l[0])
            dve.wait_ge(g2_mm, 3)
            nc.vector.tensor_copy(col[:, RW:RW + 1], PS[2][:, 0:1]).then_inc(g2_ok, 1)
            nc.vector.tensor_scalar(col[:, BOH:BOH + 1], col[:, Bout:Bout + 1], 0.5, None, ALU.mult).then_inc(g2_ok, 1)
            nc.vector.tensor_scalar(col[:, BLH:BLH + 1], col[:, Blo:Blo + 1], 0.5, None, ALU.mult).then_inc(g2_ok, 1)

            for i in range(4 * A4):
                g, f = divmod(i, A4)
                if f == 0 and g >= 2:
                    dve.wait_ge(k_mm, 2 * (g - 1))
                    dve.wait_ge(bbd_ld[g % 2], 64 * (g // 2))
                dve.wait_ge(pj_th, i + 1)
                lin = PS[i % 3][:, 256:512].rearrange("p (a m c) -> p a m c", a=A2, m=2)
                for m, dst in ((0, a_buf), (1, b_buf)):
                    nc.vector.scalar_tensor_tensor(out=dst[g % 2][:, A2 * f:A2 * f + A2], in0=gt[i % 3][:, :, m],
                                                   scalar=1.0, in1=lin[:, :, m], op0=ALU.add,
                                                   op1=ALU.mult).then_inc(pj_ok, 1)
                if i == 2:
                    z1_low(dve, nc.vector, 1, z1_l[0])

            def kstep(n, ins):
                ins.then_inc(k_ok, 1)
                dve.wait_ge(k_ok, n)
            dve.wait_ge(k_cp, 8)
            dve.wait_ge(k_sq, 8)
            kstep(1, nc.vector.tensor_reduce(ksum2[:, :], ksum[:, :, :], op=ALU.add, axis=AX.X))
            dve.wait_ge(ks_mm, 1)
            kstep(2, nc.vector.tensor_copy(g2[:, 0, 0:2], PS[7][:, 0:2]))
            kstep(3, nc.vector.scalar_tensor_tensor(out=col[:, V:V + 1], in0=g2[:, 0, 0:1], scalar=g2[:, 0, 0:1],
                                                    in1=g2[:, 0, 1:2], op0=ALU.mult, op1=ALU.subtract))
            kstep(4, nc.vector.tensor_scalar(col[:, RV:RV + 1], col[:, V:V + 1], -1.0, EPS, ALU.mult, ALU.add))
            kstep(5, nc.vector.tensor_scalar(col[:, T0:T0 + 1], g2[:, 0, 0:1], -1.0, None, ALU.mult))
            dve.wait_ge(rsq_k, 1)
            kstep(6, nc.vector.tensor_scalar(col[:, KS:KS + 1], col[:, KR:KR + 1], col[:, Aout:Aout + 1], 0.5,
                                             ALU.mult, ALU.mult))
            dve.wait_ge(g2_ok, 18)
            kstep(7, nc.vector.tensor_scalar(col[:, KT:KT + 1], col[:, KS:KS + 1], col[:, T0:T0 + 1],
                                             col[:, BOH:BOH + 1], ALU.mult, ALU.add))
            kstep(8, nc.vector.tensor_scalar(col[:, CV:CV + 1], col[:, KT:KT + 1], col[:, RW:RW + 1],
                                             col[:, BLH:BLH + 1], ALU.mult, ALU.add))
            dve.wait_ge(go_th, 8)
            for i, u in enumerate(UNITS):
                dve.wait_ge(lo_s, i + 1)
                nc.vector.scalar_tensor_tensor(out=unit(x2, u), in0=unit(tg, u), scalar=1.0, in1=unit(x2, u),
                                               op0=ALU.add, op1=ALU.mult).then_inc(lo_g, 1)
                if u not in POOL_UNITS:
                    dve.wait_ge(lo_g, i + 1)
                    v = half_n(x2.rearrange("p (b n f) -> p b n f", n=N, f=A4), u)
                    nc.vector.tensor_tensor(v, v, half_n(x1_nfb, u), ALU.add).then_inc(x2_ok[1], 1)
            for i in range(1, NS, 2):
                dve.wait_ge(x2_mm, i + 1)
                nc.vector.tensor_copy(out_tok[:, :, SB * i:SB * i + SB].rearrange("p e b d -> p b e d"),
                                      PS[1 + i % 3][:, :].rearrange("p (b e d) -> p b e d", b=SB, e=A2)
                                      ).then_inc(x2_cp[1], 1)

        def mm(o, l, r, start=True, stop=True):
            return nc.tensor.matmul(o, l, r, start=start, stop=stop)

        def split_mm(o, wt, mv):
            mm(o, wt[HI], mv[HI], True, False)
            mm(o, wt[LO], mv[HI], False, False)
            return mm(o, wt[HI], mv[LO], False, True)

        def pe_znT(pe, j, par):
            wait_zn(pe, j)
            if not isinstance(j, int) or j >= 3:
                pe.wait_ge(x1_ok, j - 2)
            zt = bank_w[:, :].bitcast(f16)
            tok = zn_tok[:, par].rearrange("p e d b k -> p (e d) b k")
            for k in (HI, LO):
                for b in range(SB):
                    at = 128 * (SB * k + b)
                    last = nc.tensor.transpose(zt[:, at:at + 128], tok[:, :, b, k], ident16[:, :])
            last.then_inc(zT_mm, 1)

        def pe_t(pe, j, hs=range(H)):
            if hs[0] == 0:
                pe.wait_ge(zT_ok, j + 1)
            for h in hs:
                if h >= 3:
                    pe.wait_ge(t_lo, H * j + h - 2)
                elif not isinstance(j, int) or j >= 1:
                    pe.wait_ge(g_th, HP * (j - 1) + h + 2)
                split_mm(bank_tg(h)[:, :], [A_bd[:, k, h].rearrange("p e d -> p (e d)") for k in (HI, LO)],
                         [znT[:, k] for k in (HI, LO)]).then_inc(t_mm, 1)

        def pe_gate(pe, j, ks):
            for k in ks:
                if k < 3:
                    pe.wait_ge(t_lo, H * j + H - 2 + k)
                else:
                    pe.wait_ge(g_th, HP * j + 1)
                split_mm(bank_tg(H + k)[:, :],
                         [Wg_bd[:, p, 2 * k:2 * k + 2].rearrange("p h e c -> p (h e c)") for p in (HI, LO)],
                         [znT[:, p] for p in (HI, LO)]).then_inc(g_mm, 1)

        def pe_scores(pe, j, ks):
            if ks[0] == 0:
                pe.wait_ge(t_lo, H * (j + 1))
                pe.wait_ge(zbd_ld, 64 * (j + 1))
            for k in ks:
                if k >= 2:
                    pe.wait_ge(s_sub, 4 * j + k - 1)
                elif not isinstance(j, int) or j >= 1:
                    pe.wait_ge(s_sub, 4 * (j - 1) + k + 3)
                for q in range(8 * k, 8 * k + 8):
                    last = split_mm(bank_s(k)[:, 64 * (q % 8):64 * (q % 8) + 64],
                                    [t_sb[:, p, q].rearrange("p h i -> p (h i)") for p in (HI, LO)],
                                    [zbd[:, :, p, N * q:N * q + N] for p in (HI, LO)])
                last.then_inc(s_mm, 1)

        def pe_PT(pe, s, ks):
            for k in ks:
                pe.wait_ge(p_lo, 4 * s + k + 1)
                if k >= 2:
                    pe.wait_ge(pt_ok[k % 2], 2 * s + 1)
                for q in range(8 * k, 8 * k + 8):
                    last = nc.tensor.transpose(bank_b(k)[:, :].bitcast(f16)[:, 128 * (q % 8):128 * (q % 8) + 128],
                                               P2[:, q].rearrange("p k m -> p (k m)"), ident16[:, :])
                last.then_inc(pt_mm, 1)

        def pe_u(pe, s, par, half):
            pe.wait_ge(Z_ld[par], 128 * (half + 1))
            for k in range(8):
                if k in (0, 3):
                    pe.wait_ge(pt_ok[k % 2], 2 * (s + 1))
                elif k >= 4:
                    pe.wait_ge(u_ok, 8 * s + k - 3)
                for q in range(4 * k, 4 * k + 4):
                    b, f = divmod(q, A4)
                    o = bank_u(k)[:, 128 * (q % 4):128 * (q % 4) + 128]
                    Zq = Z[:, par, f].rearrange("p e d b k -> p (e d) b k")[:, :, b]
                    mm(o, Zq[:, :, HI], PT[:, q], True, False)
                    last = mm(o, Zq[:, :, LO], PT[:, q], False, True)
                last.then_inc(u_mm, 1)

        def pe_o(pe, s, ks):
            if ks[0] == 0:
                pe.wait_ge(u_ok, 8 * (s + 1))
            for k in ks:
                if k >= 2:
                    pe.wait_ge(o_ok, HP * s + k - 1)
                for r in range(2):
                    last = mm(bank_b(k)[64 * r:64 * r + 64], Wv_bd[:, 2 * k + r].rearrange("p e c -> p (e c)"),
                              u_sb[:, 2 * k + r].rearrange("p q i -> p (q i)"))
                last.then_inc(o_mm, 1)

        def pe_out(pe, s, ks):
            for k in ks:
                pe.wait_ge(o_ok, HP * s + k + 1)
                last = mm(bank_w[:, :], Wo_h[:, k].rearrange("p e d -> p (e d)"), og[:, k], k == 0, k == HP - 1)
            if ks[-1] == HP - 1:
                last.then_inc(w_mm, 1)

        def pe_period(pe, j, par, half, B=True, A=True):
            s = j - 2
            if not B:
                pe_t(pe, j)
                pe_scores(pe, j, (0, 1))
                if j == 0:
                    pe.wait_ge(wprep, WP1)
                    pe.wait_ge(wprep_a, 13)
                pe_gate(pe, j, (0, 1, 2))
                pe_scores(pe, j, (2,))
                pe_gate(pe, j, (3,))
                if j == 0:
                    pe_znT(pe, 1, 1)
                pe_scores(pe, j, (3,))
                return
            pe_PT(pe, s, (0, 1))
            if A:
                pe_znT(pe, j, par)
            pe_PT(pe, s, (2, 3))
            pe_u(pe, s, par, half)
            if not A:
                pe_o(pe, s, range(HP))
                pe_out(pe, s, range(HP))
                return
            pe_t(pe, j, (0, 1, 2))
            pe_o(pe, s, (0, 1))
            pe_t(pe, j, range(3, H))
            pe_o(pe, s, (2, 3))
            pe_scores(pe, j, (0, 1))
            pe_gate(pe, j, (0, 1))
            pe_out(pe, s, (0,))
            pe_scores(pe, j, (2,))
            pe_gate(pe, j, (2,))
            pe_out(pe, s, (1, 2))
            pe_scores(pe, j, (3,))
            pe_out(pe, s, (3,))
            pe_gate(pe, j, (3,))

        @block.tensor
        def _(pe):
            pe.wait_ge(wts_in, WTS)
            pe.wait_ge(zeros_z, NZ_MASKS)
            for k in range(2):
                last = nc.tensor.transpose(PS[4][:, D * k:D * k + D], wq_in[:, k], ident[0:D, 0:D])
            last.then_inc(wT_mm, 1)
            pe.wait_ge(gn_ok, 4)
            mm(PS[0][:, 0:2 * D], seqsum[:, :], gn_sum[:, :, :].rearrange("p k d -> p (k d)")).then_inc(gn_mm, 1)
            pe.wait_ge(xp_ok, A2)
            for i in range(NS):
                if i >= 2:
                    pe.wait_ge(xT_ok, i - 1)
                for b in range(SB):
                    last = nc.tensor.transpose(PS[2 + i % 2][:, 128 * b:128 * b + 128],
                                               x_perm[:, SB * i + b].rearrange("p e d -> p (e d)"), ident[:, :])
                last.then_inc(xT_mm, 1)
                if i == 5:
                    pe_znT(pe, 0, 0)
                if i == 4:
                    pe.wait_ge(wprep, 3)
                    for h in range(H):
                        last = mm(PS[1][:, D * h:D * h + D], wqTm[:, h], wkT[:, :])
                    last.then_inc(wT_mm, 1)
            pe.wait_ge(wts2_in, WTS2)
            nc.tensor.transpose(PS[6][:, 0:128], w1_in[:, :, :].rearrange("p g d -> p (g d)"),
                                ident[:, :]).then_inc(wT_mm, 1)
            nc.tensor.transpose(PS[6][:, 128:192], w2_in[:, :, :].rearrange("p g d -> p (g d)"),
                                ident[0:64, 0:64]).then_inc(wT_mm, 1)
            pe.wait_ge(xT_ok, NS)
            pe.wait_ge(wprep, 9)
            for j in range(3):
                pe_period(pe, j, j % 2, 0, B=j == 2)
            with pe.Fori(0, LOOPS) as it:
                for i in range(2):
                    pe_period(pe, 2 * it + 3 + i, 1 - i, it + i)
            for j in range(NS - 1, NS + 2):
                pe_period(pe, j, j % 2, j // 2 - 1, A=j < NS)

            pe.wait_ge(wprep2, WPREP2)
            pe.wait_ge(g2_ok, 1)
            mm(PS[0][:, 0:2 * N], chsum[:, :], g2[:, 0:2].rearrange("p k n -> p (k n)")).then_inc(g2_mm, 1)
            pe.wait_ge(g2_ok, 8)
            mm(PS[1][:, 0:1], allsum[:, 0], col[:, V:V + 1]).then_inc(g2_mm, 1)
            mm(PS[2][:, 0:1], Wlo_bd[:, :, :].rearrange("p e d -> p (e d)"), ones_col[:, :]).then_inc(g2_mm, 1)
            pe.wait_ge(g2_ok, 10)

            def project(g):
                for f in range(A4):
                    i = A4 * g + f
                    news = f == 0 or i == A4 // 2
                    if i == 2:
                        pe.wait_ge(g2_ok, 16)
                    if i >= 3:
                        pe.wait_ge(pj_ok, 2 * (i - 2))
                    o = PS[i % 3][:, :]
                    zz = [z1[p][:, f, 4 * g:4 * g + 4].rearrange("p n b -> p (n b)") for p in (HI, LO)]
                    W = [W1_bd[:, p].rearrange("p k e m d -> p (k e m d)") for p in (HI, LO)]
                    mm(o, ones_bf[:, :], B1[:, :, :, :, :].rearrange("p k e m d -> p (k e m d)"), True, False)
                    if news:
                        pe.wait_ge(z1_h, 1 + f // 4 if g == 0 else g + 2)
                    mm(o, zz[HI], W[HI], False, False)
                    mm(o, zz[HI], W[LO], False, False)
                    if news:
                        pe.wait_ge(z1_l[g // 2], (1 + f // 4, 3, 1, 2)[g])
                    mm(o, zz[LO], W[HI], False, True).then_inc(pj_mm, 1)

            def triangle(g):
                pe.wait_ge(bbd_ld[g % 2], 64 * (g // 2 + 1))
                for h in range(2):
                    i = 2 * g + h
                    if i >= 4:
                        pe.wait_ge(k_sq, i - 3)
                    for c in range(16 * h, 16 * h + 16):
                        c8, c4 = divmod(c, 4)
                        last = mm(PS[3 + i % 4][L * c4:L * c4 + L, 128 * (c8 % 4):128 * (c8 % 4) + 128],
                                  a_buf[g % 2][:, :, c], bbd[g % 2][:, :, :, c])
                    last.then_inc(k_mm, 1)

            project(0)
            project(1)
            triangle(0)
            project(2)
            triangle(1)
            project(3)
            triangle(2)
            def out_gates(js):
                for j in js:
                    if j < 3:
                        pe.wait_ge(pj_ok, 64)
                    else:
                        pe.wait_ge(go_th, j - 2)
                    split_mm(PS[j % 3][:, :], [Wgo_bd[:, p].rearrange("p e d -> p (e d)") for p in (HI, LO)],
                             [z1[p].rearrange("p f n b -> p b n f")[:, SB * j:SB * j + SB] for p in (HI, LO)]
                             ).then_inc(go_mm, 1)
            out_gates(range(0, 6))
            triangle(3)
            out_gates((6,))
            pe.wait_ge(k_ok, 1)
            mm(PS[7][:, 0:2], allsum[:, 1], ksum2[:, :]).then_inc(ks_mm, 1)
            out_gates((7,))

            def lo(u):
                mm(bank_lo(u)[:, :], Wlo_bd[:, :, :].rearrange("p e d -> p (e d)"), half_n(kT_bnf, u)).then_inc(lo_mm, 1)
            for u, engine_sem, n in ((0, k_ok, 2),
                                     (2, go_th, 8),
                                     (4, k_sq, 8), (1, k_sq, 8), (3, k_sq, 8), (5, k_sq, 8),
                                     (6, lo_s, 1), (7, lo_s, 2)):
                pe.wait_ge(engine_sem, n)
                pe.wait_ge(kT_ld[u // 2], 64)
                lo(u)
            for i in range(NS):
                if i % 4 == 0:
                    for k, units in enumerate((POOL_UNITS, [u for u in UNITS if u not in POOL_UNITS])):
                        pe.wait_ge(x2_ok[k], max(n + 1 for n, u in enumerate(units) if u % 2 <= i // 4))
                if i >= 3:
                    pe.wait_ge(x2_cp[(i - 3) % 2], (i - 3) // 2 + 1)
                for b in range(SB):
                    at = 128 * (SB * i + b)
                    last = nc.tensor.transpose(PS[1 + i % 3][:, 128 * b:128 * b + 128], x2[:, at:at + 128], ident[:, :])
                last.then_inc(x2_mm, 1)


_INS = ["x", "L0_conv_ln_w", "L0_conv_ln_b", "L0_conv_Wq", "L0_conv_Wk", "L0_conv_Wv", "L0_conv_Wg", "L0_conv_bg",
        "L0_conv_Wo", "L0_conv_bo", "L1_conv_alpha_in", "L1_conv_beta_in", "L1_conv_W_la", "L1_conv_b_la",
        "L1_conv_W_ga", "L1_conv_b_ga", "L1_conv_W_lb", "L1_conv_b_lb", "L1_conv_W_gb", "L1_conv_b_gb",
        "L1_conv_alpha_o", "L1_conv_beta_o", "L1_conv_W_go", "L1_conv_b_go", "L1_conv_W_lo", "L1_conv_b_lo"]


def kernel(**inputs):
    import numpy as _np
    import concourse.bacc as _bacc
    from concourse.bass_utils import run_bass_kernel_spmd as _run

    nc = _bacc.Bacc("TRN2", target_bir_lowering=False, num_devices=1)
    arrays, args = {}, []
    for name in _INS:
        a = _np.ascontiguousarray(inputs[name])
        if name == "L0_conv_Wo":
            a = _np.ascontiguousarray(a.reshape(HP, 2, C, D).transpose(1, 2, 0, 3).reshape(2, C, HP * D))
        if name == "L0_conv_bg":
            a = _np.ascontiguousarray(a.reshape(HP, 2, C).transpose(1, 2, 0))
        arrays[f"in_{name}"] = a
        args.append(nc.dram_tensor(f"in_{name}", a.shape, mybir.dt.from_np(a.dtype), kind="ExternalInput").ap())
    out = nc.dram_tensor("out_x", (N, L, L, D), f32, kind="ExternalOutput").ap()
    build(nc, *args, out)
    r = _run(nc, [arrays], core_ids=[0])
    return r.results[0]["out_x"]
```
